# Optimizing a Trainium2 kernel written in Bass

```python
import numpy as np
import jax
import jax.numpy as jnp

def _softmax(x, axis=-1):
    return jax.nn.softmax(x, axis=axis)

def _gelu(x):
    return jax.nn.gelu(x, approximate=True)

def _silu(x):
    return jax.nn.silu(x)

def _sigmoid(x):
    return jax.nn.sigmoid(x)

def _layernorm(x, axis=-1, eps=1e-05):
    m = jnp.mean(x, axis=axis, keepdims=True)
    v = jnp.var(x, axis=axis, keepdims=True)
    return (x - m) / jnp.sqrt(v + eps)

def _scatter_add(tgt, idx, src, axis=0):
    return tgt.at[idx].add(src)

def _segment_sum(src, seg, n):
    return jax.ops.segment_sum(src, seg, n)
kernel_name = 'mk_prb_d2_jaxref_r8_f5cb7d'

def setup_inputs(seed: int=0):
    np.random.seed(seed)
    _w = jnp.asarray

    def _L0_attn_setup():
        import jax, jax.numpy as jnp
        import numpy as np
        EMB_DIM = 512
        N_HEADS = 32
        QKV_DIM = EMB_DIM // N_HEADS
        B, S = (4, 512)
        key = jax.random.key(seed)
        ks = jax.random.split(key, 7)
        std = 1.0 / np.sqrt(EMB_DIM)
        x = jax.random.normal(ks[0], (B, S, EMB_DIM), dtype=jnp.float32)
        Wq = jax.random.normal(ks[1], (EMB_DIM, QKV_DIM, N_HEADS), dtype=jnp.float32) * std
        bq = jnp.zeros((QKV_DIM, N_HEADS), dtype=jnp.float32)
        Wk = jax.random.normal(ks[2], (EMB_DIM, QKV_DIM, 1), dtype=jnp.float32) * std
        bk = jnp.zeros((QKV_DIM, 1), dtype=jnp.float32)
        Wv = jax.random.normal(ks[3], (EMB_DIM, QKV_DIM, 1), dtype=jnp.float32) * std
        bv = jnp.zeros((QKV_DIM, 1), dtype=jnp.float32)
        return {'x': x, 'Wq': Wq, 'bq': bq, 'Wk': Wk, 'bk': bk, 'Wv': Wv, 'bv': bv}
    _L0_attn_in = _L0_attn_setup()

    def _L0_ffn_setup():
        import jax, jax.numpy as jnp
        import numpy as np
        H = 512
        I = 1376
        R = 32
        NLEV = 16
        Q_ZERO = 7.5
        Q_STEP = 0.005
        LR_SCALE = 0.02

        def _qlinear(x, q, scale, A, Bm):
            w = (q.astype(jnp.float32) - Q_ZERO) * (scale * Q_STEP)[:, None]
            y = jnp.einsum('bsh,oh->bso', x, w)
            return y + LR_SCALE * (x @ A @ Bm)
        key = jax.random.key(seed)
        ks = jax.random.split(key, 13)
        B, S = (2, 256)
        inp = {'x': jax.random.normal(ks[0], (B, S, H), jnp.float32), 'gate_q': jax.random.randint(ks[1], (I, H), 0, NLEV, jnp.int32), 'gate_scale': jax.random.uniform(ks[2], (I,), jnp.float32), 'gate_A': jax.random.normal(ks[3], (H, R), jnp.float32), 'gate_B': jax.random.normal(ks[4], (R, I), jnp.float32), 'up_q': jax.random.randint(ks[5], (I, H), 0, NLEV, jnp.int32), 'up_scale': jax.random.uniform(ks[6], (I,), jnp.float32), 'up_A': jax.random.normal(ks[7], (H, R), jnp.float32), 'up_B': jax.random.normal(ks[8], (R, I), jnp.float32), 'down_q': jax.random.randint(ks[9], (H, I), 0, NLEV, jnp.int32), 'down_scale': jax.random.uniform(ks[10], (H,), jnp.float32), 'down_A': jax.random.normal(ks[11], (I, R), jnp.float32), 'down_B': jax.random.normal(ks[12], (R, H), jnp.float32)}
        return inp
    _L0_ffn_in = _L0_ffn_setup()

    def _L1_attn_setup():
        import jax, jax.numpy as jnp
        import numpy as np
        BATCH, SEQ, HIDDEN = (2, 512, 512)
        HEADS, HEAD_DIM, BLOCK = (32, 128, 32)
        LAYER_IDX, N_LAYERS = (1, 32)
        EPS = 1e-05

        def _decays():
            base = 1.0 / 2.0 ** (8.0 / HEADS)
            exponent = jnp.arange(HEADS, dtype=jnp.float32) + 1.0
            factor = 1.0 - LAYER_IDX / (N_LAYERS - 1 + 1e-05) + 1e-05
            slope = (base ** exponent * factor)[:, None, None]
            r = jnp.arange(BLOCK, dtype=jnp.float32) + 1.0
            q_decay = jnp.exp(-slope * r[:, None])
            k_decay = jnp.exp(-slope * (BLOCK - r)[:, None])
            diff = r[:, None] - r[None, :]
            diag = slope[None] * diff[None, None]
            diag = jnp.where(diag >= 0, -diag, -jnp.inf)
            diag_decay = jnp.exp(diag)
            block_decay = jnp.exp(-slope * BLOCK)
            return (q_decay, k_decay, diag_decay, block_decay)
        key = jax.random.key(seed)
        ks = jax.random.split(key, 5)
        s = 0.02
        return {'hidden_states': jax.random.normal(ks[0], (BATCH, SEQ, HIDDEN), jnp.float32), 'qkv_w': jax.random.normal(ks[1], (3 * HEADS * HEAD_DIM, HIDDEN), jnp.float32) * s, 'out_w': jax.random.normal(ks[2], (HIDDEN, HEADS * HEAD_DIM), jnp.float32) * s, 'gate_w': jax.random.normal(ks[3], (HEADS * HEAD_DIM, HIDDEN), jnp.float32) * s, 'norm_w': jnp.ones((HEADS * HEAD_DIM,), jnp.float32)}
    _L1_attn_in = _L1_attn_setup()

    def _L1_ffn_setup():
        import jax, jax.numpy as jnp
        import numpy as np
        HID, INT, LAT, NE, K = (512, 1024, 256, 8, 2)
        LN_EPS = 1e-05

        def _layernorm(x, gamma, beta):
            mu = jnp.mean(x, axis=-1, keepdims=True)
            var = jnp.var(x, axis=-1, keepdims=True)
            return (x - mu) * jax.lax.rsqrt(var + LN_EPS) * gamma + beta
        key = jax.random.key(seed)
        ks = jax.random.split(key, 8)
        s = lambda d: 1.0 / np.sqrt(d)
        return {'hidden_states': jax.random.normal(ks[0], (4, 256, HID), jnp.float32), 'gate_w': jax.random.normal(ks[1], (HID, NE), jnp.float32) * s(HID), 'up_w': jax.random.normal(ks[2], (HID, INT), jnp.float32) * s(HID), 'down_w': jax.random.normal(ks[3], (INT, HID), jnp.float32) * s(INT), 'fc1_w': jax.random.normal(ks[4], (HID, LAT), jnp.float32) * s(HID), 'fc2_w': jax.random.normal(ks[5], (LAT, HID), jnp.float32) * s(LAT), 'expert_w': jax.random.normal(ks[6], (LAT, LAT), jnp.float32), 'ln_gamma': jnp.ones((HID,), jnp.float32), 'ln_beta': jnp.zeros((HID,), jnp.float32)}
    _L1_ffn_in = _L1_ffn_setup()
    _d = {'L0_attn_x': _L0_attn_in['x'], 'L0_attn_Wq': _L0_attn_in['Wq'], 'L0_attn_bq': _L0_attn_in['bq'], 'L0_attn_Wk': _L0_attn_in['Wk'], 'L0_attn_bk': _L0_attn_in['bk'], 'L0_attn_Wv': _L0_attn_in['Wv'], 'L0_attn_bv': _L0_attn_in['bv'], 'L0_ffn_gate_q': _L0_ffn_in['gate_q'], 'L0_ffn_gate_scale': _L0_ffn_in['gate_scale'], 'L0_ffn_gate_A': _L0_ffn_in['gate_A'], 'L0_ffn_gate_B': _L0_ffn_in['gate_B'], 'L0_ffn_up_q': _L0_ffn_in['up_q'], 'L0_ffn_up_scale': _L0_ffn_in['up_scale'], 'L0_ffn_up_A': _L0_ffn_in['up_A'], 'L0_ffn_up_B': _L0_ffn_in['up_B'], 'L0_ffn_down_q': _L0_ffn_in['down_q'], 'L0_ffn_down_scale': _L0_ffn_in['down_scale'], 'L0_ffn_down_A': _L0_ffn_in['down_A'], 'L0_ffn_down_B': _L0_ffn_in['down_B'], 'L1_attn_qkv_w': _L1_attn_in['qkv_w'], 'L1_attn_out_w': _L1_attn_in['out_w'], 'L1_attn_gate_w': _L1_attn_in['gate_w'], 'L1_attn_norm_w': _L1_attn_in['norm_w'], 'L1_ffn_gate_w': _L1_ffn_in['gate_w'], 'L1_ffn_up_w': _L1_ffn_in['up_w'], 'L1_ffn_down_w': _L1_ffn_in['down_w'], 'L1_ffn_fc1_w': _L1_ffn_in['fc1_w'], 'L1_ffn_fc2_w': _L1_ffn_in['fc2_w'], 'L1_ffn_expert_w': _L1_ffn_in['expert_w'], 'L1_ffn_ln_gamma': _L1_ffn_in['ln_gamma'], 'L1_ffn_ln_beta': _L1_ffn_in['ln_beta']}
    _x0 = _d['L0_attn_x']
    _d['L0_attn_x'] = jax.random.normal(jax.random.fold_in(jax.random.key(seed), 1), (2, 1024, 512), dtype=_x0.dtype)
    del _x0
    return _d

def reference(L0_attn_x, L0_attn_Wq, L0_attn_bq, L0_attn_Wk, L0_attn_bk, L0_attn_Wv, L0_attn_bv, L0_ffn_gate_q, L0_ffn_gate_scale, L0_ffn_gate_A, L0_ffn_gate_B, L0_ffn_up_q, L0_ffn_up_scale, L0_ffn_up_A, L0_ffn_up_B, L0_ffn_down_q, L0_ffn_down_scale, L0_ffn_down_A, L0_ffn_down_B, L1_attn_qkv_w, L1_attn_out_w, L1_attn_gate_w, L1_attn_norm_w, L1_ffn_gate_w, L1_ffn_up_w, L1_ffn_down_w, L1_ffn_fc1_w, L1_ffn_fc2_w, L1_ffn_expert_w, L1_ffn_ln_gamma, L1_ffn_ln_beta):

    def _L0_attn_ref(x, Wq, bq, Wk, bk, Wv, bv):
        import jax, jax.numpy as jnp
        import numpy as np
        EMB_DIM = 512
        N_HEADS = 32
        QKV_DIM = EMB_DIM // N_HEADS
        B, S = (4, 512)
        q = jnp.einsum('bsD,Ddh->bsdh', x, Wq) + bq
        k = (jnp.einsum('bsD,Ddh->bsdh', x, Wk) + bk)[..., 0]
        v = (jnp.einsum('bsD,Ddh->bsdh', x, Wv) + bv)[..., 0]
        qkv_dim = q.shape[-2]
        n_heads = q.shape[-1]
        scale = 1.0 / jnp.sqrt(jnp.asarray(qkv_dim, dtype=q.dtype))
        scores = jnp.einsum('bsdh,bse->bsde', q, k) * scale
        p = jax.nn.softmax(scores, axis=-1)
        o = jnp.einsum('bsde,bse->bsd', p, v)
        out = jnp.broadcast_to(o[..., None], o.shape + (n_heads,))
        return out.reshape(x.shape[:-1] + (qkv_dim * n_heads,))

    def _L0_ffn_ref(x, gate_q, gate_scale, gate_A, gate_B, up_q, up_scale, up_A, up_B, down_q, down_scale, down_A, down_B):
        import jax, jax.numpy as jnp
        import numpy as np
        H = 512
        I = 1376
        R = 32
        NLEV = 16
        Q_ZERO = 7.5
        Q_STEP = 0.005
        LR_SCALE = 0.02

        def _qlinear(x, q, scale, A, Bm):
            w = (q.astype(jnp.float32) - Q_ZERO) * (scale * Q_STEP)[:, None]
            y = jnp.einsum('bsh,oh->bso', x, w)
            return y + LR_SCALE * (x @ A @ Bm)
        g = _qlinear(x, gate_q, gate_scale, gate_A, gate_B)
        u = _qlinear(x, up_q, up_scale, up_A, up_B)
        h = jax.nn.silu(g) * u
        return _qlinear(h, down_q, down_scale, down_A, down_B)

    def _L1_attn_ref(hidden_states, qkv_w, out_w, gate_w, norm_w):
        import jax, jax.numpy as jnp
        import numpy as np
        BATCH, SEQ, HIDDEN = (2, 512, 512)
        HEADS, HEAD_DIM, BLOCK = (32, 128, 32)
        LAYER_IDX, N_LAYERS = (1, 32)
        EPS = 1e-05

        def _decays():
            base = 1.0 / 2.0 ** (8.0 / HEADS)
            exponent = jnp.arange(HEADS, dtype=jnp.float32) + 1.0
            factor = 1.0 - LAYER_IDX / (N_LAYERS - 1 + 1e-05) + 1e-05
            slope = (base ** exponent * factor)[:, None, None]
            r = jnp.arange(BLOCK, dtype=jnp.float32) + 1.0
            q_decay = jnp.exp(-slope * r[:, None])
            k_decay = jnp.exp(-slope * (BLOCK - r)[:, None])
            diff = r[:, None] - r[None, :]
            diag = slope[None] * diff[None, None]
            diag = jnp.where(diag >= 0, -diag, -jnp.inf)
            diag_decay = jnp.exp(diag)
            block_decay = jnp.exp(-slope * BLOCK)
            return (q_decay, k_decay, diag_decay, block_decay)
        b, s, _ = hidden_states.shape
        h, d, bs = (HEADS, HEAD_DIM, BLOCK)
        nb = s // bs
        q_decay, k_decay, diag_decay, block_decay = _decays()
        qkv = jax.nn.silu(hidden_states @ qkv_w.T)
        qkv = qkv.reshape(b, s, h, 3, d)
        q = jnp.moveaxis(qkv[:, :, :, 0], 2, 1)
        k = jnp.moveaxis(qkv[:, :, :, 1], 2, 1)
        v = jnp.moveaxis(qkv[:, :, :, 2], 2, 1)

        def to_blocks(x):
            return jnp.moveaxis(x.reshape(b, h, nb, bs, d), 2, 0)
        qb, kb, vb = (to_blocks(q), to_blocks(k), to_blocks(v))

        def step(kv, blk):
            cq, ck, cv = blk
            scores = jnp.einsum('bhnd,bhmd->bhnm', cq, ck) * diag_decay
            intra = jnp.einsum('bhnm,bhmd->bhnd', scores, cv)
            inter = jnp.einsum('bhnd,bhde->bhne', cq * q_decay, kv)
            kv_next = kv * block_decay + jnp.einsum('bhnd,bhne->bhde', ck * k_decay, cv)
            return (kv_next, intra + inter)
        kv0 = jnp.zeros((b, h, d, d), hidden_states.dtype)
        _, out_blocks = jax.lax.scan(step, kv0, (qb, kb, vb))
        attn = jnp.moveaxis(out_blocks, 0, 2)
        attn = attn.reshape(b, h, s, d).transpose(0, 2, 1, 3).reshape(b, s, h * d)
        xf = attn.astype(jnp.float32)
        xf = xf * jax.lax.rsqrt(jnp.mean(xf * xf, axis=-1, keepdims=True) + EPS)
        normed = norm_w * xf.astype(attn.dtype)
        gate = jax.nn.sigmoid(hidden_states @ gate_w.T)
        return gate * normed @ out_w.T

    def _L1_ffn_ref(hidden_states, gate_w, up_w, down_w, fc1_w, fc2_w, expert_w, ln_gamma, ln_beta):
        import jax, jax.numpy as jnp
        import numpy as np
        HID, INT, LAT, NE, K = (512, 1024, 256, 8, 2)
        LN_EPS = 1e-05

        def _layernorm(x, gamma, beta):
            mu = jnp.mean(x, axis=-1, keepdims=True)
            var = jnp.var(x, axis=-1, keepdims=True)
            return (x - mu) * jax.lax.rsqrt(var + LN_EPS) * gamma + beta
        logits = jnp.einsum('bsh,he->bse', hidden_states, gate_w)
        routing_weights, selected_experts = jax.lax.top_k(logits, K)
        h = jax.nn.relu(jnp.einsum('bsh,hi->bsi', hidden_states, up_w)) ** 2
        shared_out = jnp.einsum('bsi,ih->bsh', h, down_w)
        x_latent = jnp.einsum('bsh,hl->bsl', hidden_states, fc1_w)
        expert_out = jnp.einsum('bsl,lm->bsm', x_latent, expert_w)
        moe_out = expert_out * jnp.sum(routing_weights, axis=-1, keepdims=True)
        routed_out = jnp.einsum('bsl,lh->bsh', moe_out, fc2_w)
        return _layernorm(shared_out + routed_out, ln_gamma, ln_beta)
    x = L0_attn_x
    xn = _layernorm(x, axis=-1)
    x = x + _L0_attn_ref(xn, L0_attn_Wq, L0_attn_bq, L0_attn_Wk, L0_attn_bk, L0_attn_Wv, L0_attn_bv) + _L0_ffn_ref(xn, L0_ffn_gate_q, L0_ffn_gate_scale, L0_ffn_gate_A, L0_ffn_gate_B, L0_ffn_up_q, L0_ffn_up_scale, L0_ffn_up_A, L0_ffn_up_B, L0_ffn_down_q, L0_ffn_down_scale, L0_ffn_down_A, L0_ffn_down_B)
    xn = _layernorm(x, axis=-1)
    x = x + _L1_attn_ref(xn, L1_attn_qkv_w, L1_attn_out_w, L1_attn_gate_w, L1_attn_norm_w) + _L1_ffn_ref(xn, L1_ffn_gate_w, L1_ffn_up_w, L1_ffn_down_w, L1_ffn_fc1_w, L1_ffn_fc2_w, L1_ffn_expert_w, L1_ffn_ln_gamma, L1_ffn_ln_beta)
    return x

_drawn_inputs = setup_inputs


def setup_inputs(seed=0):
    import zlib

    import numpy as np

    out = dict(_drawn_inputs(seed))
    spreads = {'L0_attn_bq': (0.0, 2.0),
     'L0_attn_bk': (0.0, 0.8),
     'L0_attn_bv': (0.0, 0.8),
     'L1_attn_norm_w': (1.0, 0.6),
     'L1_ffn_ln_gamma': (1.0, 0.6),
     'L1_ffn_ln_beta': (0.0, 0.8)}
    factors = {'L0_attn_Wq': 3.402,
     'L0_attn_Wk': 3.156,
     'L1_attn_gate_w': 7.412,
     'L1_ffn_gate_w': 31.678,
     'L1_ffn_up_w': 8.0,
     'L1_ffn_down_w': 8.0}
    for name, (base, spread) in spreads.items():
        noise = np.random.default_rng([zlib.crc32(name.encode()), seed]).standard_normal(out[name].shape)
        drawn = base * np.exp(spread * noise) if base else spread * noise
        out[name] = jnp.asarray(drawn.astype(out[name].dtype))
    for name, factor in factors.items():
        out[name] = (out[name] * factor).astype(out[name].dtype)
    return out
```

```python
from contextlib import ExitStack

import numpy as np
import concourse.bass as bass
from concourse import mybir

ALU = mybir.AluOpType
ACT = mybir.ActivationFunctionType
F32, F16, BF16, I32 = mybir.dt.float32, mybir.dt.float16, mybir.dt.bfloat16, mybir.dt.int32
AX_X = mybir.AxisListType.X

P = 128
D = 512
KT = D // P
BATCH, SEQ = 2, 1024
TOK = BATCH * SEQ
NT = TOK // P
BLK = 512
NBLK = TOK // BLK
TPB = BLK // P
EPS = 1e-5

QD, NH0 = 16, 32
INT0, RANK = 1376, 32
OT0 = -(-INT0 // P)
INT0P = OT0 * P
Q_ZERO, Q_STEP, LR_SCALE = 7.5, 0.005, 0.02
LRA, LRB = 16.0, 64.0

HEADS, HD, CH = 32, 128, 128
HPB = SEQ // BLK
CPH = BLK // CH
LAYER_IDX, N_LAYERS = 1, 32
INT1, LAT, NE = 1024, 256, 8
OT1, LT1 = INT1 // P, LAT // P
SQ_DOWN = 1.0 / 8.0
W1_UP, W1_DOWN = 0, KT * INT1
W1_FC1 = W1_DOWN + OT1 * D
W1_EXP = W1_FC1 + KT * LAT
W1_FC2 = W1_EXP + LT1 * LAT
W1_COLS = W1_FC2 + LT1 * D
W1_PER_BLK = 6
W1_CHUNK = W1_COLS // (NBLK * W1_PER_BLK)
assert W1_CHUNK * NBLK * W1_PER_BLK == W1_COLS and W1_PER_BLK % 2 == 0
R3 = 3 * RANK


def passes(w_hi, w_lo, a_hi, a_lo):
    return ((w_hi, a_hi), (w_hi, a_lo), (w_lo, a_hi))


def ds(at, n):
    return slice(at, at + n) if isinstance(at, int) else bass.ds(at, n)


def wait(eng, s, count):
    if not isinstance(count, int) or count > 0:
        eng.wait_ge(s, count)


def hold(eng, s, count, turns):
    if not isinstance(count, int):
        eng.wait_ge(s, count)
        eng.sem_inc(turns, 1)
    elif count > 0:
        eng.wait_ge(s, count)


def build(nc, t):
    with ExitStack() as ctx:
        def sb(stack, name, shape, dt=F32):
            return stack.enter_context(nc.sbuf_tensor(name, shape, dt))

        def sem(name):
            return ctx.enter_context(nc.semaphore(name))

        x_sb = sb(ctx, "x_sb", [P, NT, D])
        xnT_hi = sb(ctx, "xnT_hi", [P, KT, TOK], F16)
        xnT_lo = sb(ctx, "xnT_lo", [P, KT, TOK], BF16)
        ident = sb(ctx, "ident", [P, P])
        bank = [ctx.enter_context(nc.psum_tensor(f"bank{i}", [P, 512], F32)) for i in range(8)]

        w1_stack = ctx.enter_context(ExitStack())
        w1 = dict(hi=sb(w1_stack, "w1_hi", [P, W1_COLS], F16), lo=sb(w1_stack, "w1_lo", [P, W1_COLS], BF16))
        with ExitStack() as l0:
            w0 = dict(
                gate=sb(l0, "w0_gate", [P, KT, INT0P], F16),
                up=sb(l0, "w0_up", [P, KT, INT0P], F16),
                down=sb(l0, "w0_down", [P, OT0, D], F16),
                A_hi=sb(l0, "w0_A_hi", [P, 2 * KT + OT0, R3], F16),
                A_lo=sb(l0, "w0_A_lo", [P, 2 * KT + OT0, R3], BF16),
                B=sb(l0, "w0_B", [R3, 2 * INT0P + D], F16),
                scale=sb(l0, "w0_scale", [P, 2, OT0]),
                down_scale=sb(l0, "w0_down_scale", [P, D]),
            )
            with ExitStack() as s:
                phase_norm0_attn0(nc, t, sem, lambda *a: sb(s, *a), bank, x_sb, xnT_hi, xnT_lo, ident, w0)
            if DEBUG == 0:
                return dump(nc, t, sem, x_sb)
            with ExitStack() as s:
                phase_ffn0(nc, t, sem, lambda *a: sb(s, *a), bank, x_sb, xnT_hi, xnT_lo, w0, w1)
            if DEBUG == 1:
                return dump(nc, t, sem, x_sb)
        with ExitStack() as s:
            phase_norm1_ffn1(nc, t, sem, lambda *a: sb(s, *a), bank, x_sb, xnT_hi, xnT_lo, ident, w1)
        if DEBUG == 2:
            return dump(nc, t, sem, x_sb)
        w1_stack.close()
        with ExitStack() as s:
            phase_attn1(nc, t, lambda n: sem("attn1_" + n), lambda *a: sb(s, *a), bank, x_sb, xnT_hi, xnT_lo, ident)


DEBUG = 3


def dump(nc, t, sem, x_sb):
    out_written = sem("out_written")
    with nc.Block() as block:
        @block.sync
        def _(sp):
            sp.dma_start(t["out"].rearrange("(t p) d -> p t d", p=P), x_sb[:]).then_inc(out_written, 16)
            sp.wait_ge(out_written, 16)


def norm_small(nc, eng, steps, small, mv, n, sd_ready, sd_want, var_ready):
    done, c = steps
    veps, sd, r0, a, b, r, nmr = (small[:, i, 0:n] for i in range(7))
    mean, var = mv[:, 0:n, 0], mv[:, 0:n, 1]
    eng.wait_ge(done, c)
    nc.vector.tensor_scalar(veps, var, EPS, None, ALU.add).then_inc(var_ready, 1)
    eng.wait_ge(sd_ready, sd_want)
    nc.vector.reciprocal(r0, sd).then_inc(done, 1)
    eng.wait_ge(done, c + 1)
    nc.vector.tensor_tensor(a, r0, r0, ALU.mult).then_inc(done, 1)
    eng.wait_ge(done, c + 2)
    nc.vector.tensor_tensor(b, a, veps, ALU.mult).then_inc(done, 1)
    eng.wait_ge(done, c + 3)
    nc.vector.tensor_scalar(a, b, -0.5, 1.5, ALU.mult, ALU.add).then_inc(done, 1)
    eng.wait_ge(done, c + 4)
    nc.vector.tensor_tensor(r, r0, a, ALU.mult).then_inc(done, 1)
    eng.wait_ge(done, c + 5)
    nc.vector.scalar_tensor_tensor(nmr, r, -1.0, mean, ALU.mult, ALU.mult).then_inc(done, 1)
    return c + 6


def norm_buffers(sem, sb, tag):
    n = dict(stats=sb("stats" + tag, [P, NT, 6]), mv=sb("mv" + tag, [P, NT, 2]), small=sb("small" + tag, [P, 7, NT]),
             xn=sb("xn" + tag, [P, 2, D]))
    for k in ("stats_done", "var_ready", "sd_ready", "xn_done", "xT_done", "hi_done", "lo_done"):
        n[k] = sem(k + tag)
    return n


def norm_act(nc, act, n, bank, x_sb, xnT_hi):
    veps, sd, r, nmr = (n["small"][:, i, :] for i in (0, 1, 5, 6))
    act.wait_ge(n["var_ready"], 1)
    nc.scalar.activation(sd, veps, ACT.Sqrt).then_inc(n["sd_ready"], 1)
    act.wait_ge(n["stats_done"], 2 * NT + 6)
    for i in range(NT + 1):
        if i < NT:
            if i >= 2:
                act.wait_ge(n["xT_done"], i - 1)
            nc.scalar.activation(n["xn"][:, i % 2, :], x_sb[:, i, :], ACT.Identity, scale=r[:, i:i + 1],
                                 bias=nmr[:, i:i + 1]).then_inc(n["xn_done"], 1)
        if i >= 1:
            act.wait_ge(n["xT_done"], i)
            nc.scalar.activation(xnT_hi[:, :, (i - 1) * P:i * P],
                                 bank[(i - 1) % 2][:].rearrange("p (k t) -> p k t", k=KT), ACT.Copy).then_inc(n["hi_done"], 1)


def norm_pe(nc, pe, n, bank, ident):
    for i in range(NT):
        pe.wait_ge(n["xn_done"], i + 1)
        if i >= 2:
            pe.wait_ge(n["hi_done"], i - 1)
            pe.wait_ge(n["lo_done"], i - 1)
        for k in range(KT):
            mm = nc.tensor.transpose(bank[i % 2][:, k * P:(k + 1) * P], n["xn"][:, i % 2, k * P:(k + 1) * P], ident[:])
        mm.then_inc(n["xT_done"], 1)


def norm_dve_aggr(nc, dve, n):
    dve.wait_ge(n["stats_done"], NT)
    for i in range(NT):
        nc.vector.bn_aggr(n["mv"][:, i, :], n["stats"][:, i, :]).then_inc(n["stats_done"], 1)
    norm_small(nc, dve, (n["stats_done"], 2 * NT), n["small"], n["mv"], NT, n["sd_ready"], 1, n["var_ready"])


def norm_dve_lo(nc, dve, n, bank, xnT_hi, xnT_lo):
    for i in range(NT):
        dve.wait_ge(n["hi_done"], i + 1)
        tok = slice(i * P, (i + 1) * P)
        nc.vector.tensor_tensor(xnT_lo[:, :, tok], bank[i % 2][:].rearrange("p (k t) -> p k t", k=KT),
                                xnT_hi[:, :, tok], ALU.subtract).then_inc(n["lo_done"], 1)


def phase_norm0_attn0(nc, t, sem, sb, bank, x_sb, xnT_hi, xnT_lo, ident, w0):
    norm = norm_buffers(sem, sb, "0")
    q_int = sb("q_int", [P, 2, INT0P], I32)
    w48 = sb("w48", [P, KT, 3 * QD])
    w48_hi, w48_lo = sb("w48_hi", [P, KT, 3 * QD], F16), sb("w48_lo", [P, KT, 3 * QD], BF16)
    b48 = sb("b48", [P, 3 * QD])
    qkv = sb("qkv0", [P, NT, 3 * QD])
    kext = sb("kext", [P, 2, NT])
    smax = sb("smax", [P, 3, NT, QD])
    prob, pv = sb("prob0", [P, 2, TPB, QD, QD]), sb("pv0", [P, TPB, QD, QD])
    wq = prob[:].rearrange("p a t d e -> p (a t d e)").rearrange("p (k n) -> p k n", k=KT)
    bq = pv[:].rearrange("p t d e -> p (t d e)")[:, 0:QD * NH0]
    den, num, att = sb("den0", [P, NT, QD]), sb("num0", [P, NT, QD]), sb("att0", [P, NT, QD])

    x_in = [sem(f"x_in{i}") for i in range(NBLK)]
    q_in = [sem(f"q_in{i}") for i in range(2)]
    w_in = sem("w0_in")
    chunk_done, split_step, id_zero, id_done = sem("chunk_done"), sem("split_step"), sem("id_zero"), sem("id_done")
    scale_in = sem("scale_in")
    w48_step, w48_done = sem("w48_step"), sem("w48_done")
    qkv_done, qkv_out = sem("qkv0_done"), sem("qkv0_out")
    att_step, score_done, exp_done = sem("att_step"), sem("score0_done"), sem("exp0_done")

    x_dram = t["x"].rearrange("(t p) d -> p t d", p=P)
    chunks = []

    def staged(i, cols, rows=P):
        return q_int[0:rows, i % 2, 0:cols]

    for name in ("gate", "up"):
        for k in range(KT):
            src = t[name + "_q"].rearrange("(k p) o -> k p o", p=P)[k]
            chunks.append(("int", [(staged(len(chunks), INT0P), src)], w0[name][:, k, :]))
    down_flat = w0["down"][:].rearrange("p o d -> p (o d)")
    down_dram = t["down_q"].rearrange("(o p) d -> p o d", p=P)
    for a in range(0, OT0, 2):
        b = min(a + 2, OT0)
        view = staged(len(chunks), (b - a) * D)
        chunks.append(("int", [(view.rearrange("p (o d) -> p o d", d=D), down_dram[:, a:b, :])], down_flat[:, a * D:b * D]))
    at = 0
    for name, n in (("gate", KT), ("up", KT), ("down", OT0)):
        view = staged(len(chunks), n * R3).bitcast(F32).rearrange("p (k r) -> p k r", r=R3)
        src = t[name + "_A"].rearrange("(k p) r -> p k r", p=P)
        chunks.append(("A", [(view[:, :, c * RANK:(c + 1) * RANK], src) for c in range(3)], slice(at, at + n)))
        at += n
    at = 0
    for name, cols in (("gate", INT0P), ("up", INT0P), ("down", D)):
        view = staged(len(chunks), cols, R3).bitcast(F32)
        chunks.append(("B", [(view[c * RANK:(c + 1) * RANK, :], t[name + "_B"]) for c in range(3)], slice(at, at + cols)))
        at += cols

    with nc.Block() as block:
        @block.sync
        def _(sp):
            for i in range(NBLK):
                sp.dma_start(x_sb[:, i * TPB:(i + 1) * TPB, :], x_dram[:, i * TPB:(i + 1) * TPB, :]).then_inc(x_in[i], 16)
            sp.dma_start(wq, t["wq0"].rearrange("(k p) n -> p k n", p=P)).then_inc(w_in, 16)
            sp.dma_start(w48[:, :, QD:2 * QD], t["wk0"].rearrange("(k p) n -> p k n", p=P)).then_inc(w_in, 16)
            sp.dma_start(w48[:, :, 2 * QD:], t["wv0"].rearrange("(k p) n -> p k n", p=P)).then_inc(w_in, 16)
            sp.dma_start(bq, t["bq0"].partition_broadcast(P)).then_inc(w_in, 16)
            sp.dma_start(b48[:, QD:2 * QD], t["bk0"].partition_broadcast(P)).then_inc(w_in, 16)
            sp.dma_start(b48[:, 2 * QD:], t["bv0"].partition_broadcast(P)).then_inc(w_in, 16)
            sp.dma_start(w0["scale"][:, 0, :], t["gate_s"]).then_inc(scale_in, 16)
            sp.dma_start(w0["scale"][:, 1, :], t["up_s"]).then_inc(scale_in, 16)
            sp.dma_start(w0["down_scale"][:], t["down_s"].partition_broadcast(P)).then_inc(scale_in, 16)
            for i, (_, dmas, _) in enumerate(chunks):
                if i >= 2:
                    sp.wait_ge(chunk_done, i - 1)
                for dst, src in dmas:
                    sp.dma_start(dst, src).then_inc(q_in[i % 2], 16)

        @block.gpsimd
        def _(pool):
            nc.gpsimd.memset(ident[:], 0.0).then_inc(id_zero, 1)
            pool.wait_ge(id_zero, 1)
            nc.gpsimd.affine_select(out=ident[:], in_=ident[:], compare_op=ALU.not_equal, fill=1.0, base=0,
                                    pattern=[[-1, P]], channel_multiplier=1).then_inc(id_done, 1)
            landed, steps = [0, 0], 0
            for i, (kind, dmas, dst) in enumerate(chunks):
                landed[i % 2] += 16 * len(dmas)
                pool.wait_ge(q_in[i % 2], landed[i % 2])
                if kind == "int":
                    nc.gpsimd.tensor_scalar(dst, staged(i, dst.shape[-1]), 1.0, -Q_ZERO,
                                            ALU.mult, ALU.add).then_inc(chunk_done, 1)
                elif kind == "A":
                    n = dst.stop - dst.start
                    view = staged(i, n * R3).bitcast(F32).rearrange("p (k r) -> p k r", r=R3)
                    nc.gpsimd.tensor_copy(w0["A_hi"][:, dst, :], view).then_inc(split_step, 1)
                    steps += 1
                    pool.wait_ge(split_step, steps)
                    nc.gpsimd.tensor_tensor(w0["A_lo"][:, dst, :], view, w0["A_hi"][:, dst, :],
                                            ALU.subtract).then_inc(chunk_done, 1)
                else:
                    view = staged(i, dst.stop - dst.start, R3).bitcast(F32)
                    mid = slice(RANK, 2 * RANK)
                    pool.wait_ge(chunk_done, i)
                    nc.gpsimd.tensor_scalar(view, view, LRB, 1.0, ALU.mult, ALU.mult).then_inc(split_step, 1)
                    pool.wait_ge(split_step, steps + 1)
                    nc.gpsimd.tensor_copy(w0["B"][:, dst], view).then_inc(split_step, 1)
                    steps += 2
                    pool.wait_ge(split_step, steps)
                    nc.gpsimd.tensor_tensor(w0["B"][mid, dst], view[mid, :], w0["B"][mid, dst],
                                            ALU.subtract).then_inc(chunk_done, 1)
            pool.wait_ge(scale_in, 48)
            pool.wait_ge(chunk_done, len(chunks))
            nc.gpsimd.tensor_scalar(w0["scale"][:], w0["scale"][:], Q_STEP, 1.0, ALU.mult, ALU.mult).then_inc(split_step, 1)
            nc.gpsimd.tensor_scalar(w0["down_scale"][:], w0["down_scale"][:], Q_STEP, 1.0, ALU.mult,
                                    ALU.mult).then_inc(split_step, 1)

        @block.scalar
        def _(act):
            norm_act(nc, act, norm, bank, x_sb, xnT_hi)
            for g in range(NBLK):
                act.wait_ge(score_done, g + 1)
                nc.scalar.activation(prob[:, g % 2], prob[:, g % 2], ACT.Exp, scale=QD ** -0.5).then_inc(exp_done, 1)

        @block.tensor
        def _(pe):
            pe.wait_ge(id_done, 1)
            norm_pe(nc, pe, norm, bank, ident)
            pe.wait_ge(w48_done, 2)
            for i in range(NT):
                pe.wait_ge(norm["hi_done"], i + 1)
                pe.wait_ge(norm["lo_done"], i + 1)
                if i >= 2:
                    pe.wait_ge(qkv_out, i - 1)
                tok = slice(i * P, (i + 1) * P)
                n = 0
                for k in range(KT):
                    for a, w in passes(xnT_hi[:, k, tok], xnT_lo[:, k, tok], w48_hi[:, k, :], w48_lo[:, k, :]):
                        mm = nc.tensor.matmul(bank[2 + i % 2][:, 0:3 * QD], a, w, start=(n == 0), stop=(n == 3 * KT - 1))
                        n += 1
                mm.then_inc(qkv_done, 1)

        @block.vector
        def _(dve):
            for i in range(NT):
                if i % TPB == 0:
                    dve.wait_ge(x_in[i // TPB], 16)
                nc.vector.bn_stats(norm["stats"][:, i, :], x_sb[:, i, :]).then_inc(norm["stats_done"], 1)
            norm_dve_aggr(nc, dve, norm)
            dve.wait_ge(w_in, 96)
            nc.vector.tensor_reduce(w48[:, :, 0:QD], wq.rearrange("p k (d h) -> p k d h", h=NH0), AX_X,
                                    ALU.add).then_inc(w48_step, 1)
            nc.vector.tensor_reduce(b48[:, 0:QD], bq.rearrange("p (d h) -> p d h", h=NH0), AX_X,
                                    ALU.add).then_inc(w48_step, 1)
            dve.wait_ge(w48_step, 2)
            nc.vector.tensor_copy(w48_hi[:], w48[:]).then_inc(w48_done, 1)
            dve.wait_ge(w48_done, 1)
            nc.vector.tensor_tensor(w48_lo[:], w48[:], w48_hi[:], ALU.subtract).then_inc(w48_done, 1)

            norm_dve_lo(nc, dve, norm, bank, xnT_hi, xnT_lo)
            for i in range(NT):
                dve.wait_ge(qkv_done, i + 1)
                nc.vector.tensor_tensor(qkv[:, i, :], bank[2 + i % 2][:, 0:3 * QD], b48[:], ALU.add).then_inc(qkv_out, 1)
            dve.wait_ge(qkv_out, NT)
            q, k, v = (qkv[:, :, i * QD:(i + 1) * QD] for i in range(3))
            nc.vector.tensor_reduce(kext[:, 0, :], k, AX_X, ALU.max).then_inc(att_step, 1)
            nc.vector.tensor_reduce(kext[:, 1, :], k, AX_X, ALU.min).then_inc(att_step, 1)
            dve.wait_ge(att_step, 2)
            for j in range(2):
                nc.vector.tensor_tensor(smax[:, j], q, kext[:, j, :].unsqueeze(2).broadcast_to([P, NT, QD]),
                                        ALU.mult).then_inc(att_step, 1)
            dve.wait_ge(att_step, 4)
            nc.vector.tensor_tensor(smax[:, 2], smax[:, 0], smax[:, 1], ALU.max).then_inc(att_step, 1)
            dve.wait_ge(att_step, 5)
            full = [P, TPB, QD, QD]

            def scores(g):
                ts = slice(g * TPB, (g + 1) * TPB)
                nc.vector.tensor_tensor(pv[:], q[:, ts, :].unsqueeze(3).broadcast_to(full),
                                        k[:, ts, :].unsqueeze(2).broadcast_to(full), ALU.mult).then_inc(att_step, 1)
                dve.wait_ge(att_step, 6 + 4 * g)
                nc.vector.tensor_tensor(prob[:, g % 2], pv[:], smax[:, 2, ts, :].unsqueeze(3).broadcast_to(full),
                                        ALU.subtract).then_inc(score_done, 1)

            for g in range(NBLK):
                ts = slice(g * TPB, (g + 1) * TPB)
                scores(g)
                dve.wait_ge(exp_done, g + 1)
                dve.wait_ge(score_done, g + 1)
                nc.vector.tensor_reduce(den[:, ts, :], prob[:, g % 2], AX_X, ALU.add).then_inc(att_step, 1)
                nc.vector.tensor_tensor(pv[:], prob[:, g % 2], v[:, ts, :].unsqueeze(2).broadcast_to(full),
                                        ALU.mult).then_inc(att_step, 1)
                dve.wait_ge(att_step, 8 + 4 * g)
                nc.vector.tensor_reduce(num[:, ts, :], pv[:], AX_X, ALU.add).then_inc(att_step, 1)
                dve.wait_ge(att_step, 9 + 4 * g)
            c = 5 + 4 * NBLK
            nc.vector.reciprocal(smax[:, 0], den[:]).then_inc(att_step, 1)
            dve.wait_ge(att_step, c + 1)
            nc.vector.tensor_tensor(att[:], num[:], smax[:, 0], ALU.mult).then_inc(att_step, 1)
            dve.wait_ge(att_step, c + 2)
            dve.wait_ge(norm["xn_done"], NT)
            for i in range(NT):
                xv = x_sb[:, i, :].rearrange("p (d h) -> p d h", h=NH0)
                nc.vector.tensor_tensor(xv, xv, att[:, i, :].unsqueeze(2).broadcast_to([P, QD, NH0]),
                                        ALU.add).then_inc(att_step, 1)


def phase_ffn0(nc, t, sem, sb, bank, x_sb, xnT_hi, xnT_lo, w0, w1):
    h_hi, h_lo = sb("h0_hi", [P, OT0, BLK], F16), sb("h0_lo", [P, OT0, BLK], BF16)
    g, u, s = sb("g0", [P, 2, BLK]), sb("u0", [P, 2, BLK]), sb("s0", [P, 2, BLK])
    stack = [sb(f"xa_{n}", [R3, BLK], F16) for n in ("gate", "up", "down")]
    scaled = sb("scaled0", [P, 2, D])
    w1_stage = sb("w1_stage", [P, 2, W1_CHUNK])

    xa_done, stack_hi, stack_done = sem("xa_done"), sem("stack_hi"), sem("stack_done")
    gm_done, um_done, gl_done, ul_done = sem("gate_main"), sem("up_main"), sem("gate_low"), sem("up_low")
    gs_done, us_done = sem("gate_scaled"), sem("up_scaled")
    g_done, u_done, s_done = sem("gate_summed"), sem("up_summed"), sem("silu_done")
    h_done, h_hi_done, h_lo_done = sem("h0_done"), sem("h0_hi_done"), sem("h0_lo_done")
    dm_done, dl_done, scaled_done, xl_done, x_done = (sem("down_main"), sem("down_low"), sem("down_scaled"),
                                                      sem("x_low_added"), sem("x_done"))
    w1_in = [sem(f"w1_in{i}") for i in range(2)]
    w1_hi_done, w1_lo_done = sem("w1_hi_done"), sem("w1_lo_done")
    pool_turns = sem("pool_turns0")
    LR = LR_SCALE * LRA
    UNDO = 1.0 / (LRA * LRB)
    XA_GATE, XA_UP, HA, GL, UL = 6, 7, 7, 4, 5
    OUT_MAIN, OUT_LOW = (6, 0), (7, 1)
    lo_rows = slice(2 * RANK, R3)

    def upto(j, o):
        return j * OT0 + max(o + 1, 0)

    with nc.Block() as block:
        @block.sync
        def _(sp):
            def block_of_tokens(j):
                for c in range(W1_PER_BLK):
                    wait(sp, w1_lo_done, j * W1_PER_BLK + max(c - 1, 0))
                    at = (j * W1_PER_BLK + c) * W1_CHUNK
                    sp.dma_start(w1_stage[:, c % 2, :], t["w1"][:, ds(at, W1_CHUNK)]).then_inc(w1_in[c % 2], 16)

            block_of_tokens(0)
            with sp.Fori(1, NBLK) as j:
                block_of_tokens(j)

        @block.gpsimd
        def _(pool):
            def block_of_tokens(j):
                for o in range(OT0):
                    hold(pool, h_done, upto(j, o), pool_turns)
                    hold(pool, dm_done, TPB * j, pool_turns)
                    nc.gpsimd.tensor_scalar(h_hi[:, o, :], s[:, o % 2, :], 1.0, 0.0, ALU.mult, ALU.add).then_inc(h_hi_done, 1)
                    if o % 2 == 0:
                        c = o // 2
                        cols = ds((j * W1_PER_BLK + c) * W1_CHUNK, W1_CHUNK)
                        hold(pool, w1_in[c % 2], 16 * (j * (W1_PER_BLK // 2) + c // 2 + 1), pool_turns)
                        nc.gpsimd.tensor_copy(w1["hi"][:, cols], w1_stage[:, c % 2, :]).then_inc(w1_hi_done, 1)
                        hold(pool, w1_hi_done, j * W1_PER_BLK + c + 1, pool_turns)
                        nc.gpsimd.tensor_tensor(w1["lo"][:, cols], w1_stage[:, c % 2, :], w1["hi"][:, cols],
                                                ALU.subtract).then_inc(w1_lo_done, 1)

            block_of_tokens(0)
            with pool.Fori(1, NBLK) as j:
                block_of_tokens(j)

        @block.scalar
        def _(act):
            def stack_part(j, i, b):
                wait(act, xa_done, 3 * j + i + 1)
                wait(act, (gl_done, ul_done, dl_done)[i], (OT0, OT0, TPB)[i] * j)
                nc.scalar.activation(stack[i][:], bank[b][0:R3, :], ACT.Copy, scale=LR).then_inc(stack_hi, 1)

            def block_of_tokens(j):
                stack_part(j, 0, XA_GATE)
                stack_part(j, 1, XA_UP)
                for o in range(OT0 + 1):
                    if o < OT0:
                        wait(act, gm_done, upto(j, o))
                        wait(act, s_done, upto(j, o - 2))
                        nc.scalar.activation(g[:, o % 2, :], bank[o % 2][:], ACT.Copy,
                                             scale=w0["scale"][:, 0, o:o + 1]).then_inc(gs_done, 1)
                        wait(act, um_done, upto(j, o))
                        wait(act, h_done, upto(j, o - 2))
                        nc.scalar.activation(u[:, o % 2, :], bank[2 + o % 2][:], ACT.Copy,
                                             scale=w0["scale"][:, 1, o:o + 1]).then_inc(us_done, 1)
                    if o >= 1:
                        wait(act, g_done, upto(j, o - 1))
                        wait(act, h_lo_done, upto(j, o - 3))
                        nc.scalar.activation(s[:, (o - 1) % 2, :], g[:, (o - 1) % 2, :], ACT.Silu).then_inc(s_done, 1)
                stack_part(j, 2, HA)

            block_of_tokens(0)
            with act.Fori(1, NBLK) as j:
                block_of_tokens(j)

        @block.vector
        def _(dve):
            def stack_part(j, i, b):
                wait(dve, stack_hi, 3 * j + i + 1)
                nc.vector.scalar_tensor_tensor(stack[i][lo_rows, :], bank[b][lo_rows, :], LR, stack[i][lo_rows, :],
                                               ALU.mult, ALU.subtract).then_inc(stack_done, 1)

            def block_of_tokens(j):
                stack_part(j, 0, XA_GATE)
                stack_part(j, 1, XA_UP)
                for o in range(OT0 + 2):
                    if o < OT0:
                        wait(dve, gl_done, upto(j, o))
                        wait(dve, gs_done, upto(j, o))
                        nc.vector.scalar_tensor_tensor(g[:, o % 2, :], bank[GL][:], UNDO, g[:, o % 2, :],
                                                       ALU.mult, ALU.add).then_inc(g_done, 1)
                        wait(dve, ul_done, upto(j, o))
                        wait(dve, us_done, upto(j, o))
                        nc.vector.scalar_tensor_tensor(u[:, o % 2, :], bank[UL][:], UNDO, u[:, o % 2, :],
                                                       ALU.mult, ALU.add).then_inc(u_done, 1)
                    if o >= 2:
                        wait(dve, h_hi_done, upto(j, o - 2))
                        nc.vector.tensor_tensor(h_lo[:, o - 2, :], s[:, o % 2, :], h_hi[:, o - 2, :],
                                                ALU.subtract).then_inc(h_lo_done, 1)
                    if 1 <= o <= OT0:
                        wait(dve, s_done, upto(j, o - 1))
                        wait(dve, u_done, upto(j, o - 1))
                        b = (o - 1) % 2
                        nc.vector.tensor_tensor(s[:, b, :], s[:, b, :], u[:, b, :], ALU.mult).then_inc(h_done, 1)
                stack_part(j, 2, HA)
                for i in range(TPB):
                    x = x_sb[:, ds(j * TPB + i, 1), :].rearrange("p a d -> p (a d)")
                    n = TPB * j + i + 1
                    wait(dve, dm_done, n)
                    nc.vector.tensor_tensor(scaled[:, i % 2, :], bank[OUT_MAIN[i % 2]][:], w0["down_scale"][:],
                                            ALU.mult).then_inc(scaled_done, 1)
                    wait(dve, dl_done, n)
                    nc.vector.scalar_tensor_tensor(x, bank[OUT_LOW[i % 2]][:], UNDO, x, ALU.mult, ALU.add).then_inc(xl_done, 1)
                    wait(dve, xl_done, n)
                    wait(dve, scaled_done, n)
                    nc.vector.tensor_tensor(x, x, scaled[:, i % 2, :], ALU.add).then_inc(x_done, 1)

            block_of_tokens(0)
            with dve.Fori(1, NBLK) as j:
                block_of_tokens(j)

        @block.tensor
        def _(pe):
            def split_products(out, pairs):
                for n, (w, a) in enumerate(pairs):
                    mm = nc.tensor.matmul(out, w, a, start=(n == 0), stop=(n == len(pairs) - 1))
                return mm

            def block_of_tokens(j):
                tok = ds(j * BLK, BLK)
                xh = [xnT_hi[:, k, tok] for k in range(KT)]
                xl = [xnT_lo[:, k, tok] for k in range(KT)]
                Ah, Al = w0["A_hi"], w0["A_lo"]
                for i, b in ((0, XA_GATE), (1, XA_UP)):
                    wait(pe, xl_done if i else scaled_done, TPB * j)
                    split_products(bank[b][0:R3, :], [p for k in range(KT) for p in passes(
                        Ah[:, i * KT + k, :], Al[:, i * KT + k, :], xh[k], xl[k])]).then_inc(xa_done, 1)
                for o in range(OT0):
                    rows = slice(o * P, (o + 1) * P)
                    if o < 2:
                        wait(pe, x_done, TPB * j)
                    wait(pe, gs_done, upto(j, o - 2))
                    split_products(bank[o % 2][:], [(w0["gate"][:, k, rows], a) for k in range(KT)
                                                    for a in (xh[k], xl[k])]).then_inc(gm_done, 1)
                    wait(pe, us_done, upto(j, o - 2))
                    split_products(bank[2 + o % 2][:], [(w0["up"][:, k, rows], a) for k in range(KT)
                                                        for a in (xh[k], xl[k])]).then_inc(um_done, 1)
                    if o == 0:
                        wait(pe, stack_done, 3 * j + 2)
                    wait(pe, g_done, upto(j, o - 1))
                    nc.tensor.matmul(bank[GL][:], w0["B"][:, rows], stack[0][:], start=True, stop=True).then_inc(gl_done, 1)
                    wait(pe, u_done, upto(j, o - 1))
                    nc.tensor.matmul(bank[UL][:], w0["B"][:, INT0P + o * P:INT0P + (o + 1) * P], stack[1][:],
                                     start=True, stop=True).then_inc(ul_done, 1)
                for o in range(OT0):
                    wait(pe, h_lo_done, upto(j, o))
                    for n, (w, a) in enumerate(passes(Ah[:, 2 * KT + o, :], Al[:, 2 * KT + o, :], h_hi[:, o, :], h_lo[:, o, :])):
                        mm = nc.tensor.matmul(bank[HA][0:R3, :], w, a, start=(o == 0 and n == 0),
                                              stop=(o == OT0 - 1 and n == 2))
                mm.then_inc(xa_done, 1)
                for i in range(TPB):
                    ts = slice(i * P, (i + 1) * P)
                    if i < 2:
                        wait(pe, gs_done, upto(j, OT0 - 1))
                    else:
                        wait(pe, scaled_done, TPB * j + i - 1)
                    split_products(bank[OUT_MAIN[i % 2]][:], [(a[:, o, ts], w0["down"][:, o, :]) for o in range(OT0)
                                                              for a in (h_hi, h_lo)]).then_inc(dm_done, 1)
                    wait(pe, stack_done, 3 * j + 3)
                    if i >= 2:
                        wait(pe, xl_done, TPB * j + i - 1)
                    nc.tensor.matmul(bank[OUT_LOW[i % 2]][:], stack[2][:, ts], w0["B"][:, 2 * INT0P:],
                                     start=True, stop=True).then_inc(dl_done, 1)

            block_of_tokens(0)
            with pe.Fori(1, NBLK) as j:
                block_of_tokens(j)

def phase_norm1_ffn1(nc, t, sem, sb, bank, x_sb, xnT_hi, xnT_lo, ident, w1):
    norm = norm_buffers(sem, sb, "1")
    route_f = sb("route_f", [P, KT, NE])
    route_hi, route_lo = sb("route_hi", [P, KT, NE], F16), sb("route_lo", [P, KT, NE], BF16)
    gamma, beta = sb("gamma", [P, D]), sb("beta", [P, D])
    relu, sq = sb("relu1", [P, 2, BLK]), sb("sq1", [P, 2, BLK])
    h_hi, h_lo = sb("h1_hi", [P, OT1, BLK], F16), sb("h1_lo", [P, OT1, BLK], BF16)
    lat_hi, lat_lo = sb("lat_hi", [P, LT1, BLK], F16), sb("lat_lo", [P, LT1, BLK], BF16)
    exp_hi, exp_lo = sb("exp_hi", [P, LT1, BLK], F16), sb("exp_lo", [P, LT1, BLK], BF16)
    top, rw = sb("top8", [P, TPB, 8]), sb("rw", [P, TPB])
    routed, y = sb("routed", [P, 2, D]), sb("y1", [P, TPB, D])
    stats, mv, small = sb("stats_y", [P, TPB, 6]), sb("mv_y", [P, TPB, 2]), sb("small_y", [P, 7, TPB])

    in1, route_split = sem("ffn1_in"), sem("route_split")
    beta_done = sem("beta_added")
    lat_mm, lat_hi_done, lat_lo_done = sem("lat_mm"), sem("lat_hi_done"), sem("lat_lo_done")
    exp_mm, exp_hi_done, exp_lo_done = sem("exp_mm"), sem("exp_hi_done"), sem("exp_lo_done")
    route_mm, top_done, rw_done = sem("route_mm"), sem("top_done"), sem("rw_done")
    up_mm, relu_done, sq_done, h_hi_done, h_lo_done = (sem("up1_mm"), sem("relu_done"), sem("sq_done"),
                                                       sem("h1_hi_done"), sem("h1_lo_done"))
    fc2_mm, down_mm, routed_done, y_done = sem("fc2_mm"), sem("down1_mm"), sem("routed_done"), sem("y_done")
    ystep, yvar, ysd, yn_done, yg_done, x1_done = (sem("y_norm_step"), sem("y_var"), sem("y_sd"), sem("yn_done"),
                                                   sem("y_gamma"), sem("x1_done"))
    pool_turns, dve_turns = sem("pool_turns1"), sem("dve_turns1")
    LAT_BANK, EXP_BANK, FC2_BANK, DOWN_BANK, ROUTE_BANK = (3, 4), (5, 6), (3, 4), (5, 6), 2
    YSTEPS = 2 * TPB + 6

    def w1_tile(offset, k, width, at, n=P):
        a = offset + k * width + at
        return w1["hi"][:, a:a + n], w1["lo"][:, a:a + n]

    with nc.Block() as block:
        @block.sync
        def _(sp):
            sp.dma_start(route_f[:], t["route_w"]).then_inc(in1, 16)
            sp.dma_start(gamma[:], t["gamma"].partition_broadcast(P)).then_inc(in1, 16)
            sp.dma_start(beta[:], t["beta"].partition_broadcast(P)).then_inc(in1, 16)

        @block.gpsimd
        def _(pool):
            hold(pool, in1, 48, pool_turns)
            nc.gpsimd.tensor_copy(route_hi[:], route_f[:]).then_inc(route_split, 1)
            hold(pool, route_split, 1, pool_turns)
            nc.gpsimd.tensor_tensor(route_lo[:], route_f[:], route_hi[:], ALU.subtract).then_inc(route_split, 1)
            hold(pool, norm["xn_done"], NT, pool_turns)
            def block_of_tokens(j):
                for i in range(TPB):
                    x = x_sb[:, ds(j * TPB + i, 1), :].rearrange("p a d -> p (a d)")
                    nc.gpsimd.tensor_tensor(x, x, beta[:], ALU.add).then_inc(beta_done, 1)
                for o in range(OT1):
                    hold(pool, sq_done, OT1 * j + o + 1, pool_turns)
                    hold(pool, down_mm, TPB * j, pool_turns)
                    nc.gpsimd.tensor_scalar(h_hi[:, o, :], sq[:, o % 2, :], 1.0, 0.0, ALU.mult, ALU.add).then_inc(h_hi_done, 1)

            block_of_tokens(0)
            with pool.Fori(1, NBLK) as j:
                block_of_tokens(j)

        @block.scalar
        def _(act):
            norm_act(nc, act, norm, bank, x_sb, xnT_hi)

            def up_part(j, os):
                for o in os:
                    wait(act, relu_done, OT1 * j + o + 1)
                    wait(act, h_lo_done, OT1 * j + max(o - 1, 0))
                    nc.scalar.activation(sq[:, o % 2, :], relu[:, o % 2, :], ACT.Square).then_inc(sq_done, 1)

            def hi_part(j, dst, mm, banks, done, readers, per):
                for l in range(LT1):
                    wait(act, mm, LT1 * j + l + 1)
                    wait(act, readers, per * j)
                    nc.scalar.activation(dst[:, l, :], bank[banks[l]][:], ACT.Copy).then_inc(done, 1)

            def block_of_tokens(j):
                hi_part(j, lat_hi, lat_mm, LAT_BANK, lat_hi_done, exp_mm, LT1)
                up_part(j, range(OT1 // 2))
                hi_part(j, exp_hi, exp_mm, EXP_BANK, exp_hi_done, fc2_mm, TPB)
                up_part(j, range(OT1 // 2, OT1))
                for i in range(TPB):
                    n = TPB * j + i + 1
                    wait(act, fc2_mm, n)
                    wait(act, rw_done, j + 1)
                    wait(act, y_done, TPB * j + max(i - 1, 0))
                    nc.scalar.activation(routed[:, i % 2, :], bank[FC2_BANK[i % 2]][:], ACT.Copy,
                                         scale=rw[:, i:i + 1]).then_inc(routed_done, 1)
                wait(act, yvar, j + 1)
                nc.scalar.activation(small[:, 1, :], small[:, 0, :], ACT.Sqrt).then_inc(ysd, 1)
                wait(act, ystep, YSTEPS * (j + 1))
                for i in range(TPB):
                    nc.scalar.activation(y[:, i, :], y[:, i, :], ACT.Identity, scale=small[:, 5, i:i + 1],
                                         bias=small[:, 6, i:i + 1]).then_inc(yn_done, 1)

            block_of_tokens(0)
            with act.Fori(1, NBLK) as j:
                block_of_tokens(j)

        @block.vector
        def _(dve):
            for i in range(NT):
                nc.vector.bn_stats(norm["stats"][:, i, :], x_sb[:, i, :]).then_inc(norm["stats_done"], 1)
            norm_dve_aggr(nc, dve, norm)
            norm_dve_lo(nc, dve, norm, bank, xnT_hi, xnT_lo)

            def lo_part(j, hi, lo, banks, hi_done, done):
                for l in range(LT1):
                    wait(dve, hi_done, LT1 * j + l + 1)
                    nc.vector.tensor_tensor(lo[:, l, :], bank[banks[l]][:], hi[:, l, :], ALU.subtract).then_inc(done, 1)

            def up_part(j, os):
                for o in os:
                    if o < OT1:
                        wait(dve, up_mm, OT1 * j + o + 1)
                        wait(dve, sq_done, OT1 * j + max(o - 1, 0))
                        nc.vector.tensor_scalar(relu[:, o % 2, :], bank[o % 2][:], 0.0, SQ_DOWN, ALU.max,
                                                ALU.mult).then_inc(relu_done, 1)
                    if o >= 1:
                        wait(dve, h_hi_done, OT1 * j + o)
                        nc.vector.tensor_tensor(h_lo[:, o - 1, :], sq[:, (o - 1) % 2, :], h_hi[:, o - 1, :],
                                                ALU.subtract).then_inc(h_lo_done, 1)

            def block_of_tokens(j):
                lo_part(j, lat_hi, lat_lo, LAT_BANK, lat_hi_done, lat_lo_done)
                hold(dve, route_mm, j + 1, dve_turns)
                hold(dve, routed_done, TPB * j, dve_turns)
                for i in range(TPB):
                    nc.vector.max(top[:, i, :], bank[ROUTE_BANK][:, i * NE:(i + 1) * NE]).then_inc(top_done, 1)
                wait(dve, top_done, TPB * (j + 1))
                nc.vector.tensor_tensor(rw[:], top[:, :, 0], top[:, :, 1], ALU.add).then_inc(rw_done, 1)
                up_part(j, range(OT1 // 2))
                lo_part(j, exp_hi, exp_lo, EXP_BANK, exp_hi_done, exp_lo_done)
                up_part(j, range(OT1 // 2, OT1 + 1))
                c = YSTEPS * j
                for i in range(TPB):
                    n = TPB * j + i + 1
                    wait(dve, down_mm, n)
                    wait(dve, routed_done, n)
                    wait(dve, x1_done, TPB * j)
                    nc.vector.scalar_tensor_tensor(y[:, i, :], bank[DOWN_BANK[i % 2]][:], 1.0 / SQ_DOWN ** 2,
                                                   routed[:, i % 2, :], ALU.mult, ALU.add).then_inc(y_done, 1)
                    wait(dve, y_done, n)
                    nc.vector.bn_stats(stats[:, i, :], y[:, i, :]).then_inc(ystep, 1)
                hold(dve, ystep, c + TPB, dve_turns)
                for i in range(TPB):
                    nc.vector.bn_aggr(mv[:, i, :], stats[:, i, :]).then_inc(ystep, 1)
                norm_small(nc, dve, (ystep, c + 2 * TPB), small, mv, TPB, ysd, j + 1, yvar)
                for i in range(TPB):
                    n = TPB * j + i + 1
                    x = x_sb[:, ds(j * TPB + i, 1), :].rearrange("p a d -> p (a d)")
                    wait(dve, yn_done, n)
                    nc.vector.tensor_tensor(y[:, i, :], y[:, i, :], gamma[:], ALU.mult).then_inc(yg_done, 1)
                    wait(dve, yg_done, n)
                    wait(dve, beta_done, n)
                    nc.vector.tensor_tensor(x, x, y[:, i, :], ALU.add).then_inc(x1_done, 1)

            block_of_tokens(0)
            with dve.Fori(1, NBLK) as j:
                block_of_tokens(j)

        @block.tensor
        def _(pe):
            norm_pe(nc, pe, norm, bank, ident)
            wait(pe, norm["hi_done"], NT)
            wait(pe, norm["lo_done"], NT)
            wait(pe, route_split, 2)

            def products(out, pairs):
                for n, (w, a) in enumerate(pairs):
                    mm = nc.tensor.matmul(out, w, a, start=(n == 0), stop=(n == len(pairs) - 1))
                return mm

            def block_of_tokens(j):
                tok = ds(j * BLK, BLK)
                xh = [xnT_hi[:, k, tok] for k in range(KT)]
                xl = [xnT_lo[:, k, tok] for k in range(KT)]

                def up_part(os):
                    for o in os:
                        wait(pe, relu_done, OT1 * j + max(o - 1, 0))
                        products(bank[o % 2][:], [p for k in range(KT) for p in passes(
                            *w1_tile(W1_UP, k, INT1, o * P), xh[k], xl[k])]).then_inc(up_mm, 1)

                for l in range(LT1):
                    wait(pe, routed_done, TPB * j)
                    products(bank[LAT_BANK[l]][:], [p for k in range(KT) for p in passes(
                        *w1_tile(W1_FC1, k, LAT, l * P), xh[k], xl[k])]).then_inc(lat_mm, 1)
                wait(pe, rw_done, j)
                for i in range(TPB):
                    ts = ds(j * BLK + i * P, P)
                    mm = products(bank[ROUTE_BANK][:, i * NE:(i + 1) * NE], [p for k in range(KT) for p in passes(
                        xnT_hi[:, k, ts], xnT_lo[:, k, ts], route_hi[:, k, :], route_lo[:, k, :])])
                mm.then_inc(route_mm, 1)
                up_part(range(OT1 // 2))
                wait(pe, lat_lo_done, LT1 * (j + 1))
                wait(pe, y_done, TPB * j)
                for m in range(LT1):
                    products(bank[EXP_BANK[m]][:], [p for l in range(LT1) for p in passes(
                        *w1_tile(W1_EXP, l, LAT, m * P), lat_hi[:, l, :], lat_lo[:, l, :])]).then_inc(exp_mm, 1)
                up_part(range(OT1 // 2, OT1))
                wait(pe, exp_lo_done, LT1 * (j + 1))
                for i in range(TPB):
                    ts = slice(i * P, (i + 1) * P)
                    wait(pe, routed_done, TPB * j + max(i - 1, 0))
                    products(bank[FC2_BANK[i % 2]][:], [p for l in range(LT1) for p in passes(
                        exp_hi[:, l, ts], exp_lo[:, l, ts], *w1_tile(W1_FC2, l, D, 0, D))]).then_inc(fc2_mm, 1)
                    if i == 0:
                        wait(pe, h_lo_done, OT1 * (j + 1))
                    wait(pe, y_done, TPB * j + max(i - 1, 0))
                    products(bank[DOWN_BANK[i % 2]][:], [p for o in range(OT1) for p in passes(
                        h_hi[:, o, ts], h_lo[:, o, ts], *w1_tile(W1_DOWN, o, D, 0, D))]).then_inc(down_mm, 1)

            block_of_tokens(0)
            with pe.Fori(1, NBLK) as j:
                block_of_tokens(j)


def phase_attn1(nc, t, sem, sb, bank, x_sb, xnT_hi, xnT_lo, ident):
    Q, K, V, G, OW = range(5)
    NSLOT = 8
    NIT = 2 * HEADS
    NST = 2 * CPH - 1
    w_stage = sb("w_stage", [P, 5, D + 1])
    w_hi, w_lo = sb("w_hi", [P, 5, D], F16), sb("w_lo", [P, 5, D], BF16)
    q_hi, q_lo = sb("q_hi", [P, 2, SEQ], F16), sb("q_lo", [P, 2, SEQ], BF16)
    qd_hi, qd_lo = sb("qd_hi", [P, 2, SEQ], F16), sb("qd_lo", [P, 2, SEQ], BF16)
    k_hi, k_lo = sb("k_hi", [P, 2, SEQ], F16), sb("k_lo", [P, 2, SEQ], BF16)
    v_hi, v_lo = sb("v_hi", [P, 2, SEQ], F16), sb("v_lo", [P, 2, SEQ], BF16)
    k_f, v_f = sb("k_f", [P, SEQ]), sb("v_f", [P, SEQ])
    ident_hi, ident_lo = sb("ident_hi", [P, P], F16), sb("ident_lo", [P, P], BF16)
    gate = sb("gate1", [P, 2, SEQ])
    kT_hi, kT_lo = sb("kT_hi", [P, SEQ], F16), sb("kT_lo", [P, SEQ], BF16)
    vd_hi, vd_lo = sb("vd_hi", [P, SEQ], F16), sb("vd_lo", [P, SEQ], BF16)
    p_hi, p_lo = sb("p_hi", [P, SEQ], F16), sb("p_lo", [P, SEQ], BF16)
    st_f = sb("st_f", [P, NST + 1, HD])
    st_hi, st_lo = sb("st_hi", [P, NST + 1, HD], F16), sb("st_lo", [P, NST + 1, HD], BF16)
    sq = sb("sq", [P, SEQ])
    g_hi, g_lo = sb("g_hi", [P, SEQ], F16), sb("g_lo", [P, SEQ], BF16)
    ssum = sb("ssum", [P, TOK])
    y = sb("y_sum", [P, NT, D])
    decay = sb("decay", [P, CH + 2])
    q_decay = sb("q_decay", [P, CH])
    ones = sb("ones", [P, 1])
    small, mv = sb("small2", [P, 7, NT]), sb("mv2", [P, NT, 2])
    KT_BANK, SC_BANK, U_BANK, O_BANK, C_BANK, SS_BANK = (2, 4), 3, 4, (5, 7), (6, 7), 2

    w_in, w_done = [sem(f"w_in{m}") for m in range(5)], [sem(f"w_split{m}") for m in range(5)]
    w_step, qd_in, decay_in = sem("w_step"), sem("q_decay_in"), sem("decay_in")
    proj_done, act_done = sem("proj_done"), sem("proj_act_done")
    q_hi_done, q_lo_done, qd_done, qd_hi_done, qd_lo_done = (sem("q_hi_done"), sem("q_lo_done"), sem("qd_done"),
                                                             sem("qd_hi_done"), sem("qd_lo_done"))
    kv_hi_done, kv_lo_done = sem("kv_hi_done"), sem("kv_lo_done")
    kT_done, kT_hi_done, kT_lo_done = sem("kT_done"), sem("kT_hi_done"), sem("kT_lo_done")
    vd_done, vd_hi_done, vd_lo_done, ident_done = sem("vd_done"), sem("vd_hi_done"), sem("vd_lo_done"), sem("ident_done")
    sc_done, pm_done, p_hi_done, p_lo_done = sem("sc_done"), sem("pm_done"), sem("p_hi_done"), sem("p_lo_done")
    upd_done, st_done, st_hi_done, st_lo_done = sem("upd_done"), sem("st_done"), sem("st_hi_done"), sem("st_lo_done")
    o_done, sq_done, g_done, g_hi_done, g_lo_done = (sem("o_done"), sem("sq_done"), sem("g_done"), sem("g_hi_done"),
                                                     sem("g_lo_done"))
    ss_zero, ss_done, c_done, y_done = sem("ss_zero"), sem("ss_done"), sem("c_done"), sem("y_done")
    ones_done, ss_mm, rms_step, rms_var, rms_sd = (sem("ones_done"), sem("ss_mm"), sem("rms_step"), sem("rms_var"),
                                                   sem("rms_sd"))
    out_ready, out_written, pool_turns = sem("out_ready"), sem("out_written"), sem("pool_turns")
    sp_turns = sem("sp_turns")
    Y0 = 2

    def half(b):
        return slice(b * BLK, (b + 1) * BLK)

    def chunks4(ap):
        return ap.rearrange("p (c n) -> p c n", c=CPH)

    with nc.Block() as block:
        @block.sync
        def _(sp):
            def load(m, h):
                if m == OW:
                    sp.dma_start(w_stage[:, OW, :], t["out_w"][h]).then_inc(w_in[m], 16)
                else:
                    sp.dma_start(w_stage[:, m, 0:D].rearrange("p (k d) -> p k d", k=KT), t["proj_w"][h, :, m]).then_inc(w_in[m], 16)

            def load_q_decay(h):
                sp.dma_start(q_decay[:], t["q_decay"][h].partition_broadcast(P)).then_inc(qd_in, 16)

            def load_decay(h):
                sp.dma_start(decay[:], t["decay"][h]).then_inc(decay_in, 16)

            for m in (Q, K, V, G, OW):
                load(m, 0)
            load_q_decay(0)
            load_decay(0)
            with sp.Fori(1, HEADS) as h:
                for m in (Q, K, V, G):
                    hold(sp, w_done[m], h, sp_turns)
                    load(m, h)
                hold(sp, qd_done, 4 * h, sp_turns)
                load_q_decay(h)
                hold(sp, w_done[OW], h, sp_turns)
                load(OW, h)
                hold(sp, pm_done, 4 * h, sp_turns)
                hold(sp, vd_done, 4 * h, sp_turns)
                hold(sp, st_done, 2 * NST * h, sp_turns)
                load_decay(h)
            out = t["out"].rearrange("(t p) d -> p t d", p=P)
            for i in range(NT):
                sp.wait_ge(out_ready, i + 1)
                sp.dma_start(out[:, i, :], x_sb[:, i, :]).then_inc(out_written, 16)
            sp.wait_ge(out_written, 16 * NT)

        @block.gpsimd
        def _(pool):
            def split(dst_hi, dst_lo, src, hi_done, hi_want, lo_done):
                nc.gpsimd.tensor_scalar(dst_hi, src, 1.0, 0.0, ALU.mult, ALU.add).then_inc(hi_done, 1)
                hold(pool, hi_done, hi_want, pool_turns)
                nc.gpsimd.tensor_tensor(dst_lo, src, dst_hi, ALU.subtract).then_inc(lo_done, 1)

            def split_proj(m, h, step):
                hold(pool, w_in[m], 16 * (h + 1), pool_turns)
                split(w_hi[:, m, :], w_lo[:, m, :], w_stage[:, m, 0:D], w_step, step, w_done[m])

            def split_out(h, step):
                hold(pool, w_in[OW], 16 * (h + 1), pool_turns)
                nc.gpsimd.tensor_scalar(w_stage[:, OW, 0:D], w_stage[:, OW, 0:D], w_stage[:, OW, D:D + 1], 0.5,
                                        ALU.mult, ALU.mult).then_inc(w_step, 1)
                hold(pool, w_step, step - 1, pool_turns)
                split(w_hi[:, OW, :], w_lo[:, OW, :], w_stage[:, OW, 0:D], w_step, step, w_done[OW])

            def split_kv(i, b, n):
                src, hi, lo = ((k_f, k_hi, k_lo), (v_f, v_hi, v_lo))[n // 2]
                hold(pool, act_done, NSLOT * i + 3 + n, pool_turns)
                split(hi[:, b, half(n % 2)], lo[:, b, half(n % 2)], src[:, half(n % 2)], kv_hi_done, 4 * i + n + 1,
                      kv_lo_done)

            def split_decayed(i):
                for n in range(2):
                    hold(pool, vd_done, 2 * (i - 1) + n + 1, pool_turns)
                    split(vd_hi[:, half(n)], vd_lo[:, half(n)], v_f[:, half(n)], vd_hi_done, 2 * (i - 1) + n + 1, vd_lo_done)

            def squares(i, b):
                for n in range(2):
                    cols = slice((1 - b) * SEQ + n * BLK, (1 - b) * SEQ + (n + 1) * BLK)
                    hold(pool, sq_done, 2 * (i - 1) + n + 1, pool_turns)
                    nc.gpsimd.tensor_tensor(ssum[:, cols], ssum[:, cols], sq[:, half(n)], ALU.add).then_inc(ss_done, 1)

            nc.gpsimd.memset(ssum[:], 0.0).then_inc(ss_zero, 1)
            nc.gpsimd.memset(ones[:], 1.0).then_inc(ones_done, 1)
            nc.gpsimd.tensor_copy(ident_hi[:], ident[:]).then_inc(ident_done, 1)
            nc.gpsimd.tensor_copy(ident_lo[:], ident[:]).then_inc(ident_done, 1)
            for m in (Q, K, V, G):
                split_proj(m, 0, m + 1)
            for n in range(4):
                split_kv(0, 0, n)
            pool.wait_ge(ss_zero, 1)
            with pool.Fori(1, HEADS) as h:
                i, step = 2 * h - 1, 4 + 6 * (h - 1)
                split_decayed(i)
                split_kv(i, 1, 0)
                hold(pool, proj_done, NSLOT * i + 2, pool_turns)
                split_proj(Q, h, step + 1)
                split_kv(i, 1, 1)
                split_kv(i, 1, 2)
                hold(pool, proj_done, NSLOT * i + 4, pool_turns)
                split_proj(K, h, step + 2)
                split_kv(i, 1, 3)
                hold(pool, y_done, Y0 + 2 * NSLOT * (h - 1), pool_turns)
                split_out(h - 1, step + 4)
                hold(pool, proj_done, NSLOT * i + 6, pool_turns)
                split_proj(V, h, step + 5)
                squares(i, 1)
                split_decayed(i + 1)
                hold(pool, proj_done, NSLOT * (i + 1), pool_turns)
                split_proj(G, h, step + 6)
                for n in range(4):
                    split_kv(i + 1, 0, n)
                squares(i + 1, 0)
            i = NIT - 1
            split_decayed(i)
            for n in range(4):
                split_kv(i, 1, n)
            pool.wait_ge(y_done, Y0 + 2 * NSLOT * (HEADS - 1))
            split_out(HEADS - 1, 4 + 6 * (HEADS - 1) + 2)
            squares(i, 1)
            split_decayed(i + 1)
            squares(i + 1, 0)

        @block.scalar
        def _(act):
            def projection(i, b, s):
                act.wait_ge(proj_done, NSLOT * i + s + 1)
                src, n = bank[s % 2][:], s % 2
                if s // 2 == Q:
                    nc.scalar.activation(src, src, ACT.Silu).then_inc(act_done, 1)
                    act.wait_ge(act_done, NSLOT * i + s + 1)
                    nc.scalar.activation(q_hi[:, b, half(n)], src, ACT.Copy).then_inc(q_hi_done, 1)
                elif s // 2 == G:
                    nc.scalar.activation(gate[:, b, half(n)], src, ACT.Tanh, scale=0.5).then_inc(act_done, 1)
                else:
                    if s // 2 == K:
                        wait(act, kv_lo_done, 4 * (i - 1) + s - 1)
                    else:
                        wait(act, vd_lo_done, 2 * (i - 1) + n + 1)
                    dst = (k_f if s // 2 == K else v_f)[:, half(n)]
                    nc.scalar.activation(dst, src, ACT.Silu).then_inc(act_done, 1)

            def hi_part(i, s):
                a = i - 1
                n = {0: 0, 1: 1, 2: 0, 3: 0, 4: 1, 5: 1, 6: 0, 7: 1}[s]
                if s < 2:
                    act.wait_ge(kv_lo_done, 4 * a + 3 + n)
                    if n == 0:
                        wait(act, decay_in, decay_loads(i))
                    nc.scalar.activation(v_f[:, half(n)], v_f[:, half(n)], ACT.Copy,
                                         scale=decay[:, CH:CH + 1]).then_inc(vd_done, 1)
                    act.wait_ge(kT_done, 2 * a + n + 1)
                    nc.scalar.activation(kT_hi[:, half(n)], bank[KT_BANK[n]][:, 0:BLK // 2].bitcast(F16),
                                         ACT.Copy).then_inc(kT_hi_done, 1)
                elif s in (2, 4):
                    act.wait_ge(pm_done, 2 * a + n + 1)
                    nc.scalar.activation(p_hi[:, half(n)], bank[SC_BANK][:], ACT.Copy).then_inc(p_hi_done, 1)
                elif s in (3, 5):
                    c = slice(1, CPH + 1) if n == 0 else slice(CPH + 1, NST + 1)
                    act.wait_ge(st_done, NST * a + (CPH if n == 0 else NST))
                    nc.scalar.activation(st_hi[:, c, :], st_f[:, c, :], ACT.Copy).then_inc(st_hi_done, 1)
                else:
                    act.wait_ge(o_done, 2 * a + n + 1)
                    wait(act, ss_done, 2 * (a - 1) + n + 1)
                    nc.scalar.activation(sq[:, half(n)], bank[O_BANK[n]][:], ACT.Square).then_inc(sq_done, 1)
                    act.wait_ge(g_done, 2 * a + n + 1)
                    nc.scalar.activation(g_hi[:, half(n)], bank[O_BANK[n]][:], ACT.Copy).then_inc(g_hi_done, 1)

            def scaled_queries(i, b, n):
                act.wait_ge(qd_done, 2 * i + n + 1)
                nc.scalar.activation(qd_hi[:, b, half(n)], bank[n][:], ACT.Copy).then_inc(qd_hi_done, 1)

            def iteration(i, b, project, attend):
                for s in range(NSLOT):
                    if project:
                        projection(i, b, s)
                    if attend:
                        hi_part(i, s)
                    if project and s < 2:
                        scaled_queries(i, b, s)

            def decay_loads(i):
                return decay_of[0]

            decay_of = [16]
            iteration(0, 0, True, False)
            iteration(1, 1, True, True)
            with act.Fori(1, HEADS) as h:
                decay_of[0] = 16 * h
                iteration(2 * h, 0, True, True)
                decay_of[0] = 16 * (h + 1)
                iteration(2 * h + 1, 1, True, True)
            decay_of[0] = 16 * HEADS
            iteration(NIT, 0, False, True)
            act.wait_ge(rms_var, 1)
            nc.scalar.activation(small[:, 1, :], small[:, 0, :], ACT.Sqrt).then_inc(rms_sd, 1)

        @block.vector
        def _(dve):
            def queries(i, b, n, want):
                dve.wait_ge(q_hi_done, 2 * i + n + 1)
                nc.vector.tensor_tensor(q_lo[:, b, half(n)], bank[n][:], q_hi[:, b, half(n)],
                                        ALU.subtract).then_inc(q_lo_done, 1)
                if n == 0:
                    dve.wait_ge(qd_in, want)
                dve.wait_ge(q_lo_done, 2 * i + n + 1)
                nc.vector.tensor_tensor(chunks4(bank[n][:]), chunks4(bank[n][:]),
                                        q_decay[:].unsqueeze(1).broadcast_to([P, CPH, CH]), ALU.mult).then_inc(qd_done, 1)

            def scaled_queries_lo(i, b, n):
                dve.wait_ge(qd_hi_done, 2 * i + n + 1)
                nc.vector.tensor_tensor(qd_lo[:, b, half(n)], bank[n][:], qd_hi[:, b, half(n)],
                                        ALU.subtract).then_inc(qd_lo_done, 1)

            def keys_lo(a, n):
                dve.wait_ge(kT_hi_done, 2 * a + n + 1)
                nc.vector.tensor_copy(kT_lo[:, half(n)], bank[KT_BANK[n]][:, BLK // 2:].bitcast(BF16)).then_inc(kT_lo_done, 1)

            def mask_scores(a, n):
                dve.wait_ge(sc_done, 2 * a + n + 1)
                dve.wait_ge(vd_done, 2 * a + n + 1)
                nc.vector.tensor_tensor(chunks4(bank[SC_BANK][:]), chunks4(bank[SC_BANK][:]),
                                        decay[:, 0:CH].unsqueeze(1).broadcast_to([P, CPH, CH]), ALU.mult).then_inc(pm_done, 1)

            def scores_lo(a, n):
                dve.wait_ge(p_hi_done, 2 * a + n + 1)
                nc.vector.tensor_tensor(p_lo[:, half(n)], bank[SC_BANK][:], p_hi[:, half(n)],
                                        ALU.subtract).then_inc(p_lo_done, 1)

            def states(a, n):
                dve.wait_ge(upd_done, 2 * a + n + 1)
                wait(dve, st_hi_done, 2 * a)
                for c in (range(CPH) if n == 0 else range(CPH, NST)):
                    u = bank[U_BANK][:, (c % CPH) * HD:(c % CPH + 1) * HD]
                    if c == 0:
                        nc.vector.tensor_copy(st_f[:, 1, :], u).then_inc(st_done, 1)
                    else:
                        dve.wait_ge(st_done, NST * a + c)
                        nc.vector.scalar_tensor_tensor(st_f[:, c + 1, :], st_f[:, c, :], decay[:, CH + 1:CH + 2], u,
                                                       ALU.mult, ALU.add).then_inc(st_done, 1)

            def states_lo(a, n):
                c = slice(1, CPH + 1) if n == 0 else slice(CPH + 1, NST + 1)
                dve.wait_ge(st_hi_done, 2 * a + n + 1)
                nc.vector.tensor_tensor(st_lo[:, c, :], st_f[:, c, :], st_hi[:, c, :], ALU.subtract).then_inc(st_lo_done, 1)

            def gated(a, b, n):
                dve.wait_ge(sq_done, 2 * a + n + 1)
                dve.wait_ge(act_done, NSLOT * a + 2 * G + n + 1)
                nc.vector.scalar_tensor_tensor(bank[O_BANK[n]][:], gate[:, b, half(n)], 1.0, bank[O_BANK[n]][:],
                                               ALU.add, ALU.mult).then_inc(g_done, 1)
                dve.wait_ge(g_hi_done, 2 * a + n + 1)
                nc.vector.tensor_tensor(g_lo[:, half(n)], bank[O_BANK[n]][:], g_hi[:, half(n)],
                                        ALU.subtract).then_inc(g_lo_done, 1)

            def add_out(i, b, tiles):
                for n in tiles:
                    dve.wait_ge(c_done, NSLOT * (i - 2) + n + 1)
                    yt = y[:, b * (NT // 2) + n, :]
                    nc.vector.tensor_tensor(yt, bank[C_BANK[n % 2]][:], yt, ALU.add).then_inc(y_done, 1)

            def iteration(i, b, project, attend, output, qd_want=None):
                a, ab = i - 1, 1 - b
                for s in range(NSLOT):
                    n = {0: 0, 1: 1, 2: 0, 3: 0, 4: 1, 5: 1, 6: 0, 7: 1}[s]
                    if project and s < 2:
                        queries(i, b, s, qd_want)
                    if attend:
                        if s < 2:
                            keys_lo(a, n)
                        elif s in (2, 4):
                            mask_scores(a, n)
                        elif s in (3, 5):
                            states(a, n)
                        else:
                            gated(a, ab, n)
                    if output and 1 <= s <= 4:
                        add_out(i, b, (2 * s - 2, 2 * s - 1))
                    if project and s < 2:
                        scaled_queries_lo(i, b, s)
                    if attend and s in (2, 4):
                        scores_lo(a, n)
                    if attend and s in (3, 5):
                        states_lo(a, n)

            for b in range(2):
                nc.vector.memset(y[:, b * (NT // 2):(b + 1) * (NT // 2), :], 0.0).then_inc(y_done, 1)
            dve.wait_ge(y_done, Y0)
            iteration(0, 0, True, False, False, 16)
            iteration(1, 1, True, True, False, 16)
            with dve.Fori(1, HEADS) as h:
                iteration(2 * h, 0, True, True, True, 16 * (h + 1))
                iteration(2 * h + 1, 1, True, True, True, 16 * (h + 1))
            iteration(NIT, 0, False, True, True)
            iteration(NIT + 1, 1, False, False, True)
            dve.wait_ge(ss_mm, 1)
            nc.vector.tensor_scalar(mv[:, :, 1], bank[SS_BANK][:, 0:NT], 1.0 / (HEADS * HD), None, ALU.mult).then_inc(rms_step, 1)
            nc.vector.memset(mv[:, :, 0], 0.0).then_inc(rms_step, 1)
            norm_small(nc, dve, (rms_step, 2), small, mv, NT, rms_sd, 1, rms_var)
            dve.wait_ge(rms_step, 8)
            dve.wait_ge(y_done, Y0 + NSLOT * NIT)
            for i in range(NT):
                nc.vector.scalar_tensor_tensor(x_sb[:, i, :], y[:, i, :], small[:, 5, i:i + 1], x_sb[:, i, :],
                                               ALU.mult, ALU.add).then_inc(out_ready, 1)

        @block.tensor
        def _(pe):
            def group(out, pairs, start=True, stop=True):
                for n, (w, a) in enumerate(pairs):
                    mm = nc.tensor.matmul(out, w, a, start=start and n == 0, stop=stop and n == len(pairs) - 1)
                return mm

            def w_tile(m, k):
                return w_hi[:, m, k * P:(k + 1) * P], w_lo[:, m, k * P:(k + 1) * P]

            def projection(i, b, s, h):
                m, n = s // 2, s % 2
                if n == 0 and b == 0:
                    pe.wait_ge(w_done[m], h + 1)
                if m == K:
                    pe.wait_ge(qd_lo_done, 2 * i + n + 1)
                else:
                    wait(pe, act_done, NSLOT * i + s - 1)
                if m == V:
                    for c in range(CPH):
                        at = b * SEQ + n * BLK + c * CH
                        mm = group(bank[s % 2][:, c * HD:(c + 1) * HD], [p for k in range(KT) for p in passes(
                            xnT_hi[:, k, at:at + CH], xnT_lo[:, k, at:at + CH], *w_tile(V, k))])
                else:
                    at = b * SEQ + n * BLK
                    mm = group(bank[s % 2][:], [p for k in range(KT) for p in passes(
                        *w_tile(m, k), xnT_hi[:, k, at:at + BLK], xnT_lo[:, k, at:at + BLK])])
                mm.then_inc(proj_done, 1)

            def keys(a, b, n):
                pe.wait_ge(kv_lo_done, 4 * a + n + 1)
                if n == 0:
                    wait(pe, kT_lo_done, 2 * a)
                else:
                    wait(pe, st_done, NST * a)
                for c in range(CPH):
                    at = n * BLK + c * CH
                    for part, src, one, dt in ((0, k_hi, ident_hi, F16), (1, k_lo, ident_lo, BF16)):
                        out = bank[KT_BANK[n]][:, part * BLK // 2:(part + 1) * BLK // 2].bitcast(dt)
                        mm = nc.tensor.transpose(out[:, c * CH:(c + 1) * CH], src[:, b, at:at + CH], one[:])
                mm.then_inc(kT_done, 1)

            def scores(a, b, n):
                pe.wait_ge(kv_lo_done, 4 * a + n + 1)
                pe.wait_ge(q_lo_done, 2 * a + n + 1)
                wait(pe, p_lo_done, 2 * a + n)
                for c in range(CPH):
                    ts = slice(n * BLK + c * CH, n * BLK + (c + 1) * CH)
                    mm = group(bank[SC_BANK][:, c * CH:(c + 1) * CH], passes(
                        k_hi[:, b, ts], k_lo[:, b, ts], q_hi[:, b, ts], q_lo[:, b, ts]))
                mm.then_inc(sc_done, 1)

            def update(a, b, n):
                pe.wait_ge(kT_lo_done, 2 * a + 2)
                pe.wait_ge(vd_lo_done, 2 * a + n + 1)
                wait(pe, st_done, NST * a + n * CPH)
                for c in range(CPH if n == 0 else CPH - 1):
                    ts = slice(n * BLK + c * CH, n * BLK + (c + 1) * CH)
                    mm = group(bank[U_BANK][:, c * HD:(c + 1) * HD], passes(
                        kT_hi[:, ts], kT_lo[:, ts], vd_hi[:, ts], vd_lo[:, ts]))
                mm.then_inc(upd_done, 1)

            def attention(a, b, n):
                pe.wait_ge(p_lo_done, 2 * a + n + 1)
                pe.wait_ge(st_lo_done, 2 * a + n + 1)
                pe.wait_ge(qd_lo_done, 2 * a + n + 1)
                if n == 0:
                    wait(pe, g_lo_done, 2 * a + n)
                else:
                    wait(pe, y_done, Y0 + NSLOT * (a - 1) + NSLOT)
                for c in range(CPH):
                    chunk = n * CPH + c
                    ts = slice(n * BLK + c * CH, n * BLK + (c + 1) * CH)
                    out = bank[O_BANK[n]][:, c * CH:(c + 1) * CH]
                    mm = group(out, passes(v_hi[:, b, ts], v_lo[:, b, ts], p_hi[:, ts], p_lo[:, ts]), stop=chunk == 0)
                    if chunk:
                        mm = group(out, passes(st_hi[:, chunk, :], st_lo[:, chunk, :], qd_hi[:, b, ts], qd_lo[:, b, ts]),
                                   start=False)
                mm.then_inc(o_done, 1)

            def output(i, tiles, h):
                if tiles[0] == 0:
                    pe.wait_ge(w_done[OW], h)
                for n in tiles:
                    ts = slice(n * P, (n + 1) * P)
                    if n % TPB == 0:
                        pe.wait_ge(g_lo_done, 2 * (i - 2) + n // TPB + 1)
                    if n == 1:
                        pe.wait_ge(g_lo_done, 2 * (i - 2) + 2)
                    pe.wait_ge(y_done, Y0 + NSLOT * (i - 2) + n - 1)
                    group(bank[C_BANK[n % 2]][:], passes(g_hi[:, ts], g_lo[:, ts], w_hi[:, OW, :], w_lo[:, OW, :])).then_inc(c_done, 1)

            def iteration(i, b, h, project, attend, out):
                a, ab = i - 1, 1 - b
                for s in range(NSLOT):
                    if project:
                        projection(i, b, s, h)
                    if attend:
                        if s < 2:
                            keys(a, ab, s)
                        elif s in (2, 4):
                            scores(a, ab, s // 2 - 1)
                        elif s in (3, 5):
                            update(a, ab, (s - 3) // 2)
                        else:
                            attention(a, ab, s - 6)
                    if out and 1 <= s <= 4:
                        output(i, (2 * s - 2, 2 * s - 1), h)

            pe.wait_ge(ident_done, 2)
            iteration(0, 0, 0, True, False, False)
            iteration(1, 1, 0, True, True, False)
            with pe.Fori(1, HEADS) as h:
                iteration(2 * h, 0, h, True, True, True)
                iteration(2 * h + 1, 1, h, True, True, True)
            iteration(NIT, 0, HEADS, False, True, True)
            iteration(NIT + 1, 1, HEADS, False, False, True)
            pe.wait_ge(ss_done, 2 * NIT)
            pe.wait_ge(ones_done, 1)
            for i in range(NT):
                mm = nc.tensor.matmul(bank[SS_BANK][:, i:i + 1], ssum[:, i * P:(i + 1) * P], ones[:], start=True, stop=True)
            mm.then_inc(ss_mm, 1)


def decay_tables():
    base = np.float32(1.0 / 2.0 ** (8.0 / HEADS))
    factor = np.float32(1.0 - LAYER_IDX / (N_LAYERS - 1 + 1e-05) + 1e-05)
    slope = (base ** (np.arange(HEADS, dtype=np.float32) + 1) * factor).astype(np.float64)
    n = np.arange(CH, dtype=np.float64)
    dist = n[None, :] - n[:, None]
    mask = np.where(dist >= 0, np.exp(-slope[:, None, None] * np.maximum(dist, 0)), 0.0)
    key = np.exp(-slope[:, None] * (CH - 1 - n))[:, :, None]
    block = np.broadcast_to(np.exp(-slope * CH)[:, None, None], (HEADS, P, 1))
    tables = np.concatenate([mask, key, block], axis=2).astype(np.float32)
    query = np.exp(-slope[:, None] * (n + 1)).astype(np.float32)
    return tables, query


def kernel(**inp):
    import concourse.bacc as bacc
    from concourse.bass_utils import run_bass_kernel_spmd

    a = {k: np.asarray(v) for k, v in inp.items()}

    def pad(m, rows=None, cols=None):
        out = np.zeros((rows or m.shape[0], cols or m.shape[1]), m.dtype)
        out[:m.shape[0], :m.shape[1]] = m
        return out

    def tiles(m):
        return m.reshape(-1, P, m.shape[-1]).transpose(1, 0, 2)

    qkv = a["L1_attn_qkv_w"].reshape(HEADS, 3, HD, KT, P).transpose(0, 4, 1, 3, 2)
    gate = a["L1_attn_gate_w"].reshape(HEADS, 1, HD, KT, P).transpose(0, 4, 1, 3, 2)
    proj = np.concatenate([qkv, gate], axis=2)
    out_w = a["L1_attn_out_w"].T.reshape(HEADS, HD, D)
    out_w = np.concatenate([out_w, a["L1_attn_norm_w"].reshape(HEADS, HD, 1)], axis=2)
    tables, query = decay_tables()
    arrays = dict(
        x=a["L0_attn_x"].reshape(TOK, D),
        wq0=a["L0_attn_Wq"].reshape(D, -1), wk0=a["L0_attn_Wk"].reshape(D, -1), wv0=a["L0_attn_Wv"].reshape(D, -1),
        bq0=a["L0_attn_bq"].reshape(-1), bk0=a["L0_attn_bk"].reshape(-1), bv0=a["L0_attn_bv"].reshape(-1),
        gate_q=pad(a["L0_ffn_gate_q"].T, cols=INT0P), up_q=pad(a["L0_ffn_up_q"].T, cols=INT0P),
        down_q=pad(a["L0_ffn_down_q"].T, rows=INT0P),
        gate_s=pad(a["L0_ffn_gate_scale"][:, None], rows=INT0P).reshape(OT0, P).T,
        up_s=pad(a["L0_ffn_up_scale"][:, None], rows=INT0P).reshape(OT0, P).T,
        down_s=a["L0_ffn_down_scale"],
        gate_A=a["L0_ffn_gate_A"], up_A=a["L0_ffn_up_A"], down_A=pad(a["L0_ffn_down_A"], rows=INT0P),
        gate_B=pad(a["L0_ffn_gate_B"], cols=INT0P), up_B=pad(a["L0_ffn_up_B"], cols=INT0P), down_B=a["L0_ffn_down_B"],
        w1=np.concatenate([tiles(a["L1_ffn_" + n]).reshape(P, -1)
                           for n in ("up_w", "down_w", "fc1_w", "expert_w", "fc2_w")], axis=1),
        route_w=tiles(a["L1_ffn_gate_w"]),
        gamma=a["L1_ffn_ln_gamma"], beta=a["L1_ffn_ln_beta"],
        proj_w=proj, out_w=out_w, decay=tables, q_decay=query,
    )
    nc = bacc.Bacc("TRN2", target_bir_lowering=False, num_devices=1)
    t, feed = {}, {}
    for name, v in arrays.items():
        v = np.ascontiguousarray(v)
        feed[f"{name}_dram"] = v
        t[name] = nc.dram_tensor(f"{name}_dram", v.shape, mybir.dt.from_np(v.dtype), kind="ExternalInput").ap()
    t["out"] = nc.dram_tensor("out_dram", (TOK, D), F32, kind="ExternalOutput").ap()
    build(nc, t)
    r = run_bass_kernel_spmd(nc, [feed], core_ids=[0])
    return r.results[0]["out_dram"].reshape(BATCH, SEQ, D)
```

```python
from contextlib import ExitStack

import numpy as np
import concourse.bass as bass
from concourse import mybir

ALU = mybir.AluOpType
ACT = mybir.ActivationFunctionType
F32, F16, BF16, I32 = mybir.dt.float32, mybir.dt.float16, mybir.dt.bfloat16, mybir.dt.int32
AX_X = mybir.AxisListType.X

P = 128
D = 512
KT = D // P
BATCH, SEQ = 2, 1024
TOK = BATCH * SEQ
NT = TOK // P
BLK = 512
NBLK = TOK // BLK
TPB = BLK // P
EPS = 1e-5

QD, NH0 = 16, 32
INT0, RANK = 1376, 32
OT0 = -(-INT0 // P)
INT0P = OT0 * P
Q_ZERO, Q_STEP, LR_SCALE = 7.5, 0.005, 0.02
LRA, LRB = 16.0, 64.0

HEADS, HD, CH = 32, 128, 128
HPB = SEQ // BLK
CPH = BLK // CH
LAYER_IDX, N_LAYERS = 1, 32
INT1, LAT, NE = 1024, 256, 8
OT1, LT1 = INT1 // P, LAT // P
SQ_DOWN = 1.0 / 8.0
W1_UP, W1_DOWN = 0, KT * INT1
W1_FC1 = W1_DOWN + OT1 * D
W1_EXP = W1_FC1 + KT * LAT
W1_FC2 = W1_EXP + LT1 * LAT
W1_COLS = W1_FC2 + LT1 * D
W1_PER_BLK = 8
W1_CHUNK = W1_COLS // ((NBLK - 1) * W1_PER_BLK)
assert W1_CHUNK * (NBLK - 1) * W1_PER_BLK == W1_COLS and W1_PER_BLK % 2 == 0
R3 = 3 * RANK


def passes(w_hi, w_lo, a_hi, a_lo):
    return ((w_hi, a_hi), (w_hi, a_lo), (w_lo, a_hi))


def ds(at, n):
    return slice(at, at + n) if isinstance(at, int) else bass.ds(at, n)


def wait(eng, s, count):
    if not isinstance(count, int) or count > 0:
        eng.wait_ge(s, count)


def hold(eng, s, count, turns):
    if not isinstance(count, int):
        eng.wait_ge(s, count)
        eng.sem_inc(turns, 1)
    elif count > 0:
        eng.wait_ge(s, count)


def build(nc, t):
    with ExitStack() as ctx:
        def sb(stack, name, shape, dt=F32):
            return stack.enter_context(nc.sbuf_tensor(name, shape, dt))

        def sem(name):
            return ctx.enter_context(nc.semaphore(name))

        x_sb = sb(ctx, "x_sb", [P, NT, D])
        xnT_hi = sb(ctx, "xnT_hi", [P, KT, TOK], F16)
        xnT_lo = sb(ctx, "xnT_lo", [P, KT, TOK], BF16)
        ident = sb(ctx, "ident", [P, P])
        bank = [ctx.enter_context(nc.psum_tensor(f"bank{i}", [P, 512], F32)) for i in range(8)]

        w1_stack = ctx.enter_context(ExitStack())
        region = sb(w1_stack, "region", [P, W1_COLS])
        w1 = dict(hi=region[:, 0:W1_COLS // 2].bitcast(F16), lo=region[:, W1_COLS // 2:].bitcast(BF16))
        with ExitStack() as s:
            phase_layer0(nc, t, sem, lambda *a: sb(s, *a), bank, x_sb, xnT_hi, xnT_lo, ident, region, w1)
        if DEBUG == 1:
            return dump(nc, t, sem, x_sb)
        with ExitStack() as s:
            phase_norm1_ffn1(nc, t, sem, lambda *a: sb(s, *a), bank, x_sb, xnT_hi, xnT_lo, ident, w1)
        if DEBUG == 2:
            return dump(nc, t, sem, x_sb)
        w1_stack.close()
        with ExitStack() as s:
            phase_attn1(nc, t, lambda n: sem("attn1_" + n), lambda *a: sb(s, *a), bank, x_sb, xnT_hi, xnT_lo, ident)


DEBUG = 3


def dump(nc, t, sem, x_sb):
    out_written = sem("out_written")
    with nc.Block() as block:
        @block.sync
        def _(sp):
            sp.dma_start(t["out"].rearrange("(t p) d -> p t d", p=P), x_sb[:]).then_inc(out_written, 16)
            sp.wait_ge(out_written, 16)


def norm_small(nc, eng, steps, small, mv, n, sd_ready, sd_want, var_ready):
    done, c = steps
    veps, sd, r0, a, b, r, nmr = (small[:, i, 0:n] for i in range(7))
    mean, var = mv[:, 0:n, 0], mv[:, 0:n, 1]
    eng.wait_ge(done, c)
    nc.vector.tensor_scalar(veps, var, EPS, None, ALU.add).then_inc(var_ready, 1)
    eng.wait_ge(sd_ready, sd_want)
    nc.vector.reciprocal(r0, sd).then_inc(done, 1)
    eng.wait_ge(done, c + 1)
    nc.vector.tensor_tensor(a, r0, r0, ALU.mult).then_inc(done, 1)
    eng.wait_ge(done, c + 2)
    nc.vector.tensor_tensor(b, a, veps, ALU.mult).then_inc(done, 1)
    eng.wait_ge(done, c + 3)
    nc.vector.tensor_scalar(a, b, -0.5, 1.5, ALU.mult, ALU.add).then_inc(done, 1)
    eng.wait_ge(done, c + 4)
    nc.vector.tensor_tensor(r, r0, a, ALU.mult).then_inc(done, 1)
    eng.wait_ge(done, c + 5)
    nc.vector.scalar_tensor_tensor(nmr, r, -1.0, mean, ALU.mult, ALU.mult).then_inc(done, 1)
    return c + 6


class Norm:
    STEPS = 2 * TPB + 6

    def __init__(self, nc, sem, tag, stats, mv, small, xn, banks, bank, x_sb, xnT_hi, xnT_lo, ident):
        self.nc, self.stats, self.mv, self.small, self.xn = nc, stats, mv, small, xn
        self.bank = [bank[b] for b in banks]
        self.x, self.hi, self.lo, self.ident = x_sb, xnT_hi, xnT_lo, ident
        self.step, self.var_ready, self.sd_ready = sem("step" + tag), sem("var_ready" + tag), sem("sd_ready" + tag)
        self.xn_done, self.xT_done, self.hi_done, self.lo_done = (sem("xn_done" + tag), sem("xT_done" + tag),
                                                                  sem("hi_done" + tag), sem("lo_done" + tag))

    def dve_stats(self, dve, g):
        c, first = g * self.STEPS, g * TPB
        for i in range(first, first + TPB):
            self.nc.vector.bn_stats(self.stats[:, i, :], self.x[:, i, :]).then_inc(self.step, 1)
        dve.wait_ge(self.step, c + TPB)
        for i in range(first, first + TPB):
            self.nc.vector.bn_aggr(self.mv[:, i, :], self.stats[:, i, :]).then_inc(self.step, 1)
        norm_small(self.nc, dve, (self.step, c + 2 * TPB), self.small[:, :, first:first + TPB],
                   self.mv[:, first:first + TPB, :], TPB, self.sd_ready, g + 1, self.var_ready)

    def act_sqrt(self, act, g):
        veps, sd = (self.small[:, i, g * TPB:(g + 1) * TPB] for i in (0, 1))
        act.wait_ge(self.var_ready, g + 1)
        self.nc.scalar.activation(sd, veps, ACT.Sqrt).then_inc(self.sd_ready, 1)

    def act_rows(self, act, i):
        if i % TPB == 0:
            act.wait_ge(self.step, (i // TPB + 1) * self.STEPS)
        if i >= 2:
            act.wait_ge(self.xT_done, i - 1)
        self.nc.scalar.activation(self.xn[:, i % 2, :], self.x[:, i, :], ACT.Identity, scale=self.small[:, 5, i:i + 1],
                                  bias=self.small[:, 6, i:i + 1]).then_inc(self.xn_done, 1)

    def pe_turn(self, pe, i):
        pe.wait_ge(self.xn_done, i + 1)
        if i >= 2:
            pe.wait_ge(self.lo_done, i - 1)
        for k in range(KT):
            mm = self.nc.tensor.transpose(self.bank[i % 2][:, k * P:(k + 1) * P], self.xn[:, i % 2, k * P:(k + 1) * P],
                                          self.ident[:])
        mm.then_inc(self.xT_done, 1)

    def act_hi(self, act, i):
        act.wait_ge(self.xT_done, i + 1)
        self.nc.scalar.activation(self.hi[:, :, i * P:(i + 1) * P], self.bank[i % 2][:].rearrange("p (k t) -> p k t", k=KT),
                                  ACT.Copy).then_inc(self.hi_done, 1)

    def dve_lo(self, dve, i):
        dve.wait_ge(self.hi_done, i + 1)
        tok = slice(i * P, (i + 1) * P)
        self.nc.vector.tensor_tensor(self.lo[:, :, tok], self.bank[i % 2][:].rearrange("p (k t) -> p k t", k=KT),
                                     self.hi[:, :, tok], ALU.subtract).then_inc(self.lo_done, 1)


def phase_layer0(nc, t, sem, sb, bank, x_sb, xnT_hi, xnT_lo, ident, region, w1):
    w0 = dict(
        gate=sb("w0_gate", [P, KT, INT0P], F16), up=sb("w0_up", [P, KT, INT0P], F16), down=sb("w0_down", [P, OT0, D], F16),
        A_hi=sb("w0_A_hi", [P, 2 * KT + OT0, R3], F16), A_lo=sb("w0_A_lo", [P, 2 * KT + OT0, R3], BF16),
        B=sb("w0_B", [R3, 2 * INT0P + D], F16), scale=sb("w0_scale", [P, 2, OT0]), down_scale=sb("w0_down_scale", [P, D]),
    )
    qkv, kext, smax = sb("qkv0", [P, NT, 3 * QD]), sb("kext", [P, 2, NT]), sb("smax", [P, NT, QD])
    prob = sb("prob0", [P, TPB, QD, QD])
    den, att = sb("den0", [P, 2, TPB, QD]), sb("att0", [P, TPB, QD])
    full = [P, TPB, QD, QD]

    taken = [0]

    def short(cols):
        taken[0] += cols
        assert taken[0] <= W1_COLS
        return region[:, taken[0] - cols:taken[0]]

    NSTAGE = 4
    stage_f = short(NSTAGE * INT0P).rearrange("p (s o) -> p s o", s=NSTAGE)
    norm = Norm(nc, sem, "0", short(NT * 6).rearrange("p (t s) -> p t s", s=6), short(NT * 2).rearrange("p (t s) -> p t s", s=2),
                short(7 * NT).rearrange("p (k t) -> p k t", k=7), short(2 * D).rearrange("p (b d) -> p b d", b=2),
                (6, 7), bank, x_sb, xnT_hi, xnT_lo, ident)
    wq = short(KT * QD * NH0).rearrange("p (k n) -> p k n", k=KT)
    bq = short(QD * NH0)
    w48 = short(KT * 3 * QD).rearrange("p (k n) -> p k n", k=KT)
    w48_hi = short(KT * 3 * QD // 2).bitcast(F16).rearrange("p (k n) -> p k n", k=KT)
    w48_lo = short(KT * 3 * QD // 2).bitcast(BF16).rearrange("p (k n) -> p k n", k=KT)
    b48 = short(3 * QD)
    sext = short(2 * NT * QD).rearrange("p (a t d) -> p a t d", a=2, t=NT)

    x_in = [sem(f"x_in{i}") for i in range(NBLK)]
    stage_in = [sem(f"stage_in{i}") for i in range(NSTAGE)]
    w_in, scale_in, scale_done = sem("w0_in"), sem("scale_in"), sem("scale_done")
    chunk_done, split_step, id_zero, id_done = sem("chunk_done"), sem("split_step"), sem("id_zero"), sem("id_done")
    B_in, B_hi_done, B_done = sem("B_in"), sem("B_hi_done"), sem("B_done")
    w48_step, w48_done = sem("w48_step"), sem("w48_done")
    qkv_done, qkv_out, att_step = sem("qkv0_done"), sem("qkv0_out"), sem("att_step")
    qk_done, score_done, exp_done = sem("qk0_done"), sem("score0_done"), sem("exp0_done")
    den_done, pv_done, num_done, rden_done, att_done, att_added = (
        sem("den0_done"), sem("pv0_done"), sem("num0_done"), sem("rden0_done"), sem("att0_done"), sem("att0_added"))

    x_dram = t["x"].rearrange("(t p) d -> p t d", p=P)

    chunks = []

    def staged(i, cols, rows=P, ints=False):
        view = stage_f[0:rows, i % NSTAGE, 0:cols]
        return view.bitcast(I32) if ints else view

    def add_A(name, at, n):
        view = staged(len(chunks), n * R3).rearrange("p (k r) -> p k r", r=R3)
        src = t[name + "_A"].rearrange("(k p) r -> p k r", p=P)
        chunks.append(("A", [(view[:, :, c * RANK:(c + 1) * RANK], src) for c in range(3)], slice(at, at + n)))
        return len(chunks)

    def add_B(name, at, cols):
        view = staged(len(chunks), cols, R3)
        chunks.append(("B", [(view[c * RANK:(c + 1) * RANK, :], t[name + "_B"]) for c in range(3)], slice(at, at + cols)))
        return len(chunks)

    def add_int(name):
        for k in range(KT):
            src = t[name + "_q"].rearrange("(k p) o -> k p o", p=P)[k]
            chunks.append(("int", [(staged(len(chunks), INT0P, ints=True), src)], w0[name][:, k, :]))
        return len(chunks)

    add_A("gate", 0, KT)
    A_READY = add_A("up", KT, KT)
    GATE_READY = add_int("gate")
    UP_READY = add_int("up")
    add_A("down", 2 * KT, OT0)
    down_flat = w0["down"][:].rearrange("p o d -> p (o d)")
    down_dram = t["down_q"].rearrange("(o p) d -> p o d", p=P)
    for a in range(0, OT0, 2):
        b = min(a + 2, OT0)
        view = staged(len(chunks), (b - a) * D, ints=True)
        chunks.append(("int", [(view.rearrange("p (o d) -> p o d", d=D), down_dram[:, a:b, :])], down_flat[:, a * D:b * D]))
    DOWN_READY = add_B("down", 2 * INT0P, D)
    h_hi, h_lo = sb("h0_hi", [P, OT0, BLK], F16), sb("h0_lo", [P, OT0, BLK], BF16)
    B_stage = h_hi[0:R3].rearrange("p o t -> p (o t)").bitcast(F32)
    assert OT0 * BLK // 2 == 2 * INT0P
    g, u, s = sb("g0", [P, 2, BLK]), sb("u0", [P, 2, BLK]), sb("s0", [P, 2, BLK])
    stack = [sb(f"xa_{n}", [R3, BLK], F16) for n in ("gate", "up", "down")]
    scaled = s
    w1_stage = sb("w1_stage", [P, 2, W1_CHUNK])

    xa_done, stack_hi, stack_done = sem("xa_done"), sem("stack_hi"), sem("stack_done")
    gm_done, um_done, gl_done, ul_done = sem("gate_main"), sem("up_main"), sem("gate_low"), sem("up_low")
    gs_done, us_done = sem("gate_scaled"), sem("up_scaled")
    g_done, u_done, s_done = sem("gate_summed"), sem("up_summed"), sem("silu_done")
    h_done, h_hi_done, h_lo_done = sem("h0_done"), sem("h0_hi_done"), sem("h0_lo_done")
    dm_done, dl_done, scaled_done, xl_done, x_done = (sem("down_main"), sem("down_low"), sem("down_scaled"),
                                                      sem("x_low_added"), sem("x_done"))
    w1_in = [sem(f"w1_in{i}") for i in range(2)]
    w1_hi_done, w1_lo_done = sem("w1_hi_done"), sem("w1_lo_done")
    pool_turns, sp_turns = sem("pool_turns0"), sem("sp_turns0")
    LR = LR_SCALE * LRA
    UNDO = 1.0 / (LRA * LRB)
    XA_GATE, XA_UP, HA, GL, UL = 6, 7, 7, 4, 5
    OUT_MAIN, OUT_LOW = (6, 0), (7, 1)
    QKV_BANK = (6, 7)
    lo_rows = slice(2 * RANK, R3)

    STATS_AT = {0: 1, 2: 2, 4: 3}
    TILES_AT = {o: (TPB + 2 * (o - 2), TPB + 2 * (o - 2) + 1) for o in range(2, 8)}
    QKV_AT = {8: 0, 9: 1}
    ATT_STEPS = 5

    def upto(j, o):
        return j * OT0 + max(o + 1, 0)

    with nc.Block() as block:
        @block.sync
        def _(sp):
            def load_x(i):
                sp.dma_start(x_sb[:, i * TPB:(i + 1) * TPB, :], x_dram[:, i * TPB:(i + 1) * TPB, :]).then_inc(x_in[i], 16)

            load_x(0)
            sp.dma_start(w0["scale"][:, 0, :], t["gate_s"]).then_inc(scale_in, 16)
            sp.dma_start(w0["scale"][:, 1, :], t["up_s"]).then_inc(scale_in, 16)
            sp.dma_start(w0["down_scale"][:], t["down_s"].partition_broadcast(P)).then_inc(scale_in, 16)
            for i, (_, dmas, _) in enumerate(chunks):
                if i >= NSTAGE:
                    sp.wait_ge(chunk_done, i - NSTAGE + 1)
                for dst, src in dmas:
                    sp.dma_start(dst, src).then_inc(stage_in[i % NSTAGE], 16)
                if i + 1 == GATE_READY:
                    for m, name in enumerate(("gate_B", "up_B")):
                        for c in range(3):
                            sp.dma_start(B_stage[c * RANK:(c + 1) * RANK, m * INT0P:(m + 1) * INT0P], t[name]).then_inc(B_in, 16)
                if i + 1 == UP_READY:
                    for g in range(1, NBLK):
                        load_x(g)
                    sp.dma_start(wq, t["wq0"].rearrange("(k p) n -> p k n", p=P)).then_inc(w_in, 16)
                    sp.dma_start(w48[:, :, QD:2 * QD], t["wk0"].rearrange("(k p) n -> p k n", p=P)).then_inc(w_in, 16)
                    sp.dma_start(w48[:, :, 2 * QD:], t["wv0"].rearrange("(k p) n -> p k n", p=P)).then_inc(w_in, 16)
                    sp.dma_start(bq, t["bq0"].partition_broadcast(P)).then_inc(w_in, 16)
                    sp.dma_start(b48[:, QD:2 * QD], t["bk0"].partition_broadcast(P)).then_inc(w_in, 16)
                    sp.dma_start(b48[:, 2 * QD:], t["bv0"].partition_broadcast(P)).then_inc(w_in, 16)

            def block_of_tokens(j):
                hold(sp, att_added, TPB * j, sp_turns)
                for c in range(W1_PER_BLK):
                    if c >= 2:
                        hold(sp, w1_lo_done, (j - 1) * W1_PER_BLK + c - 1, sp_turns)
                    at = ((j - 1) * W1_PER_BLK + c) * W1_CHUNK
                    sp.dma_start(w1_stage[:, c % 2, :], t["w1"][:, ds(at, W1_CHUNK)]).then_inc(w1_in[c % 2], 16)

            with sp.Fori(1, NBLK) as j:
                block_of_tokens(j)

        @block.gpsimd
        def _(pool):
            nc.gpsimd.memset(ident[:], 0.0).then_inc(id_zero, 1)
            pool.wait_ge(id_zero, 1)
            nc.gpsimd.affine_select(out=ident[:], in_=ident[:], compare_op=ALU.not_equal, fill=1.0, base=0,
                                    pattern=[[-1, P]], channel_multiplier=1).then_inc(id_done, 1)
            pool.wait_ge(scale_in, 48)
            nc.gpsimd.tensor_scalar(w0["scale"][:], w0["scale"][:], Q_STEP, 1.0, ALU.mult, ALU.mult).then_inc(scale_done, 1)
            nc.gpsimd.tensor_scalar(w0["down_scale"][:], w0["down_scale"][:], Q_STEP, 1.0, ALU.mult,
                                    ALU.mult).then_inc(scale_done, 1)
            landed, steps = [0] * NSTAGE, [0]

            def split_chunk(i):
                kind, dmas, dst = chunks[i]
                landed[i % NSTAGE] += 16 * len(dmas)
                pool.wait_ge(stage_in[i % NSTAGE], landed[i % NSTAGE])
                if kind == "int":
                    nc.gpsimd.tensor_scalar(dst, staged(i, dst.shape[-1], ints=True), 1.0, -Q_ZERO,
                                            ALU.mult, ALU.add).then_inc(chunk_done, 1)
                elif kind == "A":
                    n = dst.stop - dst.start
                    view = staged(i, n * R3).rearrange("p (k r) -> p k r", r=R3)
                    nc.gpsimd.tensor_copy(w0["A_hi"][:, dst, :], view).then_inc(split_step, 1)
                    steps[0] += 1
                    pool.wait_ge(split_step, steps[0])
                    nc.gpsimd.tensor_tensor(w0["A_lo"][:, dst, :], view, w0["A_hi"][:, dst, :],
                                            ALU.subtract).then_inc(chunk_done, 1)
                else:
                    view = staged(i, dst.stop - dst.start, R3)
                    mid = slice(RANK, 2 * RANK)
                    pool.wait_ge(chunk_done, i)
                    nc.gpsimd.tensor_scalar(view, view, LRB, 1.0, ALU.mult, ALU.mult).then_inc(split_step, 1)
                    pool.wait_ge(split_step, steps[0] + 1)
                    nc.gpsimd.tensor_copy(w0["B"][:, dst], view).then_inc(split_step, 1)
                    steps[0] += 2
                    pool.wait_ge(split_step, steps[0])
                    nc.gpsimd.tensor_tensor(w0["B"][mid, dst], view[mid, :], w0["B"][mid, dst],
                                            ALU.subtract).then_inc(chunk_done, 1)
                    pool.wait_ge(chunk_done, i + 1)

            def softmax_part(j):
                at = j * TPB
                hold(pool, att_step, ATT_STEPS, pool_turns)
                hold(pool, att_done, j, pool_turns)
                q, k, v = (qkv[:, ds(at, TPB), i * QD:(i + 1) * QD] for i in range(3))
                nc.gpsimd.tensor_tensor(prob[:], q.unsqueeze(3).broadcast_to(full), k.unsqueeze(2).broadcast_to(full),
                                        ALU.mult).then_inc(qk_done, 1)
                hold(pool, qk_done, j + 1, pool_turns)
                nc.gpsimd.tensor_tensor(prob[:], prob[:], smax[:, ds(at, TPB), :].unsqueeze(3).broadcast_to(full),
                                        ALU.subtract).then_inc(score_done, 1)
                hold(pool, den_done, j + 1, pool_turns)
                nc.gpsimd.tensor_tensor(prob[:], prob[:], v.unsqueeze(2).broadcast_to(full), ALU.mult).then_inc(pv_done, 1)
                hold(pool, att_done, j + 1, pool_turns)
                for i in range(TPB):
                    hold(pool, x_done, TPB * j + i + 1, pool_turns)
                    x = x_sb[:, ds(at + i, 1), :].rearrange("p a (d h) -> p (a d) h", h=NH0)
                    nc.gpsimd.tensor_tensor(x, x, att[:, i, :].unsqueeze(2).broadcast_to([P, QD, NH0]),
                                            ALU.add).then_inc(att_added, 1)

            def block_of_tokens(j):
                for o in range(OT0):
                    hold(pool, h_done, upto(j, o), pool_turns)
                    hold(pool, dm_done, TPB * j, pool_turns)
                    nc.gpsimd.tensor_scalar(h_hi[:, o, :], s[:, o % 2, :], 1.0, 0.0, ALU.mult, ALU.add).then_inc(h_hi_done, 1)
                    if isinstance(j, int):
                        if UP_READY + o < len(chunks):
                            split_chunk(UP_READY + o)
                    elif o < W1_PER_BLK:
                        n = (j - 1) * W1_PER_BLK + o
                        cols = ds(n * W1_CHUNK, W1_CHUNK)
                        hold(pool, w1_in[o % 2], 16 * ((j - 1) * (W1_PER_BLK // 2) + o // 2 + 1), pool_turns)
                        nc.gpsimd.tensor_copy(w1["hi"][:, cols], w1_stage[:, o % 2, :]).then_inc(w1_hi_done, 1)
                        hold(pool, w1_hi_done, n + 1, pool_turns)
                        nc.gpsimd.tensor_tensor(w1["lo"][:, cols], w1_stage[:, o % 2, :], w1["hi"][:, cols],
                                                ALU.subtract).then_inc(w1_lo_done, 1)
                softmax_part(j)

            for i in range(UP_READY):
                split_chunk(i)
            block_of_tokens(0)
            with pool.Fori(1, NBLK) as j:
                block_of_tokens(j)

        @block.scalar
        def _(act):
            def stack_part(j, i, b):
                wait(act, xa_done, 3 * j + i + 1)
                wait(act, (gl_done, ul_done, dl_done)[i], (OT0, OT0, TPB)[i] * j)
                nc.scalar.activation(stack[i][:], bank[b][0:R3, :], ACT.Copy, scale=LR).then_inc(stack_hi, 1)

            norm.act_sqrt(act, 0)
            norm.act_rows(act, 0)
            for i in range(TPB):
                if i + 1 < TPB:
                    norm.act_rows(act, i + 1)
                norm.act_hi(act, i)
            act.wait_ge(scale_done, 2)

            def block_of_tokens(j):
                first = isinstance(j, int)
                stack_part(j, 0, XA_GATE)
                stack_part(j, 1, XA_UP)
                for o in range(OT0 + 1):
                    tiles = TILES_AT.get(o, ()) if first else ()
                    for i in tiles:
                        norm.act_rows(act, i)
                    if o < OT0:
                        wait(act, gm_done, upto(j, o))
                        wait(act, s_done, upto(j, o - 2))
                        nc.scalar.activation(g[:, o % 2, :], bank[o % 2][:], ACT.Copy,
                                             scale=w0["scale"][:, 0, o:o + 1]).then_inc(gs_done, 1)
                        wait(act, um_done, upto(j, o))
                        wait(act, h_done, upto(j, o - 2))
                        nc.scalar.activation(u[:, o % 2, :], bank[2 + o % 2][:], ACT.Copy,
                                             scale=w0["scale"][:, 1, o:o + 1]).then_inc(us_done, 1)
                    if first and o in STATS_AT:
                        norm.act_sqrt(act, STATS_AT[o])
                    for i in tiles:
                        norm.act_hi(act, i)
                    if o >= 1:
                        wait(act, g_done, upto(j, o - 1))
                        wait(act, h_lo_done, upto(j, o - 3))
                        nc.scalar.activation(s[:, (o - 1) % 2, :], g[:, (o - 1) % 2, :], ACT.Silu).then_inc(s_done, 1)
                stack_part(j, 2, HA)
                wait(act, score_done, j + 1)
                nc.scalar.activation(prob[:], prob[:], ACT.Exp, scale=QD ** -0.5).then_inc(exp_done, 1)

            block_of_tokens(0)
            with act.Fori(1, NBLK) as j:
                block_of_tokens(j)

        @block.vector
        def _(dve):
            def stack_part(j, i, b):
                wait(dve, stack_hi, 3 * j + i + 1)
                nc.vector.scalar_tensor_tensor(stack[i][lo_rows, :], bank[b][lo_rows, :], LR, stack[i][lo_rows, :],
                                               ALU.mult, ALU.subtract).then_inc(stack_done, 1)

            def project_qkv_weights():
                dve.wait_ge(w_in, 96)
                nc.vector.tensor_reduce(w48[:, :, 0:QD], wq.rearrange("p k (d h) -> p k d h", h=NH0), AX_X,
                                        ALU.add).then_inc(w48_step, 1)
                nc.vector.tensor_reduce(b48[:, 0:QD], bq.rearrange("p (d h) -> p d h", h=NH0), AX_X,
                                        ALU.add).then_inc(w48_step, 1)
                dve.wait_ge(w48_step, 2)
                nc.vector.tensor_copy(w48_hi, w48).then_inc(w48_done, 1)
                dve.wait_ge(w48_done, 1)
                nc.vector.tensor_tensor(w48_lo, w48, w48_hi, ALU.subtract).then_inc(w48_done, 1)

            def qkv_bias(part):
                dve.wait_ge(qkv_done, part + 1)
                n = NT // 2
                nc.vector.tensor_tensor(qkv[:, part * n:(part + 1) * n, :],
                                        bank[QKV_BANK[part]][:, 0:n * 3 * QD].rearrange("p (t c) -> p t c", t=n),
                                        b48.unsqueeze(1).broadcast_to([P, n, 3 * QD]), ALU.add).then_inc(qkv_out, 1)

            def score_maxima():
                q, k = qkv[:, :, 0:QD], qkv[:, :, QD:2 * QD]
                dve.wait_ge(qkv_out, 2)
                nc.vector.tensor_reduce(kext[:, 0, :], k, AX_X, ALU.max).then_inc(att_step, 1)
                nc.vector.tensor_reduce(kext[:, 1, :], k, AX_X, ALU.min).then_inc(att_step, 1)
                dve.wait_ge(att_step, 2)
                for e in range(2):
                    nc.vector.tensor_tensor(sext[:, e], q, kext[:, e, :].unsqueeze(2).broadcast_to([P, NT, QD]),
                                            ALU.mult).then_inc(att_step, 1)
                dve.wait_ge(att_step, 4)
                nc.vector.tensor_tensor(smax[:], sext[:, 0], sext[:, 1], ALU.max).then_inc(att_step, 1)

            dve.wait_ge(x_in[0], 16)
            norm.dve_stats(dve, 0)
            for i in range(TPB):
                norm.dve_lo(dve, i)
            dve.wait_ge(B_in, 16 * 6)
            B, mid = w0["B"][:, 0:2 * INT0P], slice(RANK, 2 * RANK)
            nc.vector.tensor_scalar(B, B_stage, LRB, None, ALU.mult).then_inc(B_hi_done, 1)
            dve.wait_ge(B_hi_done, 1)
            nc.vector.scalar_tensor_tensor(B[mid], B_stage[mid], LRB, B[mid], ALU.mult, ALU.subtract).then_inc(B_done, 1)

            def block_of_tokens(j):
                first = isinstance(j, int)
                stack_part(j, 0, XA_GATE)
                stack_part(j, 1, XA_UP)
                for o in range(OT0 + 2):
                    if first and o in STATS_AT:
                        dve.wait_ge(x_in[STATS_AT[o]], 16)
                        norm.dve_stats(dve, STATS_AT[o])
                    if first:
                        for i in TILES_AT.get(o, ()):
                            norm.dve_lo(dve, i)
                        if o - 1 in QKV_AT:
                            qkv_bias(QKV_AT[o - 1])
                    if o < OT0:
                        wait(dve, gl_done, upto(j, o))
                        wait(dve, gs_done, upto(j, o))
                        nc.vector.scalar_tensor_tensor(g[:, o % 2, :], bank[GL][:], UNDO, g[:, o % 2, :],
                                                       ALU.mult, ALU.add).then_inc(g_done, 1)
                        wait(dve, ul_done, upto(j, o))
                        wait(dve, us_done, upto(j, o))
                        nc.vector.scalar_tensor_tensor(u[:, o % 2, :], bank[UL][:], UNDO, u[:, o % 2, :],
                                                       ALU.mult, ALU.add).then_inc(u_done, 1)
                    if o >= 2:
                        wait(dve, h_hi_done, upto(j, o - 2))
                        nc.vector.tensor_tensor(h_lo[:, o - 2, :], s[:, o % 2, :], h_hi[:, o - 2, :],
                                                ALU.subtract).then_inc(h_lo_done, 1)
                    if 1 <= o <= OT0:
                        wait(dve, s_done, upto(j, o - 1))
                        wait(dve, u_done, upto(j, o - 1))
                        b = (o - 1) % 2
                        nc.vector.tensor_tensor(s[:, b, :], s[:, b, :], u[:, b, :], ALU.mult).then_inc(h_done, 1)
                    if first and o == 6:
                        project_qkv_weights()
                if first:
                    score_maxima()
                stack_part(j, 2, HA)
                for i in range(TPB):
                    if i == 1:
                        wait(dve, exp_done, j + 1)
                        nc.vector.tensor_reduce(den[:, 0], prob[:], AX_X, ALU.add).then_inc(den_done, 1)
                    if i == 3:
                        wait(dve, pv_done, j + 1)
                        wait(dve, att_added, TPB * j)
                        nc.vector.tensor_reduce(att[:], prob[:], AX_X, ALU.add).then_inc(num_done, 1)
                        wait(dve, den_done, j + 1)
                        nc.vector.reciprocal(den[:, 1], den[:, 0]).then_inc(rden_done, 1)
                        wait(dve, num_done, j + 1)
                        wait(dve, rden_done, j + 1)
                        nc.vector.tensor_tensor(att[:], att[:], den[:, 1], ALU.mult).then_inc(att_done, 1)
                    x = x_sb[:, ds(j * TPB + i, 1), :].rearrange("p a d -> p (a d)")
                    n = TPB * j + i + 1
                    wait(dve, dm_done, n)
                    nc.vector.tensor_tensor(scaled[:, i % 2, :], bank[OUT_MAIN[i % 2]][:], w0["down_scale"][:],
                                            ALU.mult).then_inc(scaled_done, 1)
                    wait(dve, dl_done, n)
                    nc.vector.scalar_tensor_tensor(x, bank[OUT_LOW[i % 2]][:], UNDO, x, ALU.mult, ALU.add).then_inc(xl_done, 1)
                    wait(dve, xl_done, n)
                    wait(dve, scaled_done, n)
                    nc.vector.tensor_tensor(x, x, scaled[:, i % 2, :], ALU.add).then_inc(x_done, 1)

            block_of_tokens(0)
            with dve.Fori(1, NBLK) as j:
                block_of_tokens(j)

        @block.tensor
        def _(pe):
            def split_products(out, pairs):
                for n, (w, a) in enumerate(pairs):
                    mm = nc.tensor.matmul(out, w, a, start=(n == 0), stop=(n == len(pairs) - 1))
                return mm

            def project_qkv(part):
                if part == 0:
                    pe.wait_ge(w48_done, 2)
                    pe.wait_ge(norm.lo_done, NT)
                n = NT // 2
                for i in range(part * n, (part + 1) * n):
                    tok = slice(i * P, (i + 1) * P)
                    at = (i - part * n) * 3 * QD
                    mm = split_products(bank[QKV_BANK[part]][:, at:at + 3 * QD], [p for k in range(KT) for p in passes(
                        xnT_hi[:, k, tok], xnT_lo[:, k, tok], w48_hi[:, k, :], w48_lo[:, k, :])])
                mm.then_inc(qkv_done, 1)

            pe.wait_ge(id_done, 1)
            for i in range(TPB):
                norm.pe_turn(pe, i)
            pe.wait_ge(norm.lo_done, TPB)

            def block_of_tokens(j):
                first = isinstance(j, int)
                tok = ds(j * BLK, BLK)
                xh = [xnT_hi[:, k, tok] for k in range(KT)]
                xl = [xnT_lo[:, k, tok] for k in range(KT)]
                Ah, Al = w0["A_hi"], w0["A_lo"]
                if first:
                    pe.wait_ge(chunk_done, A_READY)
                for i, b in ((0, XA_GATE), (1, XA_UP)):
                    wait(pe, xl_done if i else scaled_done, TPB * j)
                    split_products(bank[b][0:R3, :], [p for k in range(KT) for p in passes(
                        Ah[:, i * KT + k, :], Al[:, i * KT + k, :], xh[k], xl[k])]).then_inc(xa_done, 1)
                for o in range(OT0):
                    rows = slice(o * P, (o + 1) * P)
                    if o < 2:
                        wait(pe, x_done, TPB * j)
                    if first and o == 0:
                        pe.wait_ge(chunk_done, GATE_READY)
                    wait(pe, gs_done, upto(j, o - 2))
                    split_products(bank[o % 2][:], [(w0["gate"][:, k, rows], a) for k in range(KT)
                                                    for a in (xh[k], xl[k])]).then_inc(gm_done, 1)
                    tiles = TILES_AT.get(o, ()) if first else ()
                    if tiles:
                        norm.pe_turn(pe, tiles[0])
                    if first and o == 0:
                        pe.wait_ge(chunk_done, UP_READY)
                    wait(pe, us_done, upto(j, o - 2))
                    split_products(bank[2 + o % 2][:], [(w0["up"][:, k, rows], a) for k in range(KT)
                                                        for a in (xh[k], xl[k])]).then_inc(um_done, 1)
                    if tiles:
                        norm.pe_turn(pe, tiles[1])
                    if first and o in QKV_AT:
                        project_qkv(QKV_AT[o])
                    if first and o == 0:
                        pe.wait_ge(B_done, 1)
                    if o == 0:
                        wait(pe, stack_done, 3 * j + 2)
                    wait(pe, g_done, upto(j, o - 1))
                    nc.tensor.matmul(bank[GL][:], w0["B"][:, rows], stack[0][:], start=True, stop=True).then_inc(gl_done, 1)
                    wait(pe, u_done, upto(j, o - 1))
                    nc.tensor.matmul(bank[UL][:], w0["B"][:, INT0P + o * P:INT0P + (o + 1) * P], stack[1][:],
                                     start=True, stop=True).then_inc(ul_done, 1)
                if first:
                    pe.wait_ge(chunk_done, DOWN_READY)
                    pe.wait_ge(qkv_out, 2)
                for o in range(OT0):
                    wait(pe, h_lo_done, upto(j, o))
                    for n, (w, a) in enumerate(passes(Ah[:, 2 * KT + o, :], Al[:, 2 * KT + o, :], h_hi[:, o, :], h_lo[:, o, :])):
                        mm = nc.tensor.matmul(bank[HA][0:R3, :], w, a, start=(o == 0 and n == 0),
                                              stop=(o == OT0 - 1 and n == 2))
                mm.then_inc(xa_done, 1)
                for i in range(TPB):
                    ts = slice(i * P, (i + 1) * P)
                    if i < 2:
                        wait(pe, gs_done, upto(j, OT0 - 1))
                    else:
                        wait(pe, scaled_done, TPB * j + i - 1)
                    split_products(bank[OUT_MAIN[i % 2]][:], [(a[:, o, ts], w0["down"][:, o, :]) for o in range(OT0)
                                                              for a in (h_hi, h_lo)]).then_inc(dm_done, 1)
                    wait(pe, stack_done, 3 * j + 3)
                    if i >= 2:
                        wait(pe, xl_done, TPB * j + i - 1)
                    nc.tensor.matmul(bank[OUT_LOW[i % 2]][:], stack[2][:, ts], w0["B"][:, 2 * INT0P:],
                                     start=True, stop=True).then_inc(dl_done, 1)

            block_of_tokens(0)
            with pe.Fori(1, NBLK) as j:
                block_of_tokens(j)

def phase_norm1_ffn1(nc, t, sem, sb, bank, x_sb, xnT_hi, xnT_lo, ident, w1):
    norm = Norm(nc, sem, "1", sb("stats1", [P, NT, 6]), sb("mv1", [P, NT, 2]), sb("small1", [P, 7, NT]), sb("xn1", [P, 2, D]),
                (7, 2), bank, x_sb, xnT_hi, xnT_lo, ident)
    route_f = sb("route_f", [P, KT, NE])
    route_hi, route_lo = sb("route_hi", [P, KT, NE], F16), sb("route_lo", [P, KT, NE], BF16)
    gamma, beta = sb("gamma", [P, D]), sb("beta", [P, D])
    relu, sq = sb("relu1", [P, 2, BLK]), sb("sq1", [P, 2, BLK])
    h_hi, h_lo = sb("h1_hi", [P, OT1, BLK], F16), sb("h1_lo", [P, OT1, BLK], BF16)
    lat_hi, lat_lo = sb("lat_hi", [P, LT1, BLK], F16), sb("lat_lo", [P, LT1, BLK], BF16)
    exp_hi, exp_lo = sb("exp_hi", [P, LT1, BLK], F16), sb("exp_lo", [P, LT1, BLK], BF16)
    top, rw = sb("top8", [P, TPB, 8]), sb("rw", [P, TPB])
    routed, y = sb("routed", [P, 2, D]), sb("y1", [P, TPB, D])
    stats, mv, small = sb("stats_y", [P, TPB, 6]), sb("mv_y", [P, TPB, 2]), sb("small_y", [P, 7, TPB])

    in1, route_split = sem("ffn1_in"), sem("route_split")
    beta_done = sem("beta_added")
    lat_mm, lat_hi_done, lat_lo_done = sem("lat_mm"), sem("lat_hi_done"), sem("lat_lo_done")
    exp_mm, exp_hi_done, exp_lo_done = sem("exp_mm"), sem("exp_hi_done"), sem("exp_lo_done")
    route_mm, top_done, rw_done = sem("route_mm"), sem("top_done"), sem("rw_done")
    up_mm, relu_done, sq_done, h_hi_done, h_lo_done = (sem("up1_mm"), sem("relu_done"), sem("sq_done"),
                                                       sem("h1_hi_done"), sem("h1_lo_done"))
    fc2_mm, down_mm, routed_done, y_done = sem("fc2_mm"), sem("down1_mm"), sem("routed_done"), sem("y_done")
    ystep, yvar, ysd, yn_done, yg_done, x1_done = (sem("y_norm_step"), sem("y_var"), sem("y_sd"), sem("yn_done"),
                                                   sem("y_gamma"), sem("x1_done"))
    pool_turns, dve_turns = sem("pool_turns1"), sem("dve_turns1")
    LAT_BANK, EXP_BANK, FC2_BANK, DOWN_BANK, ROUTE_BANK = (3, 4), (5, 6), (3, 4), (5, 6), 2
    TILES_AT = {o: (TPB + 2 * (o - 1), TPB + 2 * (o - 1) + 1) for o in range(1, 7)}
    STATS_AT = {1: 2, 3: 3}
    YSTEPS = 2 * TPB + 6

    def w1_tile(offset, k, width, at, n=P):
        a = offset + k * width + at
        return w1["hi"][:, a:a + n], w1["lo"][:, a:a + n]

    with nc.Block() as block:
        @block.sync
        def _(sp):
            sp.dma_start(route_f[:], t["route_w"]).then_inc(in1, 16)
            sp.dma_start(gamma[:], t["gamma"].partition_broadcast(P)).then_inc(in1, 16)
            sp.dma_start(beta[:], t["beta"].partition_broadcast(P)).then_inc(in1, 16)

        @block.gpsimd
        def _(pool):
            hold(pool, in1, 48, pool_turns)
            nc.gpsimd.tensor_copy(route_hi[:], route_f[:]).then_inc(route_split, 1)
            hold(pool, route_split, 1, pool_turns)
            nc.gpsimd.tensor_tensor(route_lo[:], route_f[:], route_hi[:], ALU.subtract).then_inc(route_split, 1)

            def block_of_tokens(j):
                for o in range(OT1):
                    hold(pool, sq_done, OT1 * j + o + 1, pool_turns)
                    hold(pool, down_mm, TPB * j, pool_turns)
                    nc.gpsimd.tensor_scalar(h_hi[:, o, :], sq[:, o % 2, :], 1.0, 0.0, ALU.mult, ALU.add).then_inc(h_hi_done, 1)
                if isinstance(j, int):
                    pool.wait_ge(norm.xn_done, NT)
                for i in range(TPB):
                    x = x_sb[:, ds(j * TPB + i, 1), :].rearrange("p a d -> p (a d)")
                    nc.gpsimd.tensor_tensor(x, x, beta[:], ALU.add).then_inc(beta_done, 1)

            block_of_tokens(0)
            with pool.Fori(1, NBLK) as j:
                block_of_tokens(j)

        @block.scalar
        def _(act):
            norm.act_sqrt(act, 0)
            norm.act_rows(act, 0)
            for i in range(TPB):
                if i + 1 < TPB:
                    norm.act_rows(act, i + 1)
                norm.act_hi(act, i)
            norm.act_sqrt(act, 1)

            def up_part(j, os):
                for o in os:
                    tiles = TILES_AT.get(o, ()) if isinstance(j, int) else ()
                    for i in tiles:
                        norm.act_rows(act, i)
                    if isinstance(j, int) and o in STATS_AT:
                        norm.act_sqrt(act, STATS_AT[o])
                    for i in tiles:
                        norm.act_hi(act, i)
                    wait(act, relu_done, OT1 * j + o + 1)
                    wait(act, h_lo_done, OT1 * j + max(o - 1, 0))
                    nc.scalar.activation(sq[:, o % 2, :], relu[:, o % 2, :], ACT.Square).then_inc(sq_done, 1)

            def hi_part(j, dst, mm, banks, done, readers, per):
                for l in range(LT1):
                    wait(act, mm, LT1 * j + l + 1)
                    wait(act, readers, per * j)
                    nc.scalar.activation(dst[:, l, :], bank[banks[l]][:], ACT.Copy).then_inc(done, 1)

            def block_of_tokens(j):
                hi_part(j, lat_hi, lat_mm, LAT_BANK, lat_hi_done, exp_mm, LT1)
                up_part(j, range(OT1 // 2))
                hi_part(j, exp_hi, exp_mm, EXP_BANK, exp_hi_done, fc2_mm, TPB)
                up_part(j, range(OT1 // 2, OT1))
                for i in range(TPB):
                    n = TPB * j + i + 1
                    wait(act, fc2_mm, n)
                    wait(act, rw_done, j + 1)
                    wait(act, y_done, TPB * j + max(i - 1, 0))
                    nc.scalar.activation(routed[:, i % 2, :], bank[FC2_BANK[i % 2]][:], ACT.Copy,
                                         scale=rw[:, i:i + 1]).then_inc(routed_done, 1)
                wait(act, yvar, j + 1)
                nc.scalar.activation(small[:, 1, :], small[:, 0, :], ACT.Sqrt).then_inc(ysd, 1)
                wait(act, ystep, YSTEPS * (j + 1))
                for i in range(TPB):
                    nc.scalar.activation(y[:, i, :], y[:, i, :], ACT.Identity, scale=small[:, 5, i:i + 1],
                                         bias=small[:, 6, i:i + 1]).then_inc(yn_done, 1)

            block_of_tokens(0)
            with act.Fori(1, NBLK) as j:
                block_of_tokens(j)

        @block.vector
        def _(dve):
            norm.dve_stats(dve, 0)
            for i in range(TPB):
                norm.dve_lo(dve, i)
            norm.dve_stats(dve, 1)

            def lo_part(j, hi, lo, banks, hi_done, done):
                for l in range(LT1):
                    wait(dve, hi_done, LT1 * j + l + 1)
                    nc.vector.tensor_tensor(lo[:, l, :], bank[banks[l]][:], hi[:, l, :], ALU.subtract).then_inc(done, 1)

            def up_part(j, os):
                for o in os:
                    if isinstance(j, int):
                        if o in STATS_AT:
                            norm.dve_stats(dve, STATS_AT[o])
                        for i in TILES_AT.get(o, ()):
                            norm.dve_lo(dve, i)
                    if o < OT1:
                        wait(dve, up_mm, OT1 * j + o + 1)
                        wait(dve, sq_done, OT1 * j + max(o - 1, 0))
                        nc.vector.tensor_scalar(relu[:, o % 2, :], bank[o % 2][:], 0.0, SQ_DOWN, ALU.max,
                                                ALU.mult).then_inc(relu_done, 1)
                    if o >= 1:
                        wait(dve, h_hi_done, OT1 * j + o)
                        nc.vector.tensor_tensor(h_lo[:, o - 1, :], sq[:, (o - 1) % 2, :], h_hi[:, o - 1, :],
                                                ALU.subtract).then_inc(h_lo_done, 1)

            def block_of_tokens(j):
                lo_part(j, lat_hi, lat_lo, LAT_BANK, lat_hi_done, lat_lo_done)
                hold(dve, route_mm, j + 1, dve_turns)
                hold(dve, routed_done, TPB * j, dve_turns)
                for i in range(TPB):
                    nc.vector.max(top[:, i, :], bank[ROUTE_BANK][:, i * NE:(i + 1) * NE]).then_inc(top_done, 1)
                wait(dve, top_done, TPB * (j + 1))
                nc.vector.tensor_tensor(rw[:], top[:, :, 0], top[:, :, 1], ALU.add).then_inc(rw_done, 1)
                up_part(j, range(OT1 // 2))
                lo_part(j, exp_hi, exp_lo, EXP_BANK, exp_hi_done, exp_lo_done)
                up_part(j, range(OT1 // 2, OT1 + 1))
                c = YSTEPS * j
                for i in range(TPB):
                    n = TPB * j + i + 1
                    wait(dve, down_mm, n)
                    wait(dve, routed_done, n)
                    wait(dve, x1_done, TPB * j)
                    nc.vector.scalar_tensor_tensor(y[:, i, :], bank[DOWN_BANK[i % 2]][:], 1.0 / SQ_DOWN ** 2,
                                                   routed[:, i % 2, :], ALU.mult, ALU.add).then_inc(y_done, 1)
                    wait(dve, y_done, n)
                    nc.vector.bn_stats(stats[:, i, :], y[:, i, :]).then_inc(ystep, 1)
                hold(dve, ystep, c + TPB, dve_turns)
                for i in range(TPB):
                    nc.vector.bn_aggr(mv[:, i, :], stats[:, i, :]).then_inc(ystep, 1)
                norm_small(nc, dve, (ystep, c + 2 * TPB), small, mv, TPB, ysd, j + 1, yvar)
                for i in range(TPB):
                    n = TPB * j + i + 1
                    x = x_sb[:, ds(j * TPB + i, 1), :].rearrange("p a d -> p (a d)")
                    wait(dve, yn_done, n)
                    nc.vector.tensor_tensor(y[:, i, :], y[:, i, :], gamma[:], ALU.mult).then_inc(yg_done, 1)
                    wait(dve, yg_done, n)
                    wait(dve, beta_done, n)
                    nc.vector.tensor_tensor(x, x, y[:, i, :], ALU.add).then_inc(x1_done, 1)

            block_of_tokens(0)
            with dve.Fori(1, NBLK) as j:
                block_of_tokens(j)

        @block.tensor
        def _(pe):
            for i in range(TPB):
                norm.pe_turn(pe, i)
            pe.wait_ge(norm.lo_done, TPB)
            pe.wait_ge(route_split, 2)

            def products(out, pairs):
                for n, (w, a) in enumerate(pairs):
                    mm = nc.tensor.matmul(out, w, a, start=(n == 0), stop=(n == len(pairs) - 1))
                return mm

            def block_of_tokens(j):
                tok = ds(j * BLK, BLK)
                xh = [xnT_hi[:, k, tok] for k in range(KT)]
                xl = [xnT_lo[:, k, tok] for k in range(KT)]

                def up_part(os):
                    for o in os:
                        tiles = TILES_AT.get(o, ()) if isinstance(j, int) else ()
                        if tiles and tiles[0] == TPB:
                            pe.wait_ge(rw_done, 1)
                        for i in tiles:
                            norm.pe_turn(pe, i)
                        wait(pe, relu_done, OT1 * j + max(o - 1, 0))
                        products(bank[o % 2][:], [p for k in range(KT) for p in passes(
                            *w1_tile(W1_UP, k, INT1, o * P), xh[k], xl[k])]).then_inc(up_mm, 1)

                for l in range(LT1):
                    wait(pe, routed_done, TPB * j)
                    products(bank[LAT_BANK[l]][:], [p for k in range(KT) for p in passes(
                        *w1_tile(W1_FC1, k, LAT, l * P), xh[k], xl[k])]).then_inc(lat_mm, 1)
                wait(pe, rw_done, j)
                for i in range(TPB):
                    ts = ds(j * BLK + i * P, P)
                    mm = products(bank[ROUTE_BANK][:, i * NE:(i + 1) * NE], [p for k in range(KT) for p in passes(
                        xnT_hi[:, k, ts], xnT_lo[:, k, ts], route_hi[:, k, :], route_lo[:, k, :])])
                mm.then_inc(route_mm, 1)
                up_part(range(OT1 // 2))
                wait(pe, lat_lo_done, LT1 * (j + 1))
                wait(pe, y_done, TPB * j)
                for m in range(LT1):
                    products(bank[EXP_BANK[m]][:], [p for l in range(LT1) for p in passes(
                        *w1_tile(W1_EXP, l, LAT, m * P), lat_hi[:, l, :], lat_lo[:, l, :])]).then_inc(exp_mm, 1)
                up_part(range(OT1 // 2, OT1))
                wait(pe, exp_lo_done, LT1 * (j + 1))
                for i in range(TPB):
                    ts = slice(i * P, (i + 1) * P)
                    wait(pe, routed_done, TPB * j + max(i - 1, 0))
                    products(bank[FC2_BANK[i % 2]][:], [p for l in range(LT1) for p in passes(
                        exp_hi[:, l, ts], exp_lo[:, l, ts], *w1_tile(W1_FC2, l, D, 0, D))]).then_inc(fc2_mm, 1)
                    if i == 0:
                        wait(pe, h_lo_done, OT1 * (j + 1))
                    wait(pe, y_done, TPB * j + max(i - 1, 0))
                    products(bank[DOWN_BANK[i % 2]][:], [p for o in range(OT1) for p in passes(
                        h_hi[:, o, ts], h_lo[:, o, ts], *w1_tile(W1_DOWN, o, D, 0, D))]).then_inc(down_mm, 1)

            block_of_tokens(0)
            with pe.Fori(1, NBLK) as j:
                block_of_tokens(j)


def phase_attn1(nc, t, sem, sb, bank, x_sb, xnT_hi, xnT_lo, ident):
    Q, K, V, G, OW = range(5)
    NSLOT = 8
    NIT = 2 * HEADS
    NST = 2 * CPH - 1
    w_stage = sb("w_stage", [P, 5, D + 1])
    w_hi, w_lo = sb("w_hi", [P, 5, D], F16), sb("w_lo", [P, 5, D], BF16)
    q_hi, q_lo = sb("q_hi", [P, 2, SEQ], F16), sb("q_lo", [P, 2, SEQ], BF16)
    qd_hi, qd_lo = sb("qd_hi", [P, 2, SEQ], F16), sb("qd_lo", [P, 2, SEQ], BF16)
    k_hi, k_lo = sb("k_hi", [P, 2, SEQ], F16), sb("k_lo", [P, 2, SEQ], BF16)
    v_hi, v_lo = sb("v_hi", [P, 2, SEQ], F16), sb("v_lo", [P, 2, SEQ], BF16)
    k_f, v_f = sb("k_f", [P, SEQ]), sb("v_f", [P, SEQ])
    ident_hi, ident_lo = sb("ident_hi", [P, P], F16), sb("ident_lo", [P, P], BF16)
    gate = sb("gate1", [P, 2, SEQ])
    kT_hi, kT_lo = sb("kT_hi", [P, SEQ], F16), sb("kT_lo", [P, SEQ], BF16)
    vd_hi, vd_lo = sb("vd_hi", [P, SEQ], F16), sb("vd_lo", [P, SEQ], BF16)
    p_hi, p_lo = sb("p_hi", [P, SEQ], F16), sb("p_lo", [P, SEQ], BF16)
    st_f = sb("st_f", [P, NST + 1, HD])
    st_hi, st_lo = sb("st_hi", [P, NST + 1, HD], F16), sb("st_lo", [P, NST + 1, HD], BF16)
    sq = sb("sq", [P, SEQ])
    g_hi, g_lo = sb("g_hi", [P, SEQ], F16), sb("g_lo", [P, SEQ], BF16)
    ssum = sb("ssum", [P, TOK])
    y = sb("y_sum", [P, NT, D])
    decay = sb("decay", [P, CH + 2])
    q_decay = sb("q_decay", [P, CH])
    ones = sb("ones", [P, 1])
    small, mv = sb("small2", [P, 7, NT]), sb("mv2", [P, NT, 2])
    KT_BANK, SC_BANK, U_BANK, O_BANK, C_BANK, SS_BANK = (2, 4), 3, 4, (5, 7), (6, 7), 2

    w_in, w_done = [sem(f"w_in{m}") for m in range(5)], [sem(f"w_split{m}") for m in range(5)]
    w_step, qd_in, decay_in = sem("w_step"), sem("q_decay_in"), sem("decay_in")
    proj_done, act_done = sem("proj_done"), sem("proj_act_done")
    q_hi_done, q_lo_done, qd_done, qd_hi_done, qd_lo_done = (sem("q_hi_done"), sem("q_lo_done"), sem("qd_done"),
                                                             sem("qd_hi_done"), sem("qd_lo_done"))
    kv_hi_done, kv_lo_done = sem("kv_hi_done"), sem("kv_lo_done")
    kT_done, kT_hi_done, kT_lo_done = sem("kT_done"), sem("kT_hi_done"), sem("kT_lo_done")
    vd_done, vd_hi_done, vd_lo_done, ident_done = sem("vd_done"), sem("vd_hi_done"), sem("vd_lo_done"), sem("ident_done")
    sc_done, pm_done, p_hi_done, p_lo_done = sem("sc_done"), sem("pm_done"), sem("p_hi_done"), sem("p_lo_done")
    upd_done, st_done, st_hi_done, st_lo_done = sem("upd_done"), sem("st_done"), sem("st_hi_done"), sem("st_lo_done")
    o_done, sq_done, g_done, g_hi_done, g_lo_done = (sem("o_done"), sem("sq_done"), sem("g_done"), sem("g_hi_done"),
                                                     sem("g_lo_done"))
    ss_zero, ss_done, c_done, y_done = sem("ss_zero"), sem("ss_done"), sem("c_done"), sem("y_done")
    ones_done, ss_mm, rms_step, rms_var, rms_sd = (sem("ones_done"), sem("ss_mm"), sem("rms_step"), sem("rms_var"),
                                                   sem("rms_sd"))
    out_ready, out_written, pool_turns = sem("out_ready"), sem("out_written"), sem("pool_turns")
    sp_turns = sem("sp_turns")
    Y0 = 2

    def half(b):
        return slice(b * BLK, (b + 1) * BLK)

    def chunks4(ap):
        return ap.rearrange("p (c n) -> p c n", c=CPH)

    with nc.Block() as block:
        @block.sync
        def _(sp):
            def load(m, h):
                if m == OW:
                    sp.dma_start(w_stage[:, OW, :], t["out_w"][h]).then_inc(w_in[m], 16)
                else:
                    sp.dma_start(w_stage[:, m, 0:D].rearrange("p (k d) -> p k d", k=KT), t["proj_w"][h, :, m]).then_inc(w_in[m], 16)

            def load_q_decay(h):
                sp.dma_start(q_decay[:], t["q_decay"][h].partition_broadcast(P)).then_inc(qd_in, 16)

            def load_decay(h):
                sp.dma_start(decay[:], t["decay"][h]).then_inc(decay_in, 16)

            for m in (Q, K, V, G, OW):
                load(m, 0)
            load_q_decay(0)
            load_decay(0)
            with sp.Fori(1, HEADS) as h:
                for m in (Q, K, V, G):
                    hold(sp, w_done[m], h, sp_turns)
                    load(m, h)
                hold(sp, qd_done, 4 * h, sp_turns)
                load_q_decay(h)
                hold(sp, w_done[OW], h, sp_turns)
                load(OW, h)
                hold(sp, pm_done, 4 * h, sp_turns)
                hold(sp, vd_done, 4 * h, sp_turns)
                hold(sp, st_done, 2 * NST * h, sp_turns)
                load_decay(h)
            out = t["out"].rearrange("(t p) d -> p t d", p=P)
            for i in range(NT):
                sp.wait_ge(out_ready, i + 1)
                sp.dma_start(out[:, i, :], x_sb[:, i, :]).then_inc(out_written, 16)
            sp.wait_ge(out_written, 16 * NT)

        @block.gpsimd
        def _(pool):
            def split(dst_hi, dst_lo, src, hi_done, hi_want, lo_done):
                nc.gpsimd.tensor_scalar(dst_hi, src, 1.0, 0.0, ALU.mult, ALU.add).then_inc(hi_done, 1)
                hold(pool, hi_done, hi_want, pool_turns)
                nc.gpsimd.tensor_tensor(dst_lo, src, dst_hi, ALU.subtract).then_inc(lo_done, 1)

            def split_proj(m, h, step):
                hold(pool, w_in[m], 16 * (h + 1), pool_turns)
                split(w_hi[:, m, :], w_lo[:, m, :], w_stage[:, m, 0:D], w_step, step, w_done[m])

            def split_out(h, step):
                hold(pool, w_in[OW], 16 * (h + 1), pool_turns)
                nc.gpsimd.tensor_scalar(w_stage[:, OW, 0:D], w_stage[:, OW, 0:D], w_stage[:, OW, D:D + 1], 0.5,
                                        ALU.mult, ALU.mult).then_inc(w_step, 1)
                hold(pool, w_step, step - 1, pool_turns)
                split(w_hi[:, OW, :], w_lo[:, OW, :], w_stage[:, OW, 0:D], w_step, step, w_done[OW])

            def split_kv(i, b, n):
                src, hi, lo = ((k_f, k_hi, k_lo), (v_f, v_hi, v_lo))[n // 2]
                hold(pool, act_done, NSLOT * i + 3 + n, pool_turns)
                split(hi[:, b, half(n % 2)], lo[:, b, half(n % 2)], src[:, half(n % 2)], kv_hi_done, 4 * i + n + 1,
                      kv_lo_done)

            def split_decayed(i):
                for n in range(2):
                    hold(pool, vd_done, 2 * (i - 1) + n + 1, pool_turns)
                    split(vd_hi[:, half(n)], vd_lo[:, half(n)], v_f[:, half(n)], vd_hi_done, 2 * (i - 1) + n + 1, vd_lo_done)

            def squares(i, b):
                for n in range(2):
                    cols = slice((1 - b) * SEQ + n * BLK, (1 - b) * SEQ + (n + 1) * BLK)
                    hold(pool, sq_done, 2 * (i - 1) + n + 1, pool_turns)
                    nc.gpsimd.tensor_tensor(ssum[:, cols], ssum[:, cols], sq[:, half(n)], ALU.add).then_inc(ss_done, 1)

            nc.gpsimd.memset(ssum[:], 0.0).then_inc(ss_zero, 1)
            nc.gpsimd.memset(ones[:], 1.0).then_inc(ones_done, 1)
            nc.gpsimd.tensor_copy(ident_hi[:], ident[:]).then_inc(ident_done, 1)
            nc.gpsimd.tensor_copy(ident_lo[:], ident[:]).then_inc(ident_done, 1)
            for m in (Q, K, V, G):
                split_proj(m, 0, m + 1)
            for n in range(4):
                split_kv(0, 0, n)
            pool.wait_ge(ss_zero, 1)
            with pool.Fori(1, HEADS) as h:
                i, step = 2 * h - 1, 4 + 6 * (h - 1)
                split_decayed(i)
                split_kv(i, 1, 0)
                hold(pool, proj_done, NSLOT * i + 2, pool_turns)
                split_proj(Q, h, step + 1)
                split_kv(i, 1, 1)
                split_kv(i, 1, 2)
                hold(pool, proj_done, NSLOT * i + 4, pool_turns)
                split_proj(K, h, step + 2)
                split_kv(i, 1, 3)
                hold(pool, y_done, Y0 + 2 * NSLOT * (h - 1), pool_turns)
                split_out(h - 1, step + 4)
                hold(pool, proj_done, NSLOT * i + 6, pool_turns)
                split_proj(V, h, step + 5)
                squares(i, 1)
                split_decayed(i + 1)
                hold(pool, proj_done, NSLOT * (i + 1), pool_turns)
                split_proj(G, h, step + 6)
                for n in range(4):
                    split_kv(i + 1, 0, n)
                squares(i + 1, 0)
            i = NIT - 1
            split_decayed(i)
            for n in range(4):
                split_kv(i, 1, n)
            pool.wait_ge(y_done, Y0 + 2 * NSLOT * (HEADS - 1))
            split_out(HEADS - 1, 4 + 6 * (HEADS - 1) + 2)
            squares(i, 1)
            split_decayed(i + 1)
            squares(i + 1, 0)

        @block.scalar
        def _(act):
            def projection(i, b, s):
                act.wait_ge(proj_done, NSLOT * i + s + 1)
                src, n = bank[s % 2][:], s % 2
                if s // 2 == Q:
                    nc.scalar.activation(src, src, ACT.Silu).then_inc(act_done, 1)
                    act.wait_ge(act_done, NSLOT * i + s + 1)
                    nc.scalar.activation(q_hi[:, b, half(n)], src, ACT.Copy).then_inc(q_hi_done, 1)
                elif s // 2 == G:
                    nc.scalar.activation(gate[:, b, half(n)], src, ACT.Tanh, scale=0.5).then_inc(act_done, 1)
                else:
                    if s // 2 == K:
                        wait(act, kv_lo_done, 4 * (i - 1) + s - 1)
                    else:
                        wait(act, vd_lo_done, 2 * (i - 1) + n + 1)
                    dst = (k_f if s // 2 == K else v_f)[:, half(n)]
                    nc.scalar.activation(dst, src, ACT.Silu).then_inc(act_done, 1)

            def hi_part(i, s):
                a = i - 1
                n = {0: 0, 1: 1, 2: 0, 3: 0, 4: 1, 5: 1, 6: 0, 7: 1}[s]
                if s < 2:
                    act.wait_ge(kv_lo_done, 4 * a + 3 + n)
                    if n == 0:
                        wait(act, decay_in, decay_loads(i))
                    nc.scalar.activation(v_f[:, half(n)], v_f[:, half(n)], ACT.Copy,
                                         scale=decay[:, CH:CH + 1]).then_inc(vd_done, 1)
                    act.wait_ge(kT_done, 2 * a + n + 1)
                    nc.scalar.activation(kT_hi[:, half(n)], bank[KT_BANK[n]][:, 0:BLK // 2].bitcast(F16),
                                         ACT.Copy).then_inc(kT_hi_done, 1)
                elif s in (2, 4):
                    act.wait_ge(pm_done, 2 * a + n + 1)
                    nc.scalar.activation(p_hi[:, half(n)], bank[SC_BANK][:], ACT.Copy).then_inc(p_hi_done, 1)
                elif s in (3, 5):
                    c = slice(1, CPH + 1) if n == 0 else slice(CPH + 1, NST + 1)
                    act.wait_ge(st_done, NST * a + (CPH if n == 0 else NST))
                    nc.scalar.activation(st_hi[:, c, :], st_f[:, c, :], ACT.Copy).then_inc(st_hi_done, 1)
                else:
                    act.wait_ge(o_done, 2 * a + n + 1)
                    wait(act, ss_done, 2 * (a - 1) + n + 1)
                    nc.scalar.activation(sq[:, half(n)], bank[O_BANK[n]][:], ACT.Square).then_inc(sq_done, 1)
                    act.wait_ge(g_done, 2 * a + n + 1)
                    nc.scalar.activation(g_hi[:, half(n)], bank[O_BANK[n]][:], ACT.Copy).then_inc(g_hi_done, 1)

            def scaled_queries(i, b, n):
                act.wait_ge(qd_done, 2 * i + n + 1)
                nc.scalar.activation(qd_hi[:, b, half(n)], bank[n][:], ACT.Copy).then_inc(qd_hi_done, 1)

            def iteration(i, b, project, attend):
                for s in range(NSLOT):
                    if project:
                        projection(i, b, s)
                    if attend:
                        hi_part(i, s)
                    if project and s < 2:
                        scaled_queries(i, b, s)

            def decay_loads(i):
                return decay_of[0]

            decay_of = [16]
            iteration(0, 0, True, False)
            iteration(1, 1, True, True)
            with act.Fori(1, HEADS) as h:
                decay_of[0] = 16 * h
                iteration(2 * h, 0, True, True)
                decay_of[0] = 16 * (h + 1)
                iteration(2 * h + 1, 1, True, True)
            decay_of[0] = 16 * HEADS
            iteration(NIT, 0, False, True)
            act.wait_ge(rms_var, 1)
            nc.scalar.activation(small[:, 1, :], small[:, 0, :], ACT.Sqrt).then_inc(rms_sd, 1)

        @block.vector
        def _(dve):
            def queries(i, b, n, want):
                dve.wait_ge(q_hi_done, 2 * i + n + 1)
                nc.vector.tensor_tensor(q_lo[:, b, half(n)], bank[n][:], q_hi[:, b, half(n)],
                                        ALU.subtract).then_inc(q_lo_done, 1)
                if n == 0:
                    dve.wait_ge(qd_in, want)
                dve.wait_ge(q_lo_done, 2 * i + n + 1)
                nc.vector.tensor_tensor(chunks4(bank[n][:]), chunks4(bank[n][:]),
                                        q_decay[:].unsqueeze(1).broadcast_to([P, CPH, CH]), ALU.mult).then_inc(qd_done, 1)

            def scaled_queries_lo(i, b, n):
                dve.wait_ge(qd_hi_done, 2 * i + n + 1)
                nc.vector.tensor_tensor(qd_lo[:, b, half(n)], bank[n][:], qd_hi[:, b, half(n)],
                                        ALU.subtract).then_inc(qd_lo_done, 1)

            def keys_lo(a, n):
                dve.wait_ge(kT_hi_done, 2 * a + n + 1)
                nc.vector.tensor_copy(kT_lo[:, half(n)], bank[KT_BANK[n]][:, BLK // 2:].bitcast(BF16)).then_inc(kT_lo_done, 1)

            def mask_scores(a, n):
                dve.wait_ge(sc_done, 2 * a + n + 1)
                dve.wait_ge(vd_done, 2 * a + n + 1)
                nc.vector.tensor_tensor(chunks4(bank[SC_BANK][:]), chunks4(bank[SC_BANK][:]),
                                        decay[:, 0:CH].unsqueeze(1).broadcast_to([P, CPH, CH]), ALU.mult).then_inc(pm_done, 1)

            def scores_lo(a, n):
                dve.wait_ge(p_hi_done, 2 * a + n + 1)
                nc.vector.tensor_tensor(p_lo[:, half(n)], bank[SC_BANK][:], p_hi[:, half(n)],
                                        ALU.subtract).then_inc(p_lo_done, 1)

            def states(a, n):
                dve.wait_ge(upd_done, 2 * a + n + 1)
                wait(dve, st_hi_done, 2 * a)
                for c in (range(CPH) if n == 0 else range(CPH, NST)):
                    u = bank[U_BANK][:, (c % CPH) * HD:(c % CPH + 1) * HD]
                    if c == 0:
                        nc.vector.tensor_copy(st_f[:, 1, :], u).then_inc(st_done, 1)
                    else:
                        dve.wait_ge(st_done, NST * a + c)
                        nc.vector.scalar_tensor_tensor(st_f[:, c + 1, :], st_f[:, c, :], decay[:, CH + 1:CH + 2], u,
                                                       ALU.mult, ALU.add).then_inc(st_done, 1)

            def states_lo(a, n):
                c = slice(1, CPH + 1) if n == 0 else slice(CPH + 1, NST + 1)
                dve.wait_ge(st_hi_done, 2 * a + n + 1)
                nc.vector.tensor_tensor(st_lo[:, c, :], st_f[:, c, :], st_hi[:, c, :], ALU.subtract).then_inc(st_lo_done, 1)

            def gated(a, b, n):
                dve.wait_ge(sq_done, 2 * a + n + 1)
                dve.wait_ge(act_done, NSLOT * a + 2 * G + n + 1)
                nc.vector.scalar_tensor_tensor(bank[O_BANK[n]][:], gate[:, b, half(n)], 1.0, bank[O_BANK[n]][:],
                                               ALU.add, ALU.mult).then_inc(g_done, 1)
                dve.wait_ge(g_hi_done, 2 * a + n + 1)
                nc.vector.tensor_tensor(g_lo[:, half(n)], bank[O_BANK[n]][:], g_hi[:, half(n)],
                                        ALU.subtract).then_inc(g_lo_done, 1)

            def add_out(i, b, tiles):
                for n in tiles:
                    dve.wait_ge(c_done, NSLOT * (i - 2) + n + 1)
                    yt = y[:, b * (NT // 2) + n, :]
                    nc.vector.tensor_tensor(yt, bank[C_BANK[n % 2]][:], yt, ALU.add).then_inc(y_done, 1)

            def iteration(i, b, project, attend, output, qd_want=None):
                a, ab = i - 1, 1 - b
                for s in range(NSLOT):
                    n = {0: 0, 1: 1, 2: 0, 3: 0, 4: 1, 5: 1, 6: 0, 7: 1}[s]
                    if project and s < 2:
                        queries(i, b, s, qd_want)
                    if attend:
                        if s < 2:
                            keys_lo(a, n)
                        elif s in (2, 4):
                            mask_scores(a, n)
                        elif s in (3, 5):
                            states(a, n)
                        else:
                            gated(a, ab, n)
                    if output and 1 <= s <= 4:
                        add_out(i, b, (2 * s - 2, 2 * s - 1))
                    if project and s < 2:
                        scaled_queries_lo(i, b, s)
                    if attend and s in (2, 4):
                        scores_lo(a, n)
                    if attend and s in (3, 5):
                        states_lo(a, n)

            for b in range(2):
                nc.vector.memset(y[:, b * (NT // 2):(b + 1) * (NT // 2), :], 0.0).then_inc(y_done, 1)
            dve.wait_ge(y_done, Y0)
            iteration(0, 0, True, False, False, 16)
            iteration(1, 1, True, True, False, 16)
            with dve.Fori(1, HEADS) as h:
                iteration(2 * h, 0, True, True, True, 16 * (h + 1))
                iteration(2 * h + 1, 1, True, True, True, 16 * (h + 1))
            iteration(NIT, 0, False, True, True)
            iteration(NIT + 1, 1, False, False, True)
            dve.wait_ge(ss_mm, 1)
            nc.vector.tensor_scalar(mv[:, :, 1], bank[SS_BANK][:, 0:NT], 1.0 / (HEADS * HD), None, ALU.mult).then_inc(rms_step, 1)
            nc.vector.memset(mv[:, :, 0], 0.0).then_inc(rms_step, 1)
            norm_small(nc, dve, (rms_step, 2), small, mv, NT, rms_sd, 1, rms_var)
            dve.wait_ge(rms_step, 8)
            dve.wait_ge(y_done, Y0 + NSLOT * NIT)
            for i in range(NT):
                nc.vector.scalar_tensor_tensor(x_sb[:, i, :], y[:, i, :], small[:, 5, i:i + 1], x_sb[:, i, :],
                                               ALU.mult, ALU.add).then_inc(out_ready, 1)

        @block.tensor
        def _(pe):
            def group(out, pairs, start=True, stop=True):
                for n, (w, a) in enumerate(pairs):
                    mm = nc.tensor.matmul(out, w, a, start=start and n == 0, stop=stop and n == len(pairs) - 1)
                return mm

            def w_tile(m, k):
                return w_hi[:, m, k * P:(k + 1) * P], w_lo[:, m, k * P:(k + 1) * P]

            def projection(i, b, s, h):
                m, n = s // 2, s % 2
                if n == 0 and b == 0:
                    pe.wait_ge(w_done[m], h + 1)
                if m == K:
                    pe.wait_ge(qd_lo_done, 2 * i + n + 1)
                else:
                    wait(pe, act_done, NSLOT * i + s - 1)
                if m == V:
                    for c in range(CPH):
                        at = b * SEQ + n * BLK + c * CH
                        mm = group(bank[s % 2][:, c * HD:(c + 1) * HD], [p for k in range(KT) for p in passes(
                            xnT_hi[:, k, at:at + CH], xnT_lo[:, k, at:at + CH], *w_tile(V, k))])
                else:
                    at = b * SEQ + n * BLK
                    mm = group(bank[s % 2][:], [p for k in range(KT) for p in passes(
                        *w_tile(m, k), xnT_hi[:, k, at:at + BLK], xnT_lo[:, k, at:at + BLK])])
                mm.then_inc(proj_done, 1)

            def keys(a, b, n):
                pe.wait_ge(kv_lo_done, 4 * a + n + 1)
                if n == 0:
                    wait(pe, kT_lo_done, 2 * a)
                else:
                    wait(pe, st_done, NST * a)
                for c in range(CPH):
                    at = n * BLK + c * CH
                    for part, src, one, dt in ((0, k_hi, ident_hi, F16), (1, k_lo, ident_lo, BF16)):
                        out = bank[KT_BANK[n]][:, part * BLK // 2:(part + 1) * BLK // 2].bitcast(dt)
                        mm = nc.tensor.transpose(out[:, c * CH:(c + 1) * CH], src[:, b, at:at + CH], one[:])
                mm.then_inc(kT_done, 1)

            def scores(a, b, n):
                pe.wait_ge(kv_lo_done, 4 * a + n + 1)
                pe.wait_ge(q_lo_done, 2 * a + n + 1)
                wait(pe, p_lo_done, 2 * a + n)
                for c in range(CPH):
                    ts = slice(n * BLK + c * CH, n * BLK + (c + 1) * CH)
                    mm = group(bank[SC_BANK][:, c * CH:(c + 1) * CH], passes(
                        k_hi[:, b, ts], k_lo[:, b, ts], q_hi[:, b, ts], q_lo[:, b, ts]))
                mm.then_inc(sc_done, 1)

            def update(a, b, n):
                pe.wait_ge(kT_lo_done, 2 * a + 2)
                pe.wait_ge(vd_lo_done, 2 * a + n + 1)
                wait(pe, st_done, NST * a + n * CPH)
                for c in range(CPH if n == 0 else CPH - 1):
                    ts = slice(n * BLK + c * CH, n * BLK + (c + 1) * CH)
                    mm = group(bank[U_BANK][:, c * HD:(c + 1) * HD], passes(
                        kT_hi[:, ts], kT_lo[:, ts], vd_hi[:, ts], vd_lo[:, ts]))
                mm.then_inc(upd_done, 1)

            def attention(a, b, n):
                pe.wait_ge(p_lo_done, 2 * a + n + 1)
                pe.wait_ge(st_lo_done, 2 * a + n + 1)
                pe.wait_ge(qd_lo_done, 2 * a + n + 1)
                if n == 0:
                    wait(pe, g_lo_done, 2 * a + n)
                else:
                    wait(pe, y_done, Y0 + NSLOT * (a - 1) + NSLOT)
                for c in range(CPH):
                    chunk = n * CPH + c
                    ts = slice(n * BLK + c * CH, n * BLK + (c + 1) * CH)
                    out = bank[O_BANK[n]][:, c * CH:(c + 1) * CH]
                    mm = group(out, passes(v_hi[:, b, ts], v_lo[:, b, ts], p_hi[:, ts], p_lo[:, ts]), stop=chunk == 0)
                    if chunk:
                        mm = group(out, passes(st_hi[:, chunk, :], st_lo[:, chunk, :], qd_hi[:, b, ts], qd_lo[:, b, ts]),
                                   start=False)
                mm.then_inc(o_done, 1)

            def output(i, tiles, h):
                if tiles[0] == 0:
                    pe.wait_ge(w_done[OW], h)
                for n in tiles:
                    ts = slice(n * P, (n + 1) * P)
                    if n % TPB == 0:
                        pe.wait_ge(g_lo_done, 2 * (i - 2) + n // TPB + 1)
                    if n == 1:
                        pe.wait_ge(g_lo_done, 2 * (i - 2) + 2)
                    pe.wait_ge(y_done, Y0 + NSLOT * (i - 2) + n - 1)
                    group(bank[C_BANK[n % 2]][:], passes(g_hi[:, ts], g_lo[:, ts], w_hi[:, OW, :], w_lo[:, OW, :])).then_inc(c_done, 1)

            def iteration(i, b, h, project, attend, out):
                a, ab = i - 1, 1 - b
                for s in range(NSLOT):
                    if project:
                        projection(i, b, s, h)
                    if attend:
                        if s < 2:
                            keys(a, ab, s)
                        elif s in (2, 4):
                            scores(a, ab, s // 2 - 1)
                        elif s in (3, 5):
                            update(a, ab, (s - 3) // 2)
                        else:
                            attention(a, ab, s - 6)
                    if out and 1 <= s <= 4:
                        output(i, (2 * s - 2, 2 * s - 1), h)

            pe.wait_ge(ident_done, 2)
            iteration(0, 0, 0, True, False, False)
            iteration(1, 1, 0, True, True, False)
            with pe.Fori(1, HEADS) as h:
                iteration(2 * h, 0, h, True, True, True)
                iteration(2 * h + 1, 1, h, True, True, True)
            iteration(NIT, 0, HEADS, False, True, True)
            iteration(NIT + 1, 1, HEADS, False, False, True)
            pe.wait_ge(ss_done, 2 * NIT)
            pe.wait_ge(ones_done, 1)
            for i in range(NT):
                mm = nc.tensor.matmul(bank[SS_BANK][:, i:i + 1], ssum[:, i * P:(i + 1) * P], ones[:], start=True, stop=True)
            mm.then_inc(ss_mm, 1)


def decay_tables():
    base = np.float32(1.0 / 2.0 ** (8.0 / HEADS))
    factor = np.float32(1.0 - LAYER_IDX / (N_LAYERS - 1 + 1e-05) + 1e-05)
    slope = (base ** (np.arange(HEADS, dtype=np.float32) + 1) * factor).astype(np.float64)
    n = np.arange(CH, dtype=np.float64)
    dist = n[None, :] - n[:, None]
    mask = np.where(dist >= 0, np.exp(-slope[:, None, None] * np.maximum(dist, 0)), 0.0)
    key = np.exp(-slope[:, None] * (CH - 1 - n))[:, :, None]
    block = np.broadcast_to(np.exp(-slope * CH)[:, None, None], (HEADS, P, 1))
    tables = np.concatenate([mask, key, block], axis=2).astype(np.float32)
    query = np.exp(-slope[:, None] * (n + 1)).astype(np.float32)
    return tables, query


def kernel(**inp):
    import concourse.bacc as bacc
    from concourse.bass_utils import run_bass_kernel_spmd

    a = {k: np.asarray(v) for k, v in inp.items()}

    def pad(m, rows=None, cols=None):
        out = np.zeros((rows or m.shape[0], cols or m.shape[1]), m.dtype)
        out[:m.shape[0], :m.shape[1]] = m
        return out

    def tiles(m):
        return m.reshape(-1, P, m.shape[-1]).transpose(1, 0, 2)

    qkv = a["L1_attn_qkv_w"].reshape(HEADS, 3, HD, KT, P).transpose(0, 4, 1, 3, 2)
    gate = a["L1_attn_gate_w"].reshape(HEADS, 1, HD, KT, P).transpose(0, 4, 1, 3, 2)
    proj = np.concatenate([qkv, gate], axis=2)
    out_w = a["L1_attn_out_w"].T.reshape(HEADS, HD, D)
    out_w = np.concatenate([out_w, a["L1_attn_norm_w"].reshape(HEADS, HD, 1)], axis=2)
    tables, query = decay_tables()
    arrays = dict(
        x=a["L0_attn_x"].reshape(TOK, D),
        wq0=a["L0_attn_Wq"].reshape(D, -1), wk0=a["L0_attn_Wk"].reshape(D, -1), wv0=a["L0_attn_Wv"].reshape(D, -1),
        bq0=a["L0_attn_bq"].reshape(-1), bk0=a["L0_attn_bk"].reshape(-1), bv0=a["L0_attn_bv"].reshape(-1),
        gate_q=pad(a["L0_ffn_gate_q"].T, cols=INT0P), up_q=pad(a["L0_ffn_up_q"].T, cols=INT0P),
        down_q=pad(a["L0_ffn_down_q"].T, rows=INT0P),
        gate_s=pad(a["L0_ffn_gate_scale"][:, None], rows=INT0P).reshape(OT0, P).T,
        up_s=pad(a["L0_ffn_up_scale"][:, None], rows=INT0P).reshape(OT0, P).T,
        down_s=a["L0_ffn_down_scale"],
        gate_A=a["L0_ffn_gate_A"], up_A=a["L0_ffn_up_A"], down_A=pad(a["L0_ffn_down_A"], rows=INT0P),
        gate_B=pad(a["L0_ffn_gate_B"], cols=INT0P), up_B=pad(a["L0_ffn_up_B"], cols=INT0P), down_B=a["L0_ffn_down_B"],
        w1=np.concatenate([tiles(a["L1_ffn_" + n]).reshape(P, -1)
                           for n in ("up_w", "down_w", "fc1_w", "expert_w", "fc2_w")], axis=1),
        route_w=tiles(a["L1_ffn_gate_w"]),
        gamma=a["L1_ffn_ln_gamma"], beta=a["L1_ffn_ln_beta"],
        proj_w=proj, out_w=out_w, decay=tables, q_decay=query,
    )
    nc = bacc.Bacc("TRN2", target_bir_lowering=False, num_devices=1)
    t, feed = {}, {}
    for name, v in arrays.items():
        v = np.ascontiguousarray(v)
        feed[f"{name}_dram"] = v
        t[name] = nc.dram_tensor(f"{name}_dram", v.shape, mybir.dt.from_np(v.dtype), kind="ExternalInput").ap()
    t["out"] = nc.dram_tensor("out_dram", (TOK, D), F32, kind="ExternalOutput").ap()
    build(nc, t)
    r = run_bass_kernel_spmd(nc, [feed], core_ids=[0])
    return r.results[0]["out_dram"].reshape(BATCH, SEQ, D)
```

```python
from contextlib import ExitStack

import numpy as np
import concourse.bass as bass
from concourse import mybir

ALU = mybir.AluOpType
ACT = mybir.ActivationFunctionType
F32, F16, BF16, I32 = mybir.dt.float32, mybir.dt.float16, mybir.dt.bfloat16, mybir.dt.int32
AX_X = mybir.AxisListType.X

P = 128
D = 512
KT = D // P
BATCH, SEQ = 2, 1024
TOK = BATCH * SEQ
NT = TOK // P
BLK = 512
NBLK = TOK // BLK
TPB = BLK // P
EPS = 1e-5

QD, NH0 = 16, 32
INT0, RANK = 1376, 32
OT0 = -(-INT0 // P)
INT0P = OT0 * P
Q_ZERO, Q_STEP, LR_SCALE = 7.5, 0.005, 0.02
LRA, LRB = 16.0, 64.0

HEADS, HD, CH = 32, 128, 128
CPH = BLK // CH
LAYER_IDX, N_LAYERS = 1, 32
INT1, LAT, NE = 1024, 256, 8
OT1, LT1 = INT1 // P, LAT // P
SQ_DOWN = 1.0 / 8.0
W1_UP, W1_DOWN = 0, KT * INT1
W1_FC1 = W1_DOWN + OT1 * D
W1_EXP = W1_FC1 + KT * LAT
W1_FC2 = W1_EXP + LT1 * LAT
W1_COLS = W1_FC2 + LT1 * D
W1_PER_BLK = 8
W1_CHUNK = W1_COLS // ((NBLK - 1) * W1_PER_BLK)
assert W1_CHUNK * (NBLK - 1) * W1_PER_BLK == W1_COLS and W1_PER_BLK % 2 == 0
R3 = 3 * RANK


def passes(w_hi, w_lo, a_hi, a_lo):
    return ((w_hi, a_hi), (w_hi, a_lo), (w_lo, a_hi))


def ds(at, n):
    return slice(at, at + n) if isinstance(at, int) else bass.ds(at, n)


def wait(eng, s, count):
    if not isinstance(count, int) or count > 0:
        eng.wait_ge(s, count)


def hold(eng, s, count, turns):
    if not isinstance(count, int):
        eng.wait_ge(s, count)
        eng.sem_inc(turns, 1)
    elif count > 0:
        eng.wait_ge(s, count)


class Place:

    def __init__(self, flat):
        self.flat, self.taken = flat, 0

    def __call__(self, shape, dt=F32):
        cols = int(np.prod(shape[1:])) // (2 if dt in (F16, BF16) else 1)
        view = self.flat[0:shape[0], self.taken:self.taken + cols]
        self.taken += cols
        assert self.taken <= self.flat.shape[1]
        view = view if dt == F32 else view.bitcast(dt)
        if len(shape) == 2:
            return view
        names = " ".join("abc"[:len(shape) - 1])
        return view.rearrange(f"p ({names}) -> p {names}", **dict(zip("abc", shape[1:])))


def build(nc, t):
    with ExitStack() as ctx:
        def sb(stack, name, shape, dt=F32):
            return stack.enter_context(nc.sbuf_tensor(name, shape, dt))

        turns = {name: ctx.enter_context(nc.semaphore(name)) for name in ("pool_turns", "sp_turns", "dve_turns")}

        def sem(name):
            return turns[name] if name in turns else ctx.enter_context(nc.semaphore(name))

        def sem_attn1(name):
            return sem(name if name in turns else "attn1_" + name)

        x_sb = sb(ctx, "x_sb", [P, NT, D])
        xnT_hi = sb(ctx, "xnT_hi", [P, KT, TOK], F16)
        xnT_lo = sb(ctx, "xnT_lo", [P, KT, TOK], BF16)
        ident = sb(ctx, "ident", [P, P])
        norm1_small = sb(ctx, "stats1", [P, TPB, 6]), sb(ctx, "mv1", [P, TPB, 2]), sb(ctx, "small1", [P, 7, TPB])
        bank = [ctx.enter_context(nc.psum_tensor(f"bank{i}", [P, 512], F32)) for i in range(8)]

        region = sb(ctx, "region", [P, W1_COLS])
        w1 = dict(hi=region[:, 0:W1_COLS // 2].bitcast(F16), lo=region[:, W1_COLS // 2:].bitcast(BF16))
        norm1 = Norm(nc, sem, "1", *norm1_small, True, None, (6, 7), bank, x_sb, xnT_hi, xnT_lo, ident)
        with ExitStack() as s:
            phase_layer0(nc, t, sem, lambda *a: sb(s, *a), bank, x_sb, xnT_hi, xnT_lo, ident, region, w1, norm1)
        y = sb(ctx, "y_sum", [P, NT, D])
        hw = HeadWeights(nc, t, sem_attn1, lambda *a: sb(ctx, *a))
        with ExitStack() as s:
            ffn1_tail = phase_norm1_ffn1(nc, t, sem, lambda *a: sb(s, *a), bank, x_sb, xnT_hi, xnT_lo, ident, w1, y, hw, norm1)
        with ExitStack() as s:
            phase_attn1(nc, t, sem_attn1, lambda *a: sb(s, *a), bank, x_sb, xnT_hi, xnT_lo, region, y, hw, ffn1_tail)


def variance(nc, eng, step, want, small, mv, n, var_ready):
    eng.wait_ge(step, want)
    nc.vector.tensor_scalar(small[:, 0, 0:n], mv[:, 0:n, 1], EPS, None, ALU.add).then_inc(var_ready, 1)


def norm_factors(nc, eng, done, c, small, mv, n, sd_ready, sd_want):
    veps, sd, r0, a, b, r, nmr = (small[:, i, 0:n] for i in range(7))
    mean = mv[:, 0:n, 0]
    eng.wait_ge(sd_ready, sd_want)
    nc.vector.reciprocal(r0, sd).then_inc(done, 1)
    eng.wait_ge(done, c + 1)
    nc.vector.tensor_tensor(a, r0, r0, ALU.mult).then_inc(done, 1)
    eng.wait_ge(done, c + 2)
    nc.vector.tensor_tensor(b, a, veps, ALU.mult).then_inc(done, 1)
    eng.wait_ge(done, c + 3)
    nc.vector.tensor_scalar(a, b, -0.5, 1.5, ALU.mult, ALU.add).then_inc(done, 1)
    eng.wait_ge(done, c + 4)
    nc.vector.tensor_tensor(r, r0, a, ALU.mult).then_inc(done, 1)
    eng.wait_ge(done, c + 5)
    nc.vector.scalar_tensor_tensor(nmr, r, -1.0, mean, ALU.mult, ALU.mult).then_inc(done, 1)


class Norm:
    STEPS = 2 * TPB + 6

    def __init__(self, nc, sem, tag, stats, mv, small, one_group, xn, banks, bank, x_sb, xnT_hi, xnT_lo, ident):
        self.nc, self.stats, self.mv, self.small, self.one_group = nc, stats, mv, small, one_group
        self.xn, self.bank = xn, [bank[b] for b in banks]
        self.x, self.hi, self.lo, self.ident = x_sb, xnT_hi, xnT_lo, ident
        self.step, self.var_ready, self.sd_ready = sem("step" + tag), sem("var_ready" + tag), sem("sd_ready" + tag)
        self.xn_done, self.xT_done, self.hi_done, self.lo_done = (sem("xn_done" + tag), sem("xT_done" + tag),
                                                                  sem("hi_done" + tag), sem("lo_done" + tag))

    def slot(self, g, i):
        return i if self.one_group else g * TPB + i

    def row_tile(self, g, i):
        return self.x[:, ds(g * TPB + i, 1), :].rearrange("p a d -> p (a d)")

    def earlier(self, g, i):
        return i >= 2 or isinstance(g, int) and g >= 1

    def dve_moments(self, dve, g, turns=None, loaded=None):
        c, first = g * self.STEPS, self.slot(g, 0)
        for i in range(TPB):
            if loaded and i % 2 == 0:
                dve.wait_ge(loaded[i // 2], 16)
            self.nc.vector.bn_stats(self.stats[:, first + i, :], self.row_tile(g, i)).then_inc(self.step, 1)
        hold(dve, self.step, c + TPB, turns)
        for i in range(TPB):
            self.nc.vector.bn_aggr(self.mv[:, first + i, :], self.stats[:, first + i, :]).then_inc(self.step, 1)
        variance(self.nc, dve, self.step, c + 2 * TPB, self.small[:, :, first:first + TPB],
                 self.mv[:, first:first + TPB, :], TPB, self.var_ready)

    def dve_factors(self, dve, g):
        first = self.slot(g, 0)
        norm_factors(self.nc, dve, self.step, g * self.STEPS + 2 * TPB, self.small[:, :, first:first + TPB],
                     self.mv[:, first:first + TPB, :], TPB, self.sd_ready, g + 1)

    def act_sqrt(self, act, g):
        first = self.slot(g, 0)
        veps, sd = (self.small[:, i, first:first + TPB] for i in (0, 1))
        act.wait_ge(self.var_ready, g + 1)
        self.nc.scalar.activation(sd, veps, ACT.Sqrt).then_inc(self.sd_ready, 1)

    def act_rows(self, act, g, i):
        at = self.slot(g, i)
        if i == 0:
            act.wait_ge(self.step, (g + 1) * self.STEPS)
        if self.earlier(g, i):
            act.wait_ge(self.xT_done, g * TPB + i - 1)
        self.nc.scalar.activation(self.xn[:, i % 2, :], self.row_tile(g, i), ACT.Identity,
                                  scale=self.small[:, 5, at:at + 1], bias=self.small[:, 6, at:at + 1]).then_inc(self.xn_done, 1)

    def pe_turn(self, pe, g, i):
        pe.wait_ge(self.xn_done, g * TPB + i + 1)
        if self.earlier(g, i):
            pe.wait_ge(self.lo_done, g * TPB + i - 1)
        for k in range(KT):
            mm = self.nc.tensor.transpose(self.bank[i % 2][:, k * P:(k + 1) * P], self.xn[:, i % 2, k * P:(k + 1) * P],
                                          self.ident[:])
        mm.then_inc(self.xT_done, 1)

    def act_hi(self, act, g, i):
        act.wait_ge(self.xT_done, g * TPB + i + 1)
        self.nc.scalar.activation(self.hi[:, :, ds((g * TPB + i) * P, P)],
                                  self.bank[i % 2][:].rearrange("p (k t) -> p k t", k=KT), ACT.Copy).then_inc(self.hi_done, 1)

    def dve_lo(self, dve, g, i):
        dve.wait_ge(self.hi_done, g * TPB + i + 1)
        tok = ds((g * TPB + i) * P, P)
        self.nc.vector.tensor_tensor(self.lo[:, :, tok], self.bank[i % 2][:].rearrange("p (k t) -> p k t", k=KT),
                                     self.hi[:, :, tok], ALU.subtract).then_inc(self.lo_done, 1)


def phase_layer0(nc, t, sem, sb, bank, x_sb, xnT_hi, xnT_lo, ident, region, w1, norm1):
    GU_COLS = KT * 4 * RANK
    A_COLS = GU_COLS + OT0 * R3
    w0 = dict(
        gate=sb("w0_gate", [P, KT, INT0P], F16), up=sb("w0_up", [P, KT, INT0P], F16), down=sb("w0_down", [P, OT0, D], F16),
        A_hi=sb("w0_A_hi", [P, A_COLS], F16), A_lo=sb("w0_A_lo", [P, A_COLS], BF16),
        B=sb("w0_B", [P, 2 * INT0P + D], F16),
        scale=sb("w0_scale", [P, 2, OT0]), down_scale=sb("w0_down_scale", [P, D]),
    )
    qkv, kext, smax = sb("qkv0", [P, NT, 3 * QD]), sb("kext", [P, 2, NT]), sb("smax", [P, NT, QD])
    prob = sb("prob0", [P, TPB, QD, QD])
    den, att = sb("den0", [P, 2, TPB, QD]), sb("att0", [P, TPB, QD])
    full = [P, TPB, QD, QD]
    norm1.xn = prob[:].rearrange("p t d e -> p (t d e)").rearrange("p (a b) -> p a b", a=2)

    short = Place(region)
    NSTAGE = 4
    stage_f = short([P, NSTAGE, INT0P])
    norm = Norm(nc, sem, "0", short([P, NT, 6]), short([P, NT, 2]), short([P, 7, NT]), False, short([P, 2, D]),
                (6, 7), bank, x_sb, xnT_hi, xnT_lo, ident)
    wq, bq = short([P, KT, QD * NH0]), short([P, QD * NH0])
    w48, b48 = short([P, KT, 3 * QD]), short([P, 3 * QD])
    w48_hi, w48_lo = short([P, KT, 3 * QD], F16), short([P, KT, 3 * QD], BF16)
    sext = short([P, 2, NT, QD])

    x0_in, x_in = [sem(f"x0_in{i}") for i in range(2)], [None] + [sem(f"x_in{i}") for i in range(1, NBLK)]
    stage_in = [sem(f"stage_in{i}") for i in range(NSTAGE)]
    w_in, scale_in, scale_done = sem("w0_in"), sem("scale_in"), sem("scale_done")
    chunk_done, split_step, id_zero, id_done = sem("chunk_done"), sem("split_step"), sem("id_zero"), sem("id_done")
    B_in, B_hi_done, B_done = sem("B_in"), sem("B_hi_done"), sem("B_done")
    B_zero = sem("B_zero")
    w48_step, w48_done = sem("w48_step"), sem("w48_done")
    qkv_done, qkv_out, att_step = sem("qkv0_done"), sem("qkv0_out"), sem("att_step")
    qk_done, score_done, exp_done = sem("qk0_done"), sem("score0_done"), sem("exp0_done")
    den_done, pv_done, num_done, rden_done, att_done, att_added = (
        sem("den0_done"), sem("pv0_done"), sem("num0_done"), sem("rden0_done"), sem("att0_done"), sem("att0_added"))

    x_dram = t["x"].rearrange("(t p) d -> p t d", p=P)

    chunks = []

    def staged(i, cols, rows=P, ints=False):
        view = stage_f[0:rows, i % NSTAGE, 0:cols]
        return view.bitcast(I32) if ints else view

    def add_A(names, at, n):
        view = staged(len(chunks), n * len(names) * RANK).rearrange("p (k r) -> p k r", k=n)
        chunks.append(("A", [(view[:, :, c * RANK:(c + 1) * RANK], t[name + "_A"].rearrange("(k p) r -> p k r", p=P))
                             for c, name in enumerate(names)], slice(at, at + n * len(names) * RANK)))
        return len(chunks)

    def add_B(name, at, cols):
        view = staged(len(chunks), cols, R3)
        chunks.append(("B", [(view[c * RANK:(c + 1) * RANK, :], t[name + "_B"]) for c in range(3)], slice(at, at + cols)))
        return len(chunks)

    def add_int(name, tiles):
        cols = slice(tiles.start * P, tiles.stop * P)
        view = staged(len(chunks), KT * (cols.stop - cols.start), ints=True)
        src = t[name + "_q"].rearrange("(k p) o -> p k o", p=P)[:, :, cols]
        chunks.append(("int", [(view.rearrange("p (k o) -> p k o", k=KT), src)], w0[name][:, :, cols]))
        return len(chunks)

    A_READY = add_A(("gate", "gate", "up", "up"), 0, KT)
    PAIRS = [slice(o, min(o + 2, OT0)) for o in range(0, OT0, 2)]
    GATE_READY, UP_READY = zip(*((add_int("gate", pair), add_int("up", pair)) for pair in PAIRS))
    add_A(("down",) * 3, GU_COLS, OT0)
    down_dram = t["down_q"].rearrange("(o p) d -> p o d", p=P)
    for a in range(0, OT0, 2):
        b = min(a + 2, OT0)
        view = staged(len(chunks), (b - a) * D, ints=True).rearrange("p (o d) -> p o d", d=D)
        chunks.append(("int", [(view, down_dram[:, a:b, :])], w0["down"][:, a:b, :]))
    DOWN_READY = add_B("down", 2 * INT0P, D)
    SPLIT_FIRST = UP_READY[2]
    SPLIT_AT = [range(min(i, DOWN_READY), min(i + 2, DOWN_READY)) for i in range(SPLIT_FIRST, SPLIT_FIRST + 2 * OT0, 2)]
    assert SPLIT_AT[-1].stop == DOWN_READY
    h_hi, h_lo = sb("h0_hi", [P, OT0, BLK], F16), sb("h0_lo", [P, OT0, BLK], BF16)
    B_stage = h_hi[:].rearrange("p o t -> p (o t)").bitcast(F32)
    assert OT0 * BLK // 2 == 2 * INT0P
    g, u, s = sb("g0", [P, 2, BLK]), sb("u0", [P, 2, BLK]), sb("s0", [P, 2, BLK])
    stack = [sb("xa_gate", [R3, BLK], F16), sb("xa_up", [P, BLK], F16), sb("xa_down", [R3, BLK], F16)]
    stack_rows = [(slice(0, 2 * RANK), slice(0, RANK), slice(2 * RANK, R3)),
                  (slice(2 * RANK, P), slice(2 * RANK, R3), slice(RANK, 2 * RANK)),
                  (slice(0, R3), slice(2 * RANK, R3), slice(2 * RANK, R3))]
    scaled = s
    w1_stage = sb("w1_stage", [P, 2, W1_CHUNK])

    xa_done, stack_hi, stack_done = sem("xa_done"), sem("stack_hi"), sem("stack_done")
    gm_done, um_done, gl_done, ul_done = sem("gate_main"), sem("up_main"), sem("gate_low"), sem("up_low")
    gs_done, us_done = sem("gate_scaled"), sem("up_scaled")
    g_done, u_done, s_done = sem("gate_summed"), sem("up_summed"), sem("silu_done")
    h_done, h_hi_done, h_lo_done = sem("h0_done"), sem("h0_hi_done"), sem("h0_lo_done")
    dm_done, dl_done, scaled_done, xl_done, x_done = (sem("down_main"), sem("down_low"), sem("down_scaled"),
                                                      sem("x_low_added"), sem("x_done"))
    w1_in = [sem(f"w1_in{i}") for i in range(2)]
    w1_hi_done, w1_lo_done = sem("w1_hi_done"), sem("w1_lo_done")
    pool_turns, sp_turns, dve_turns = sem("pool_turns"), sem("sp_turns"), sem("dve_turns")
    LR = LR_SCALE * LRA
    UNDO = 1.0 / (LRA * LRB)
    XA, HA, GL, UL = 6, 7, 4, 5
    OUT_MAIN, OUT_LOW = (6, 0), (7, 1)
    QKV_BANK = (6, 7)

    STATS_AT = {0: 1, 2: 2, 4: 3}
    TILES_AT = {o: ((o // 2, 2 * (o % 2)), (o // 2, 2 * (o % 2) + 1)) for o in range(2, 8)}
    STATS1_AT, TILES1_AT = 3, {5: (0, 1), 7: (2, 3)}
    QKV_AT = {8: 0, 9: 1}
    ATT_STEPS = 5

    def inserted(j, o):
        if isinstance(j, int):
            return norm, STATS_AT.get(o), TILES_AT.get(o, ())
        return norm1, j - 1 if o == STATS1_AT else None, [(j - 1, i) for i in TILES1_AT.get(o, ())]

    def upto(j, o):
        return j * OT0 + max(o + 1, 0)

    with nc.Block() as block:
        @block.sync
        def _(sp):
            def load_x(i):
                sp.dma_start(x_sb[:, i * TPB:(i + 1) * TPB, :], x_dram[:, i * TPB:(i + 1) * TPB, :]).then_inc(x_in[i], 16)

            for i in range(2):
                pair = slice(2 * i, 2 * i + 2)
                sp.dma_start(x_sb[:, pair, :], x_dram[:, pair, :]).then_inc(x0_in[i], 16)
            sp.dma_start(w0["scale"][:, 0, :], t["gate_s"]).then_inc(scale_in, 16)
            sp.dma_start(w0["scale"][:, 1, :], t["up_s"]).then_inc(scale_in, 16)
            sp.dma_start(w0["down_scale"][:], t["down_s"].partition_broadcast(P)).then_inc(scale_in, 16)
            for i, (_, dmas, _) in enumerate(chunks):
                if i >= NSTAGE:
                    sp.wait_ge(chunk_done, i - NSTAGE + 1)
                for dst, src in dmas:
                    sp.dma_start(dst, src).then_inc(stage_in[i % NSTAGE], 16)
                if i + 1 == UP_READY[0]:
                    for m, name in enumerate(("gate_B", "up_B")):
                        for c in range(m, m + 3):
                            sp.dma_start(B_stage[c * RANK:(c + 1) * RANK, m * INT0P:(m + 1) * INT0P], t[name]).then_inc(B_in, 16)
                if i + 1 in UP_READY[1:NBLK]:
                    load_x(UP_READY.index(i + 1))
                if i + 1 == UP_READY[-1]:
                    sp.dma_start(wq, t["wq0"].rearrange("(k p) n -> p k n", p=P)).then_inc(w_in, 16)
                    sp.dma_start(w48[:, :, QD:2 * QD], t["wk0"].rearrange("(k p) n -> p k n", p=P)).then_inc(w_in, 16)
                    sp.dma_start(w48[:, :, 2 * QD:], t["wv0"].rearrange("(k p) n -> p k n", p=P)).then_inc(w_in, 16)
                    sp.dma_start(bq, t["bq0"].partition_broadcast(P)).then_inc(w_in, 16)
                    sp.dma_start(b48[:, QD:2 * QD], t["bk0"].partition_broadcast(P)).then_inc(w_in, 16)
                    sp.dma_start(b48[:, 2 * QD:], t["bv0"].partition_broadcast(P)).then_inc(w_in, 16)

            def block_of_tokens(j):
                hold(sp, att_added, TPB * j, sp_turns)
                for c in range(W1_PER_BLK):
                    if c >= 2:
                        hold(sp, w1_lo_done, (j - 1) * W1_PER_BLK + c - 1, sp_turns)
                    at = ((j - 1) * W1_PER_BLK + c) * W1_CHUNK
                    sp.dma_start(w1_stage[:, c % 2, :], t["w1"][:, ds(at, W1_CHUNK)]).then_inc(w1_in[c % 2], 16)

            with sp.Fori(1, NBLK) as j:
                block_of_tokens(j)

        @block.gpsimd
        def _(pool):
            nc.gpsimd.memset(ident[:], 0.0).then_inc(id_zero, 1)
            pool.wait_ge(id_zero, 1)
            nc.gpsimd.affine_select(out=ident[:], in_=ident[:], compare_op=ALU.not_equal, fill=1.0, base=0,
                                    pattern=[[-1, P]], channel_multiplier=1).then_inc(id_done, 1)
            pool.wait_ge(scale_in, 48)
            nc.gpsimd.tensor_scalar(w0["scale"][:], w0["scale"][:], Q_STEP, 1.0, ALU.mult, ALU.mult).then_inc(scale_done, 1)
            nc.gpsimd.tensor_scalar(w0["down_scale"][:], w0["down_scale"][:], Q_STEP, 1.0, ALU.mult,
                                    ALU.mult).then_inc(scale_done, 1)
            landed, steps = [0] * NSTAGE, [0]

            def split_chunk(i):
                kind, dmas, dst = chunks[i]
                landed[i % NSTAGE] += 16 * len(dmas)
                pool.wait_ge(stage_in[i % NSTAGE], landed[i % NSTAGE])
                if kind == "int":
                    nc.gpsimd.tensor_scalar(dst, dmas[0][0], 1.0, -Q_ZERO, ALU.mult, ALU.add).then_inc(chunk_done, 1)
                elif kind == "A":
                    view = staged(i, dst.stop - dst.start)
                    nc.gpsimd.tensor_copy(w0["A_hi"][:, dst], view).then_inc(split_step, 1)
                    steps[0] += 1
                    pool.wait_ge(split_step, steps[0])
                    nc.gpsimd.tensor_tensor(w0["A_lo"][:, dst], view, w0["A_hi"][:, dst], ALU.subtract).then_inc(chunk_done, 1)
                else:
                    view = staged(i, dst.stop - dst.start, R3)
                    mid = slice(RANK, 2 * RANK)
                    pool.wait_ge(chunk_done, i)
                    nc.gpsimd.tensor_scalar(view, view, LRB, 1.0, ALU.mult, ALU.mult).then_inc(split_step, 1)
                    pool.wait_ge(split_step, steps[0] + 1)
                    nc.gpsimd.tensor_copy(w0["B"][0:R3, dst], view).then_inc(split_step, 1)
                    steps[0] += 2
                    pool.wait_ge(split_step, steps[0])
                    nc.gpsimd.tensor_tensor(w0["B"][mid, dst], view[mid, :], w0["B"][mid, dst],
                                            ALU.subtract).then_inc(chunk_done, 1)
                    pool.wait_ge(chunk_done, i + 1)

            def softmax_part(j):
                at = j * TPB
                hold(pool, att_step, ATT_STEPS, pool_turns)
                hold(pool, att_done, j, pool_turns)
                hold(pool, norm1.xT_done, TPB * j, pool_turns)
                q, k, v = (qkv[:, ds(at, TPB), i * QD:(i + 1) * QD] for i in range(3))
                nc.gpsimd.tensor_tensor(prob[:], q.unsqueeze(3).broadcast_to(full), k.unsqueeze(2).broadcast_to(full),
                                        ALU.mult).then_inc(qk_done, 1)
                hold(pool, qk_done, j + 1, pool_turns)
                nc.gpsimd.tensor_tensor(prob[:], prob[:], smax[:, ds(at, TPB), :].unsqueeze(3).broadcast_to(full),
                                        ALU.subtract).then_inc(score_done, 1)
                hold(pool, den_done, j + 1, pool_turns)
                nc.gpsimd.tensor_tensor(prob[:], prob[:], v.unsqueeze(2).broadcast_to(full), ALU.mult).then_inc(pv_done, 1)
                hold(pool, att_done, j + 1, pool_turns)
                for i in range(TPB):
                    hold(pool, x_done, TPB * j + i + 1, pool_turns)
                    x = x_sb[:, ds(at + i, 1), :].rearrange("p a (d h) -> p (a d) h", h=NH0)
                    nc.gpsimd.tensor_tensor(x, x, att[:, i, :].unsqueeze(2).broadcast_to([P, QD, NH0]),
                                            ALU.add).then_inc(att_added, 1)

            def block_of_tokens(j):
                for o in range(OT0):
                    hold(pool, h_done, upto(j, o), pool_turns)
                    hold(pool, dm_done, TPB * j, pool_turns)
                    nc.gpsimd.tensor_scalar(h_hi[:, o, :], s[:, o % 2, :], 1.0, 0.0, ALU.mult, ALU.add).then_inc(h_hi_done, 1)
                    if isinstance(j, int):
                        for i in SPLIT_AT[o]:
                            split_chunk(i)
                    elif o < W1_PER_BLK:
                        n = (j - 1) * W1_PER_BLK + o
                        cols = ds(n * W1_CHUNK, W1_CHUNK)
                        hold(pool, w1_in[o % 2], 16 * ((j - 1) * (W1_PER_BLK // 2) + o // 2 + 1), pool_turns)
                        nc.gpsimd.tensor_copy(w1["hi"][:, cols], w1_stage[:, o % 2, :]).then_inc(w1_hi_done, 1)
                        hold(pool, w1_hi_done, n + 1, pool_turns)
                        nc.gpsimd.tensor_tensor(w1["lo"][:, cols], w1_stage[:, o % 2, :], w1["hi"][:, cols],
                                                ALU.subtract).then_inc(w1_lo_done, 1)
                softmax_part(j)

            for i in range(SPLIT_FIRST):
                split_chunk(i)
            block_of_tokens(0)
            with pool.Fori(1, NBLK) as j:
                block_of_tokens(j)

        @block.scalar
        def _(act):
            def stack_part(j, i, b):
                wait(act, xa_done, 2 * j + (2 if i == 2 else 1))
                wait(act, (gl_done, ul_done, dl_done)[i], (OT0, OT0, TPB)[i] * j)
                rows = stack_rows[i][0]
                nc.scalar.activation(stack[i][rows], bank[b][rows], ACT.Copy, scale=LR).then_inc(stack_hi, 1)

            norm.act_sqrt(act, 0)
            norm.act_rows(act, 0, 0)
            for i in range(TPB):
                if i + 1 < TPB:
                    norm.act_rows(act, 0, i + 1)
                norm.act_hi(act, 0, i)
            act.wait_ge(scale_done, 2)

            def block_of_tokens(j):
                stack_part(j, 0, XA)
                stack_part(j, 1, XA)
                for o in range(OT0 + 1):
                    n, stats_group, tiles = inserted(j, o)
                    for tile in tiles:
                        n.act_rows(act, *tile)
                    if o < OT0:
                        wait(act, gm_done, upto(j, o))
                        wait(act, s_done, upto(j, o - 2))
                        nc.scalar.activation(g[:, o % 2, :], bank[o % 2][:], ACT.Copy,
                                             scale=w0["scale"][:, 0, o:o + 1]).then_inc(gs_done, 1)
                        wait(act, um_done, upto(j, o))
                        wait(act, h_done, upto(j, o - 2))
                        nc.scalar.activation(u[:, o % 2, :], bank[2 + o % 2][:], ACT.Copy,
                                             scale=w0["scale"][:, 1, o:o + 1]).then_inc(us_done, 1)
                    for tile in tiles:
                        n.act_hi(act, *tile)
                    if o >= 1:
                        wait(act, g_done, upto(j, o - 1))
                        wait(act, h_lo_done, upto(j, o - 3))
                        nc.scalar.activation(s[:, (o - 1) % 2, :], g[:, (o - 1) % 2, :], ACT.Silu).then_inc(s_done, 1)
                    if stats_group is not None:
                        n.act_sqrt(act, stats_group)
                stack_part(j, 2, HA)
                wait(act, score_done, j + 1)
                nc.scalar.activation(prob[:], prob[:], ACT.Exp, scale=QD ** -0.5).then_inc(exp_done, 1)

            block_of_tokens(0)
            with act.Fori(1, NBLK) as j:
                block_of_tokens(j)

        @block.vector
        def _(dve):
            def stack_part(j, i, b):
                wait(dve, stack_hi, 3 * j + i + 1)
                _, src, lo = stack_rows[i]
                nc.vector.scalar_tensor_tensor(stack[i][lo], bank[b][src], LR, stack[i][src],
                                               ALU.mult, ALU.subtract).then_inc(stack_done, 1)

            def project_qkv_weights():
                dve.wait_ge(w_in, 96)
                nc.vector.tensor_reduce(w48[:, :, 0:QD], wq.rearrange("p k (d h) -> p k d h", h=NH0), AX_X,
                                        ALU.add).then_inc(w48_step, 1)
                nc.vector.tensor_reduce(b48[:, 0:QD], bq.rearrange("p (d h) -> p d h", h=NH0), AX_X,
                                        ALU.add).then_inc(w48_step, 1)
                dve.wait_ge(w48_step, 2)
                nc.vector.tensor_copy(w48_hi, w48).then_inc(w48_done, 1)
                dve.wait_ge(w48_done, 1)
                nc.vector.tensor_tensor(w48_lo, w48, w48_hi, ALU.subtract).then_inc(w48_done, 1)

            def qkv_bias(part):
                dve.wait_ge(qkv_done, part + 1)
                n = NT // 2
                nc.vector.tensor_tensor(qkv[:, part * n:(part + 1) * n, :],
                                        bank[QKV_BANK[part]][:, 0:n * 3 * QD].rearrange("p (t c) -> p t c", t=n),
                                        b48.unsqueeze(1).broadcast_to([P, n, 3 * QD]), ALU.add).then_inc(qkv_out, 1)

            def score_maxima():
                q, k = qkv[:, :, 0:QD], qkv[:, :, QD:2 * QD]
                dve.wait_ge(qkv_out, 2)
                nc.vector.tensor_reduce(kext[:, 0, :], k, AX_X, ALU.max).then_inc(att_step, 1)
                nc.vector.tensor_reduce(kext[:, 1, :], k, AX_X, ALU.min).then_inc(att_step, 1)
                dve.wait_ge(att_step, 2)
                for e in range(2):
                    nc.vector.tensor_tensor(sext[:, e], q, kext[:, e, :].unsqueeze(2).broadcast_to([P, NT, QD]),
                                            ALU.mult).then_inc(att_step, 1)
                dve.wait_ge(att_step, 4)
                nc.vector.tensor_tensor(smax[:], sext[:, 0], sext[:, 1], ALU.max).then_inc(att_step, 1)

            nc.vector.memset(B_stage[R3:P, 0:INT0P], 0.0).then_inc(B_zero, 1)
            nc.vector.memset(B_stage[0:RANK, INT0P:2 * INT0P], 0.0).then_inc(B_zero, 1)
            nc.vector.memset(stack[1][0:RANK, :], 0.0).then_inc(B_zero, 1)
            norm.dve_moments(dve, 0, loaded=x0_in)
            norm.dve_factors(dve, 0)
            for i in range(TPB):
                norm.dve_lo(dve, 0, i)
            dve.wait_ge(B_in, 16 * 6)
            dve.wait_ge(B_zero, 3)
            B = w0["B"]
            nc.vector.tensor_scalar(B[:, 0:2 * INT0P], B_stage, LRB, None, ALU.mult).then_inc(B_hi_done, 1)
            dve.wait_ge(B_hi_done, 1)
            for rows, cols in ((slice(RANK, 2 * RANK), slice(0, INT0P)), (slice(R3, P), slice(INT0P, 2 * INT0P))):
                nc.vector.scalar_tensor_tensor(B[rows, cols], B_stage[rows, cols], LRB, B[rows, cols], ALU.mult,
                                               ALU.subtract).then_inc(B_done, 1)

            def block_of_tokens(j):
                first = isinstance(j, int)
                stack_part(j, 0, XA)
                stack_part(j, 1, XA)
                for o in range(OT0 + 2):
                    n, stats_group, tiles = inserted(j, o)
                    if stats_group is not None:
                        if first:
                            dve.wait_ge(x_in[stats_group], 16)
                        else:
                            dve.wait_ge(att_added, TPB * j)
                        n.dve_moments(dve, stats_group, dve_turns)
                    before = inserted(j, o - 1)[1]
                    if before is not None:
                        n.dve_factors(dve, before)
                    for tile in tiles:
                        n.dve_lo(dve, *tile)
                    if first:
                        if o - 1 in QKV_AT:
                            qkv_bias(QKV_AT[o - 1])
                    if o < OT0:
                        wait(dve, gl_done, upto(j, o))
                        wait(dve, gs_done, upto(j, o))
                        nc.vector.scalar_tensor_tensor(g[:, o % 2, :], bank[GL][:], UNDO, g[:, o % 2, :],
                                                       ALU.mult, ALU.add).then_inc(g_done, 1)
                        wait(dve, ul_done, upto(j, o))
                        wait(dve, us_done, upto(j, o))
                        nc.vector.scalar_tensor_tensor(u[:, o % 2, :], bank[UL][:], UNDO, u[:, o % 2, :],
                                                       ALU.mult, ALU.add).then_inc(u_done, 1)
                    if o >= 2:
                        wait(dve, h_hi_done, upto(j, o - 2))
                        nc.vector.tensor_tensor(h_lo[:, o - 2, :], s[:, o % 2, :], h_hi[:, o - 2, :],
                                                ALU.subtract).then_inc(h_lo_done, 1)
                    if 1 <= o <= OT0:
                        wait(dve, s_done, upto(j, o - 1))
                        wait(dve, u_done, upto(j, o - 1))
                        b = (o - 1) % 2
                        nc.vector.tensor_tensor(s[:, b, :], s[:, b, :], u[:, b, :], ALU.mult).then_inc(h_done, 1)
                    if first and o == 6:
                        project_qkv_weights()
                if first:
                    score_maxima()
                stack_part(j, 2, HA)
                for i in range(TPB):
                    if i == 1:
                        wait(dve, exp_done, j + 1)
                        nc.vector.tensor_reduce(den[:, 0], prob[:], AX_X, ALU.add).then_inc(den_done, 1)
                    if i == 3:
                        wait(dve, pv_done, j + 1)
                        wait(dve, att_added, TPB * j)
                        nc.vector.tensor_reduce(att[:], prob[:], AX_X, ALU.add).then_inc(num_done, 1)
                        wait(dve, den_done, j + 1)
                        nc.vector.reciprocal(den[:, 1], den[:, 0]).then_inc(rden_done, 1)
                        wait(dve, num_done, j + 1)
                        wait(dve, rden_done, j + 1)
                        nc.vector.tensor_tensor(att[:], att[:], den[:, 1], ALU.mult).then_inc(att_done, 1)
                    x = x_sb[:, ds(j * TPB + i, 1), :].rearrange("p a d -> p (a d)")
                    n = TPB * j + i + 1
                    wait(dve, dm_done, n)
                    nc.vector.tensor_tensor(scaled[:, i % 2, :], bank[OUT_MAIN[i % 2]][:], w0["down_scale"][:],
                                            ALU.mult).then_inc(scaled_done, 1)
                    wait(dve, dl_done, n)
                    nc.vector.scalar_tensor_tensor(x, bank[OUT_LOW[i % 2]][:], UNDO, x, ALU.mult, ALU.add).then_inc(xl_done, 1)
                    wait(dve, xl_done, n)
                    wait(dve, scaled_done, n)
                    nc.vector.tensor_tensor(x, x, scaled[:, i % 2, :], ALU.add).then_inc(x_done, 1)

            block_of_tokens(0)
            with dve.Fori(1, NBLK) as j:
                block_of_tokens(j)

        @block.tensor
        def _(pe):
            def split_products(out, pairs):
                for n, (w, a) in enumerate(pairs):
                    mm = nc.tensor.matmul(out, w, a, start=(n == 0), stop=(n == len(pairs) - 1))
                return mm

            def project_qkv(part):
                if part == 0:
                    pe.wait_ge(w48_done, 2)
                    pe.wait_ge(norm.lo_done, NT)
                n = NT // 2
                for i in range(part * n, (part + 1) * n):
                    tok = slice(i * P, (i + 1) * P)
                    at = (i - part * n) * 3 * QD
                    mm = split_products(bank[QKV_BANK[part]][:, at:at + 3 * QD], [p for k in range(KT) for p in passes(
                        xnT_hi[:, k, tok], xnT_lo[:, k, tok], w48_hi[:, k, :], w48_lo[:, k, :])])
                mm.then_inc(qkv_done, 1)

            pe.wait_ge(id_done, 1)
            for i in range(TPB):
                norm.pe_turn(pe, 0, i)
            pe.wait_ge(norm.lo_done, TPB)

            def block_of_tokens(j):
                first = isinstance(j, int)
                tok = ds(j * BLK, BLK)
                xh = [xnT_hi[:, k, tok] for k in range(KT)]
                xl = [xnT_lo[:, k, tok] for k in range(KT)]
                Ah, Al = w0["A_hi"], w0["A_lo"]
                if first:
                    pe.wait_ge(chunk_done, A_READY)
                wait(pe, scaled_done, TPB * j)
                split_products(bank[XA][:], [p for k in range(KT) for p in passes(
                    Ah[:, k * P:(k + 1) * P], Al[:, k * P:(k + 1) * P], xh[k], xl[k])]).then_inc(xa_done, 1)
                for o in range(OT0):
                    rows = slice(o * P, (o + 1) * P)
                    if o < 2:
                        wait(pe, x_done, TPB * j)
                    if first and o % 2 == 0:
                        pe.wait_ge(chunk_done, GATE_READY[o // 2])
                    wait(pe, gs_done, upto(j, o - 2))
                    split_products(bank[o % 2][:], [(w0["gate"][:, k, rows], a) for k in range(KT)
                                                    for a in (xh[k], xl[k])]).then_inc(gm_done, 1)
                    n, _, tiles = inserted(j, o)
                    if first and o % 2 == 0:
                        pe.wait_ge(chunk_done, UP_READY[o // 2])
                    wait(pe, us_done, upto(j, o - 2))
                    split_products(bank[2 + o % 2][:], [(w0["up"][:, k, rows], a) for k in range(KT)
                                                        for a in (xh[k], xl[k])]).then_inc(um_done, 1)
                    if tiles:
                        n.pe_turn(pe, *tiles[0])
                    if first and o in QKV_AT:
                        project_qkv(QKV_AT[o])
                    if first and o == 0:
                        pe.wait_ge(B_done, 2)
                    if o == 0:
                        wait(pe, stack_done, 3 * j + 2)
                    wait(pe, g_done, upto(j, o - 1))
                    nc.tensor.matmul(bank[GL][:], w0["B"][0:R3, rows], stack[0][:], start=True, stop=True).then_inc(gl_done, 1)
                    wait(pe, u_done, upto(j, o - 1))
                    nc.tensor.matmul(bank[UL][:], w0["B"][:, INT0P + o * P:INT0P + (o + 1) * P], stack[1][:],
                                     start=True, stop=True).then_inc(ul_done, 1)
                    if tiles:
                        n.pe_turn(pe, *tiles[1])
                if first:
                    pe.wait_ge(chunk_done, DOWN_READY)
                    pe.wait_ge(qkv_out, 2)
                for o in range(OT0):
                    wait(pe, h_lo_done, upto(j, o))
                    A = slice(GU_COLS + o * R3, GU_COLS + (o + 1) * R3)
                    for n, (w, a) in enumerate(passes(Ah[:, A], Al[:, A], h_hi[:, o, :], h_lo[:, o, :])):
                        mm = nc.tensor.matmul(bank[HA][0:R3, :], w, a, start=(o == 0 and n == 0),
                                              stop=(o == OT0 - 1 and n == 2))
                mm.then_inc(xa_done, 1)
                for i in range(TPB):
                    ts = slice(i * P, (i + 1) * P)
                    if i < 2:
                        wait(pe, gs_done, upto(j, OT0 - 1))
                    else:
                        wait(pe, scaled_done, TPB * j + i - 1)
                    split_products(bank[OUT_MAIN[i % 2]][:], [(a[:, o, ts], w0["down"][:, o, :]) for o in range(OT0)
                                                              for a in (h_hi, h_lo)]).then_inc(dm_done, 1)
                    wait(pe, stack_done, 3 * j + 3)
                    if i >= 2:
                        wait(pe, xl_done, TPB * j + i - 1)
                    nc.tensor.matmul(bank[OUT_LOW[i % 2]][:], stack[2][:, ts], w0["B"][0:R3, 2 * INT0P:],
                                     start=True, stop=True).then_inc(dl_done, 1)

            block_of_tokens(0)
            with pe.Fori(1, NBLK) as j:
                block_of_tokens(j)

Q, K, V, G, OW = range(5)


class HeadWeights:

    def __init__(self, nc, t, sem, sb):
        self.nc, self.t = nc, t
        self.stage = sb("w_stage", [P, 5, D + 1])
        self.hi, self.lo = sb("w_hi", [P, 5, D], F16), sb("w_lo", [P, 5, D], BF16)
        self.ident_hi, self.ident_lo = sb("ident_hi", [P, P], F16), sb("ident_lo", [P, P], BF16)
        self.loaded, self.done = [sem(f"w_in{m}") for m in range(5)], [sem(f"w_split{m}") for m in range(5)]
        self.step, self.ident_done = sem("w_step"), sem("ident_done")

    def load(self, sp, m, h):
        if m == OW:
            sp.dma_start(self.stage[:, OW, :], self.t["out_w"][h]).then_inc(self.loaded[m], 16)
        else:
            sp.dma_start(self.stage[:, m, 0:D].rearrange("p (k d) -> p k d", k=KT),
                         self.t["proj_w"][h, :, m]).then_inc(self.loaded[m], 16)

    def split(self, pool, m, step, turns):
        nc, src = self.nc, self.stage[:, m, 0:D]
        nc.gpsimd.tensor_scalar(self.hi[:, m, :], src, 1.0, 0.0, ALU.mult, ALU.add).then_inc(self.step, 1)
        hold(pool, self.step, step, turns)
        nc.gpsimd.tensor_tensor(self.lo[:, m, :], src, self.hi[:, m, :], ALU.subtract).then_inc(self.done[m], 1)

    def split_proj(self, pool, m, h, step, turns):
        hold(pool, self.loaded[m], 16 * (h + 1), turns)
        self.split(pool, m, step, turns)

    def split_out(self, pool, h, step, turns):
        hold(pool, self.loaded[OW], 16 * (h + 1), turns)
        w = self.stage[:, OW, :]
        self.nc.gpsimd.tensor_scalar(w[:, 0:D], w[:, 0:D], w[:, D:D + 1], 0.5, ALU.mult, ALU.mult).then_inc(self.step, 1)
        hold(pool, self.step, step - 1, turns)
        self.split(pool, OW, step, turns)


def phase_norm1_ffn1(nc, t, sem, sb, bank, x_sb, xnT_hi, xnT_lo, ident, w1, y_place, hw, norm):
    place = Place(y_place[:].rearrange("p t d -> p (t d)"))
    norm.xn, norm.bank = place([P, 2, D]), [bank[7], bank[2]]
    route_f = sb("route_f", [P, KT, NE])
    route_hi, route_lo = sb("route_hi", [P, KT, NE], F16), sb("route_lo", [P, KT, NE], BF16)
    gamma, beta = place([P, D]), place([P, D])
    relu, sq = place([P, 2, BLK]), place([P, 2, BLK])
    h_hi, h_lo = sb("h1_hi", [P, OT1, BLK], F16), sb("h1_lo", [P, OT1, BLK], BF16)
    lat_hi, lat_lo = sb("lat_hi", [P, LT1, BLK], F16), sb("lat_lo", [P, LT1, BLK], BF16)
    exp_hi, exp_lo = sb("exp_hi", [P, LT1, BLK], F16), sb("exp_lo", [P, LT1, BLK], BF16)
    top, rw = sb("top8", [P, TPB, 8]), sb("rw", [P, TPB])
    routed, y = place([P, 2, D]), place([P, TPB, D])
    stats, mv, small = place([P, TPB, 6]), place([P, TPB, 2]), place([P, 7, TPB])

    in1, route_split = sem("ffn1_in"), sem("route_split")
    beta_done = sem("beta_added")
    lat_mm, lat_hi_done, lat_lo_done = sem("lat_mm"), sem("lat_hi_done"), sem("lat_lo_done")
    exp_mm, exp_hi_done, exp_lo_done = sem("exp_mm"), sem("exp_hi_done"), sem("exp_lo_done")
    route_mm, top_done, rw_done = sem("route_mm"), sem("top_done"), sem("rw_done")
    up_mm, relu_done, sq_done, h_hi_done, h_lo_done = (sem("up1_mm"), sem("relu_done"), sem("sq_done"),
                                                       sem("h1_hi_done"), sem("h1_lo_done"))
    fc2_mm, down_mm, routed_done, y_done = sem("fc2_mm"), sem("down1_mm"), sem("routed_done"), sem("y_done")
    ystep, yvar, ysd, yn_done, yg_done, x1_done = (sem("y_norm_step"), sem("y_var"), sem("y_sd"), sem("yn_done"),
                                                   sem("y_gamma"), sem("x1_done"))
    pool_turns, dve_turns = sem("pool_turns"), sem("dve_turns")
    LAT_BANK, EXP_BANK, FC2_BANK, DOWN_BANK, ROUTE_BANK = (3, 4), (5, 6), (3, 4), (5, 6), 2
    LAST = NBLK - 1
    TILES_AT = {o: (o - 1,) for o in range(1, 1 + TPB)}
    YSTEPS = 2 * TPB + 6

    def act_tail(act, j):
        wait(act, yvar, j + 1)
        nc.scalar.activation(small[:, 1, :], small[:, 0, :], ACT.Sqrt).then_inc(ysd, 1)
        wait(act, ystep, YSTEPS * (j + 1))
        for i in range(TPB):
            nc.scalar.activation(y[:, i, :], y[:, i, :], ACT.Identity, scale=small[:, 5, i:i + 1],
                                 bias=small[:, 6, i:i + 1]).then_inc(yn_done, 1)

    def dve_tail(dve, j):
        c = YSTEPS * j
        hold(dve, ystep, c + TPB, dve_turns)
        for i in range(TPB):
            nc.vector.bn_aggr(mv[:, i, :], stats[:, i, :]).then_inc(ystep, 1)
        variance(nc, dve, ystep, c + 2 * TPB, small, mv, TPB, yvar)
        norm_factors(nc, dve, ystep, c + 2 * TPB, small, mv, TPB, ysd, j + 1)
        for i in range(TPB):
            n = TPB * j + i + 1
            x = x_sb[:, ds(j * TPB + i, 1), :].rearrange("p a d -> p (a d)")
            wait(dve, yn_done, n)
            nc.vector.tensor_tensor(y[:, i, :], y[:, i, :], gamma, ALU.mult).then_inc(yg_done, 1)
            wait(dve, yg_done, n)
            wait(dve, beta_done, n)
            nc.vector.tensor_tensor(x, x, y[:, i, :], ALU.add).then_inc(x1_done, 1)
        if isinstance(j, int):
            dve.wait_ge(x1_done, TPB * (j + 1))

    def w1_tile(offset, k, width, at, n=P):
        a = offset + k * width + at
        return w1["hi"][:, a:a + n], w1["lo"][:, a:a + n]

    with nc.Block() as block:
        @block.sync
        def _(sp):
            sp.dma_start(route_f[:], t["route_w"]).then_inc(in1, 16)
            sp.dma_start(gamma, t["gamma"].partition_broadcast(P)).then_inc(in1, 16)
            sp.dma_start(beta, t["beta"].partition_broadcast(P)).then_inc(in1, 16)
            for m in (Q, K, V, G, OW):
                hw.load(sp, m, 0)

        @block.gpsimd
        def _(pool):
            hold(pool, in1, 48, pool_turns)
            nc.gpsimd.tensor_copy(route_hi[:], route_f[:]).then_inc(route_split, 1)
            hold(pool, route_split, 1, pool_turns)
            nc.gpsimd.tensor_tensor(route_lo[:], route_f[:], route_hi[:], ALU.subtract).then_inc(route_split, 1)

            def block_of_tokens(j):
                for o in range(OT1):
                    hold(pool, sq_done, OT1 * j + o + 1, pool_turns)
                    hold(pool, down_mm, TPB * j, pool_turns)
                    nc.gpsimd.tensor_scalar(h_hi[:, o, :], sq[:, o % 2, :], 1.0, 0.0, ALU.mult, ALU.add).then_inc(h_hi_done, 1)
                if isinstance(j, int):
                    pool.wait_ge(norm.xn_done, NT)
                for i in range(TPB):
                    x = x_sb[:, ds(j * TPB + i, 1), :].rearrange("p a d -> p (a d)")
                    nc.gpsimd.tensor_tensor(x, x, beta, ALU.add).then_inc(beta_done, 1)

            block_of_tokens(0)
            nc.gpsimd.tensor_copy(hw.ident_hi[:], ident[:]).then_inc(hw.ident_done, 1)
            nc.gpsimd.tensor_copy(hw.ident_lo[:], ident[:]).then_inc(hw.ident_done, 1)
            for m in (Q, K, V, G):
                hw.split_proj(pool, m, 0, m + 1, pool_turns)
            with pool.Fori(1, NBLK) as j:
                block_of_tokens(j)

        @block.scalar
        def _(act):
            norm.act_sqrt(act, LAST)

            def up_part(j, os):
                for o in os:
                    tiles = TILES_AT.get(o, ()) if isinstance(j, int) else ()
                    for i in tiles:
                        norm.act_rows(act, LAST, i)
                    for i in tiles:
                        norm.act_hi(act, LAST, i)
                    wait(act, relu_done, OT1 * j + o + 1)
                    wait(act, h_lo_done, OT1 * j + max(o - 1, 0))
                    nc.scalar.activation(sq[:, o % 2, :], relu[:, o % 2, :], ACT.Square).then_inc(sq_done, 1)

            def hi_part(j, dst, mm, banks, done, readers, per):
                for l in range(LT1):
                    wait(act, mm, LT1 * j + l + 1)
                    wait(act, readers, per * j)
                    nc.scalar.activation(dst[:, l, :], bank[banks[l]][:], ACT.Copy).then_inc(done, 1)

            def block_of_tokens(j):
                hi_part(j, lat_hi, lat_mm, LAT_BANK, lat_hi_done, exp_mm, LT1)
                up_part(j, range(OT1 // 2))
                hi_part(j, exp_hi, exp_mm, EXP_BANK, exp_hi_done, fc2_mm, TPB)
                up_part(j, range(OT1 // 2, OT1))
                for i in range(TPB):
                    n = TPB * j + i + 1
                    wait(act, fc2_mm, n)
                    wait(act, rw_done, j + 1)
                    wait(act, y_done, TPB * j + max(i - 1, 0))
                    nc.scalar.activation(routed[:, i % 2, :], bank[FC2_BANK[i % 2]][:], ACT.Copy,
                                         scale=rw[:, i:i + 1]).then_inc(routed_done, 1)

            block_of_tokens(0)
            with act.Fori(1, NBLK) as j:
                act_tail(act, j - 1)
                block_of_tokens(j)

        @block.vector
        def _(dve):
            norm.dve_moments(dve, LAST)
            norm.dve_factors(dve, LAST)

            def lo_part(j, hi, lo, banks, hi_done, done):
                for l in range(LT1):
                    wait(dve, hi_done, LT1 * j + l + 1)
                    nc.vector.tensor_tensor(lo[:, l, :], bank[banks[l]][:], hi[:, l, :], ALU.subtract).then_inc(done, 1)

            def up_part(j, os):
                for o in os:
                    if isinstance(j, int):
                        for i in TILES_AT.get(o, ()):
                            norm.dve_lo(dve, LAST, i)
                    if o < OT1:
                        wait(dve, up_mm, OT1 * j + o + 1)
                        wait(dve, sq_done, OT1 * j + max(o - 1, 0))
                        nc.vector.tensor_scalar(relu[:, o % 2, :], bank[o % 2][:], 0.0, SQ_DOWN, ALU.max,
                                                ALU.mult).then_inc(relu_done, 1)
                    if o >= 1:
                        wait(dve, h_hi_done, OT1 * j + o)
                        nc.vector.tensor_tensor(h_lo[:, o - 1, :], sq[:, (o - 1) % 2, :], h_hi[:, o - 1, :],
                                                ALU.subtract).then_inc(h_lo_done, 1)

            def block_of_tokens(j):
                lo_part(j, lat_hi, lat_lo, LAT_BANK, lat_hi_done, lat_lo_done)
                hold(dve, route_mm, j + 1, dve_turns)
                hold(dve, routed_done, TPB * j, dve_turns)
                for i in range(TPB):
                    nc.vector.max(top[:, i, :], bank[ROUTE_BANK][:, i * NE:(i + 1) * NE]).then_inc(top_done, 1)
                wait(dve, top_done, TPB * (j + 1))
                nc.vector.tensor_tensor(rw[:], top[:, :, 0], top[:, :, 1], ALU.add).then_inc(rw_done, 1)
                up_part(j, range(OT1 // 2))
                lo_part(j, exp_hi, exp_lo, EXP_BANK, exp_hi_done, exp_lo_done)
                up_part(j, range(OT1 // 2, OT1 + 1))
                for i in range(TPB):
                    n = TPB * j + i + 1
                    wait(dve, down_mm, n)
                    wait(dve, routed_done, n)
                    wait(dve, x1_done, TPB * j)
                    nc.vector.scalar_tensor_tensor(y[:, i, :], bank[DOWN_BANK[i % 2]][:], 1.0 / SQ_DOWN ** 2,
                                                   routed[:, i % 2, :], ALU.mult, ALU.add).then_inc(y_done, 1)
                    wait(dve, y_done, n)
                    nc.vector.bn_stats(stats[:, i, :], y[:, i, :]).then_inc(ystep, 1)

            block_of_tokens(0)
            with dve.Fori(1, NBLK) as j:
                dve_tail(dve, j - 1)
                block_of_tokens(j)

        @block.tensor
        def _(pe):

            def products(out, pairs):
                for n, (w, a) in enumerate(pairs):
                    mm = nc.tensor.matmul(out, w, a, start=(n == 0), stop=(n == len(pairs) - 1))
                return mm

            def block_of_tokens(j):
                tok = ds(j * BLK, BLK)
                xh = [xnT_hi[:, k, tok] for k in range(KT)]
                xl = [xnT_lo[:, k, tok] for k in range(KT)]

                def up_part(os):
                    for o in os:
                        tiles = TILES_AT.get(o, ()) if isinstance(j, int) else ()
                        wait(pe, relu_done, OT1 * j + max(o - 1, 0))
                        products(bank[o % 2][:], [p for k in range(KT) for p in passes(
                            *w1_tile(W1_UP, k, INT1, o * P), xh[k], xl[k])]).then_inc(up_mm, 1)
                        for i in tiles:
                            pe.wait_ge(rw_done, 1)
                            norm.pe_turn(pe, LAST, i)

                for l in range(LT1):
                    wait(pe, routed_done, TPB * j)
                    products(bank[LAT_BANK[l]][:], [p for k in range(KT) for p in passes(
                        *w1_tile(W1_FC1, k, LAT, l * P), xh[k], xl[k])]).then_inc(lat_mm, 1)
                if isinstance(j, int):
                    pe.wait_ge(route_split, 2)
                wait(pe, rw_done, j)
                for i in range(TPB):
                    ts = ds(j * BLK + i * P, P)
                    mm = products(bank[ROUTE_BANK][:, i * NE:(i + 1) * NE], [p for k in range(KT) for p in passes(
                        xnT_hi[:, k, ts], xnT_lo[:, k, ts], route_hi[:, k, :], route_lo[:, k, :])])
                mm.then_inc(route_mm, 1)
                up_part(range(OT1 // 2))
                wait(pe, lat_lo_done, LT1 * (j + 1))
                wait(pe, y_done, TPB * j)
                for m in range(LT1):
                    products(bank[EXP_BANK[m]][:], [p for l in range(LT1) for p in passes(
                        *w1_tile(W1_EXP, l, LAT, m * P), lat_hi[:, l, :], lat_lo[:, l, :])]).then_inc(exp_mm, 1)
                up_part(range(OT1 // 2, OT1))
                wait(pe, exp_lo_done, LT1 * (j + 1))

                def fc2(i):
                    ts = slice(i * P, (i + 1) * P)
                    wait(pe, routed_done, TPB * j + max(i - 1, 0))
                    products(bank[FC2_BANK[i % 2]][:], [p for l in range(LT1) for p in passes(
                        exp_hi[:, l, ts], exp_lo[:, l, ts], *w1_tile(W1_FC2, l, D, 0, D))]).then_inc(fc2_mm, 1)

                def down(i):
                    ts = slice(i * P, (i + 1) * P)
                    if i == 0:
                        wait(pe, h_lo_done, OT1 * (j + 1))
                    wait(pe, y_done, TPB * j + max(i - 1, 0))
                    products(bank[DOWN_BANK[i % 2]][:], [p for o in range(OT1) for p in passes(
                        h_hi[:, o, ts], h_lo[:, o, ts], *w1_tile(W1_DOWN, o, D, 0, D))]).then_inc(down_mm, 1)

                fc2(0)
                for i in range(TPB):
                    if i + 1 < TPB:
                        fc2(i + 1)
                    down(i)

            block_of_tokens(0)
            with pe.Fori(1, NBLK) as j:
                block_of_tokens(j)

    return act_tail, dve_tail


def phase_attn1(nc, t, sem, sb, bank, x_sb, xnT_hi, xnT_lo, region, y, hw, ffn1_tail):
    NSLOT = 8
    NIT = 2 * HEADS
    NST = 2 * CPH - 1
    place = Place(region)
    (q_hi, q_lo), (qd_hi, qd_lo), (k_hi, k_lo), (v_hi, v_lo) = ((place([P, 2, SEQ], F16), place([P, 2, SEQ], BF16))
                                                                for _ in range(4))
    k_f, v_f = place([P, SEQ]), place([P, SEQ])
    gate = sb("gate1", [P, 2, SEQ])
    kT_hi, kT_lo = sb("kT_hi", [P, SEQ], F16), sb("kT_lo", [P, SEQ], BF16)
    vd_hi, vd_lo = sb("vd_hi", [P, SEQ], F16), sb("vd_lo", [P, SEQ], BF16)
    p_hi, p_lo = sb("p_hi", [P, SEQ], F16), sb("p_lo", [P, SEQ], BF16)
    st_f = sb("st_f", [P, NST + 1, HD])
    st_hi, st_lo = sb("st_hi", [P, NST + 1, HD], F16), sb("st_lo", [P, NST + 1, HD], BF16)
    sq = sb("sq", [P, SEQ])
    g_hi, g_lo = sb("g_hi", [P, SEQ], F16), sb("g_lo", [P, SEQ], BF16)
    ssum = sb("ssum", [P, TOK])
    decay = sb("decay", [P, CH + 2])
    q_decay = sb("q_decay", [P, CH])
    ones = sb("ones", [P, 1])
    small, mv = sb("small2", [P, 7, NT]), sb("mv2", [P, NT, 2])
    KT_BANK, SC_BANK, U_BANK, O_BANK, C_BANK, SS_BANK = (2, 4), 3, 4, (5, 7), (6, 7), 2

    w_hi, w_lo, w_done = hw.hi, hw.lo, hw.done
    act_tail, dve_tail = ffn1_tail
    qd_in, decay_in = sem("q_decay_in"), sem("decay_in")
    proj_done, act_done = sem("proj_done"), sem("proj_act_done")
    q_hi_done, q_lo_done, qd_done, qd_hi_done, qd_lo_done = (sem("q_hi_done"), sem("q_lo_done"), sem("qd_done"),
                                                             sem("qd_hi_done"), sem("qd_lo_done"))
    kv_hi_done, kv_lo_done = sem("kv_hi_done"), sem("kv_lo_done")
    kT_done, kT_hi_done, kT_lo_done = sem("kT_done"), sem("kT_hi_done"), sem("kT_lo_done")
    vd_done, vd_hi_done, vd_lo_done = sem("vd_done"), sem("vd_hi_done"), sem("vd_lo_done")
    sc_done, pm_done, p_hi_done, p_lo_done = sem("sc_done"), sem("pm_done"), sem("p_hi_done"), sem("p_lo_done")
    upd_done, st_done, st_hi_done, st_lo_done = sem("upd_done"), sem("st_done"), sem("st_hi_done"), sem("st_lo_done")
    o_done, sq_done, g_done, g_hi_done, g_lo_done = (sem("o_done"), sem("sq_done"), sem("g_done"), sem("g_hi_done"),
                                                     sem("g_lo_done"))
    ss_zero, ss_done, c_done, y_done = sem("ss_zero"), sem("ss_done"), sem("c_done"), sem("y_done")
    ones_done, ss_mm, rms_step, rms_var, rms_sd = (sem("ones_done"), sem("ss_mm"), sem("rms_step"), sem("rms_var"),
                                                   sem("rms_sd"))
    out_ready, out_written, pool_turns = sem("out_ready"), sem("out_written"), sem("pool_turns")
    sp_turns = sem("sp_turns")
    out_ready = [out_ready, sem("out_ready_b1")]
    NTB = NT // BATCH
    RMS_STEPS = 8
    y_scaled = sem("y_scaled")

    def rms(b):
        cols = slice(b * NTB, (b + 1) * NTB)
        return small[:, :, cols], mv[:, cols, :]

    Y0 = 2

    def half(b):
        return slice(b * BLK, (b + 1) * BLK)

    def chunks4(ap):
        return ap.rearrange("p (c n) -> p c n", c=CPH)

    with nc.Block() as block:
        @block.sync
        def _(sp):
            def load_q_decay(h):
                sp.dma_start(q_decay[:], t["q_decay"][h].partition_broadcast(P)).then_inc(qd_in, 16)

            def load_decay(h):
                sp.dma_start(decay[:], t["decay"][h]).then_inc(decay_in, 16)

            load_q_decay(0)
            load_decay(0)
            with sp.Fori(1, HEADS) as h:
                for m in (Q, K, V, G):
                    hold(sp, w_done[m], h, sp_turns)
                    hw.load(sp, m, h)
                hold(sp, qd_done, 4 * h, sp_turns)
                load_q_decay(h)
                hold(sp, w_done[OW], h, sp_turns)
                hw.load(sp, OW, h)
                hold(sp, pm_done, 4 * h, sp_turns)
                hold(sp, vd_done, 4 * h, sp_turns)
                hold(sp, st_done, 2 * NST * h, sp_turns)
                load_decay(h)
            out = t["out"].rearrange("(t p) d -> p t d", p=P)
            parts = ((0, 0, 4), (1, 0, 2), (1, 2, 2), (1, 4, 2), (0, 4, 4), (1, 6, 2))
            for b, n, count in parts:
                sp.wait_ge(out_ready[b], n + count)
                tiles = slice(b * NTB + n, b * NTB + n + count)
                sp.dma_start(out[:, tiles, :], x_sb[:, tiles, :]).then_inc(out_written, 16)
            sp.wait_ge(out_written, 16 * len(parts))

        @block.gpsimd
        def _(pool):
            def split(dst_hi, dst_lo, src, hi_done, hi_want, lo_done):
                nc.gpsimd.tensor_scalar(dst_hi, src, 1.0, 0.0, ALU.mult, ALU.add).then_inc(hi_done, 1)
                hold(pool, hi_done, hi_want, pool_turns)
                nc.gpsimd.tensor_tensor(dst_lo, src, dst_hi, ALU.subtract).then_inc(lo_done, 1)

            def split_kv(i, b, n):
                src, hi, lo = ((k_f, k_hi, k_lo), (v_f, v_hi, v_lo))[n // 2]
                hold(pool, act_done, NSLOT * i + 3 + n, pool_turns)
                split(hi[:, b, half(n % 2)], lo[:, b, half(n % 2)], src[:, half(n % 2)], kv_hi_done, 4 * i + n + 1,
                      kv_lo_done)

            def split_decayed(i):
                for n in range(2):
                    hold(pool, vd_done, 2 * (i - 1) + n + 1, pool_turns)
                    split(vd_hi[:, half(n)], vd_lo[:, half(n)], v_f[:, half(n)], vd_hi_done, 2 * (i - 1) + n + 1, vd_lo_done)

            def squares(i, b):
                for n in range(2):
                    cols = slice((1 - b) * SEQ + n * BLK, (1 - b) * SEQ + (n + 1) * BLK)
                    hold(pool, sq_done, 2 * (i - 1) + n + 1, pool_turns)
                    nc.gpsimd.tensor_tensor(ssum[:, cols], ssum[:, cols], sq[:, half(n)], ALU.add).then_inc(ss_done, 1)

            nc.gpsimd.memset(ssum[:], 0.0).then_inc(ss_zero, 1)
            nc.gpsimd.memset(ones[:], 1.0).then_inc(ones_done, 1)
            for n in range(4):
                split_kv(0, 0, n)
            pool.wait_ge(ss_zero, 1)
            with pool.Fori(1, HEADS) as h:
                i, step = 2 * h - 1, 4 + 6 * (h - 1)
                split_decayed(i)
                split_kv(i, 1, 0)
                hold(pool, proj_done, NSLOT * i + 2, pool_turns)
                hw.split_proj(pool, Q, h, step + 1, pool_turns)
                split_kv(i, 1, 1)
                split_kv(i, 1, 2)
                hold(pool, proj_done, NSLOT * i + 4, pool_turns)
                hw.split_proj(pool, K, h, step + 2, pool_turns)
                split_kv(i, 1, 3)
                hold(pool, y_done, Y0 + 2 * NSLOT * (h - 1), pool_turns)
                hw.split_out(pool, h - 1, step + 4, pool_turns)
                hold(pool, proj_done, NSLOT * i + 6, pool_turns)
                hw.split_proj(pool, V, h, step + 5, pool_turns)
                squares(i, 1)
                split_decayed(i + 1)
                hold(pool, proj_done, NSLOT * (i + 1), pool_turns)
                hw.split_proj(pool, G, h, step + 6, pool_turns)
                for n in range(4):
                    split_kv(i + 1, 0, n)
                squares(i + 1, 0)
            i = NIT - 1
            split_decayed(i)
            for n in range(4):
                split_kv(i, 1, n)
            pool.wait_ge(y_done, Y0 + 2 * NSLOT * (HEADS - 1))
            hw.split_out(pool, HEADS - 1, 4 + 6 * (HEADS - 1) + 2, pool_turns)
            squares(i, 1)
            split_decayed(i + 1)
            squares(i + 1, 0)
            for n in range(NTB):
                pool.wait_ge(y_scaled, n + 1)
                nc.gpsimd.tensor_tensor(x_sb[:, n, :], x_sb[:, n, :], y[:, n, :], ALU.add).then_inc(out_ready[0], 1)

        @block.scalar
        def _(act):
            def projection(i, b, s):
                act.wait_ge(proj_done, NSLOT * i + s + 1)
                src, n = bank[s % 2][:], s % 2
                if s // 2 == Q:
                    nc.scalar.activation(src, src, ACT.Silu).then_inc(act_done, 1)
                    act.wait_ge(act_done, NSLOT * i + s + 1)
                    nc.scalar.activation(q_hi[:, b, half(n)], src, ACT.Copy).then_inc(q_hi_done, 1)
                elif s // 2 == G:
                    nc.scalar.activation(gate[:, b, half(n)], src, ACT.Tanh, scale=0.5).then_inc(act_done, 1)
                else:
                    if s // 2 == K:
                        wait(act, kv_lo_done, 4 * (i - 1) + s - 1)
                    else:
                        wait(act, vd_lo_done, 2 * (i - 1) + n + 1)
                    dst = (k_f if s // 2 == K else v_f)[:, half(n)]
                    nc.scalar.activation(dst, src, ACT.Silu).then_inc(act_done, 1)

            def hi_part(i, s, decay_want):
                a = i - 1
                n = {0: 0, 1: 1, 2: 0, 3: 0, 4: 1, 5: 1, 6: 0, 7: 1}[s]
                if s < 2:
                    act.wait_ge(kv_lo_done, 4 * a + 3 + n)
                    if n == 0:
                        act.wait_ge(decay_in, decay_want)
                    nc.scalar.activation(v_f[:, half(n)], v_f[:, half(n)], ACT.Copy,
                                         scale=decay[:, CH:CH + 1]).then_inc(vd_done, 1)
                    act.wait_ge(kT_done, 2 * a + n + 1)
                    nc.scalar.activation(kT_hi[:, half(n)], bank[KT_BANK[n]][:, 0:BLK // 2].bitcast(F16),
                                         ACT.Copy).then_inc(kT_hi_done, 1)
                elif s in (2, 4):
                    act.wait_ge(pm_done, 2 * a + n + 1)
                    nc.scalar.activation(p_hi[:, half(n)], bank[SC_BANK][:], ACT.Copy).then_inc(p_hi_done, 1)
                elif s in (3, 5):
                    c = slice(1, CPH + 1) if n == 0 else slice(CPH + 1, NST + 1)
                    act.wait_ge(st_done, NST * a + (CPH if n == 0 else NST))
                    nc.scalar.activation(st_hi[:, c, :], st_f[:, c, :], ACT.Copy).then_inc(st_hi_done, 1)
                else:
                    act.wait_ge(o_done, 2 * a + n + 1)
                    wait(act, ss_done, 2 * (a - 1) + n + 1)
                    nc.scalar.activation(sq[:, half(n)], bank[O_BANK[n]][:], ACT.Square).then_inc(sq_done, 1)
                    act.wait_ge(g_done, 2 * a + n + 1)
                    nc.scalar.activation(g_hi[:, half(n)], bank[O_BANK[n]][:], ACT.Copy).then_inc(g_hi_done, 1)

            def scaled_queries(i, b, n):
                act.wait_ge(qd_done, 2 * i + n + 1)
                nc.scalar.activation(qd_hi[:, b, half(n)], bank[n][:], ACT.Copy).then_inc(qd_hi_done, 1)

            def iteration(i, b, project, attend, decay_want=None):
                for s in range(NSLOT):
                    if project:
                        projection(i, b, s)
                    if attend:
                        hi_part(i, s, decay_want)
                    if project and s < 2:
                        scaled_queries(i, b, s)
                    if not attend and s == 3:
                        act_tail(act, NBLK - 1)

            iteration(0, 0, True, False)
            iteration(1, 1, True, True, 16)
            with act.Fori(1, HEADS) as h:
                iteration(2 * h, 0, True, True, 16 * h)
                iteration(2 * h + 1, 1, True, True, 16 * (h + 1))
            iteration(NIT, 0, False, True, 16 * HEADS)

            def rms_sqrt(b):
                act.wait_ge(rms_var, b + 1)
                sm = rms(b)[0]
                nc.scalar.activation(sm[:, 1, :], sm[:, 0, :], ACT.Sqrt).then_inc(rms_sd, 1)

            rms_sqrt(0)
            act.wait_ge(rms_step, RMS_STEPS)
            for n in range(NTB):
                if n == NTB // 2:
                    rms_sqrt(1)
                act.wait_ge(y_done, Y0 + NSLOT * (NIT - 2) + n + 1)
                nc.scalar.activation(y[:, n, :], y[:, n, :], ACT.Copy, scale=small[:, 5, n:n + 1]).then_inc(y_scaled, 1)

        @block.vector
        def _(dve):
            def queries(i, b, n, want):
                dve.wait_ge(q_hi_done, 2 * i + n + 1)
                nc.vector.tensor_tensor(q_lo[:, b, half(n)], bank[n][:], q_hi[:, b, half(n)],
                                        ALU.subtract).then_inc(q_lo_done, 1)
                if n == 0:
                    dve.wait_ge(qd_in, want)
                dve.wait_ge(q_lo_done, 2 * i + n + 1)
                nc.vector.tensor_tensor(chunks4(bank[n][:]), chunks4(bank[n][:]),
                                        q_decay[:].unsqueeze(1).broadcast_to([P, CPH, CH]), ALU.mult).then_inc(qd_done, 1)

            def scaled_queries_lo(i, b, n):
                dve.wait_ge(qd_hi_done, 2 * i + n + 1)
                nc.vector.tensor_tensor(qd_lo[:, b, half(n)], bank[n][:], qd_hi[:, b, half(n)],
                                        ALU.subtract).then_inc(qd_lo_done, 1)

            def keys_lo(a, n):
                dve.wait_ge(kT_hi_done, 2 * a + n + 1)
                nc.vector.tensor_copy(kT_lo[:, half(n)], bank[KT_BANK[n]][:, BLK // 2:].bitcast(BF16)).then_inc(kT_lo_done, 1)

            def mask_scores(a, n):
                dve.wait_ge(sc_done, 2 * a + n + 1)
                dve.wait_ge(vd_done, 2 * a + n + 1)
                nc.vector.tensor_tensor(chunks4(bank[SC_BANK][:]), chunks4(bank[SC_BANK][:]),
                                        decay[:, 0:CH].unsqueeze(1).broadcast_to([P, CPH, CH]), ALU.mult).then_inc(pm_done, 1)

            def scores_lo(a, n):
                dve.wait_ge(p_hi_done, 2 * a + n + 1)
                nc.vector.tensor_tensor(p_lo[:, half(n)], bank[SC_BANK][:], p_hi[:, half(n)],
                                        ALU.subtract).then_inc(p_lo_done, 1)

            def states(a, n):
                dve.wait_ge(upd_done, 2 * a + n + 1)
                wait(dve, st_hi_done, 2 * a)
                for c in (range(CPH) if n == 0 else range(CPH, NST)):
                    u = bank[U_BANK][:, (c % CPH) * HD:(c % CPH + 1) * HD]
                    if c == 0:
                        nc.vector.tensor_copy(st_f[:, 1, :], u).then_inc(st_done, 1)
                    else:
                        dve.wait_ge(st_done, NST * a + c)
                        nc.vector.scalar_tensor_tensor(st_f[:, c + 1, :], st_f[:, c, :], decay[:, CH + 1:CH + 2], u,
                                                       ALU.mult, ALU.add).then_inc(st_done, 1)

            def states_lo(a, n):
                c = slice(1, CPH + 1) if n == 0 else slice(CPH + 1, NST + 1)
                dve.wait_ge(st_hi_done, 2 * a + n + 1)
                nc.vector.tensor_tensor(st_lo[:, c, :], st_f[:, c, :], st_hi[:, c, :], ALU.subtract).then_inc(st_lo_done, 1)

            def gated(a, b, n):
                dve.wait_ge(sq_done, 2 * a + n + 1)
                dve.wait_ge(act_done, NSLOT * a + 2 * G + n + 1)
                nc.vector.scalar_tensor_tensor(bank[O_BANK[n]][:], gate[:, b, half(n)], 1.0, bank[O_BANK[n]][:],
                                               ALU.add, ALU.mult).then_inc(g_done, 1)
                dve.wait_ge(g_hi_done, 2 * a + n + 1)
                nc.vector.tensor_tensor(g_lo[:, half(n)], bank[O_BANK[n]][:], g_hi[:, half(n)],
                                        ALU.subtract).then_inc(g_lo_done, 1)

            def add_out(i, b, tiles):
                for n in tiles:
                    dve.wait_ge(c_done, NSLOT * (i - 2) + n + 1)
                    yt = y[:, b * (NT // 2) + n, :]
                    nc.vector.tensor_tensor(yt, bank[C_BANK[n % 2]][:], yt, ALU.add).then_inc(y_done, 1)

            def iteration(i, b, project, attend, output, qd_want=None):
                a, ab = i - 1, 1 - b
                for s in range(NSLOT):
                    n = {0: 0, 1: 1, 2: 0, 3: 0, 4: 1, 5: 1, 6: 0, 7: 1}[s]
                    if project and s < 2:
                        queries(i, b, s, qd_want)
                    if attend:
                        if s < 2:
                            keys_lo(a, n)
                        elif s in (2, 4):
                            mask_scores(a, n)
                        elif s in (3, 5):
                            states(a, n)
                        else:
                            gated(a, ab, n)
                    if output and 1 <= s <= 4:
                        add_out(i, b, (2 * s - 2, 2 * s - 1))
                    if project and s < 2:
                        scaled_queries_lo(i, b, s)
                    if attend and s in (2, 4):
                        scores_lo(a, n)
                    if attend and s in (3, 5):
                        states_lo(a, n)

            iteration(0, 0, True, False, False, 16)
            dve_tail(dve, NBLK - 1)
            for b in range(2):
                nc.vector.memset(y[:, b * (NT // 2):(b + 1) * (NT // 2), :], 0.0).then_inc(y_done, 1)
            dve.wait_ge(y_done, Y0)
            iteration(1, 1, True, True, False, 16)
            with dve.Fori(1, HEADS) as h:
                iteration(2 * h, 0, True, True, True, 16 * (h + 1))
                iteration(2 * h + 1, 1, True, True, True, 16 * (h + 1))
            def rms_variance(b):
                dve.wait_ge(ss_mm, b + 1)
                sm, m = rms(b)
                nc.vector.tensor_scalar(m[:, :, 1], bank[SS_BANK][:, b * NTB:(b + 1) * NTB], 1.0 / (HEADS * HD), None,
                                        ALU.mult).then_inc(rms_step, 1)
                nc.vector.memset(m[:, :, 0], 0.0).then_inc(rms_step, 1)
                variance(nc, dve, rms_step, b * RMS_STEPS + 2, sm, m, NTB, rms_var)

            def rms_factors(b):
                norm_factors(nc, dve, rms_step, b * RMS_STEPS + 2, *rms(b), NTB, rms_sd, b + 1)

            iteration(NIT, 0, False, True, True)
            rms_variance(0)
            for s in range(1, 5):
                add_out(NIT + 1, 1, (2 * s - 2, 2 * s - 1))
                if s == 1:
                    rms_factors(0)
                if s == 3:
                    rms_variance(1)
            rms_factors(1)
            dve.wait_ge(rms_step, 2 * RMS_STEPS)
            dve.wait_ge(y_done, Y0 + NSLOT * NIT)
            for i in range(NTB, NT):
                nc.vector.scalar_tensor_tensor(x_sb[:, i, :], y[:, i, :], small[:, 5, i:i + 1], x_sb[:, i, :],
                                               ALU.mult, ALU.add).then_inc(out_ready[1], 1)

        @block.tensor
        def _(pe):
            def group(out, pairs, start=True, stop=True):
                for n, (w, a) in enumerate(pairs):
                    mm = nc.tensor.matmul(out, w, a, start=start and n == 0, stop=stop and n == len(pairs) - 1)
                return mm

            def w_tile(m, k):
                return w_hi[:, m, k * P:(k + 1) * P], w_lo[:, m, k * P:(k + 1) * P]

            def projection(i, b, s, h):
                m, n = s // 2, s % 2
                if n == 0 and b == 0:
                    pe.wait_ge(w_done[m], h + 1)
                if m == K:
                    pe.wait_ge(qd_lo_done, 2 * i + n + 1)
                else:
                    wait(pe, act_done, NSLOT * i + s - 1)
                if m == V:
                    for c in range(CPH):
                        at = b * SEQ + n * BLK + c * CH
                        mm = group(bank[s % 2][:, c * HD:(c + 1) * HD], [p for k in range(KT) for p in passes(
                            xnT_hi[:, k, at:at + CH], xnT_lo[:, k, at:at + CH], *w_tile(V, k))])
                else:
                    at = b * SEQ + n * BLK
                    mm = group(bank[s % 2][:], [p for k in range(KT) for p in passes(
                        *w_tile(m, k), xnT_hi[:, k, at:at + BLK], xnT_lo[:, k, at:at + BLK])])
                mm.then_inc(proj_done, 1)

            def keys(a, b, n):
                pe.wait_ge(kv_lo_done, 4 * a + n + 1)
                if n == 0:
                    wait(pe, kT_lo_done, 2 * a)
                else:
                    wait(pe, st_done, NST * a)
                for c in range(CPH):
                    at = n * BLK + c * CH
                    for part, src, one, dt in ((0, k_hi, hw.ident_hi, F16), (1, k_lo, hw.ident_lo, BF16)):
                        out = bank[KT_BANK[n]][:, part * BLK // 2:(part + 1) * BLK // 2].bitcast(dt)
                        mm = nc.tensor.transpose(out[:, c * CH:(c + 1) * CH], src[:, b, at:at + CH], one[:])
                mm.then_inc(kT_done, 1)

            def scores(a, b, n):
                pe.wait_ge(kv_lo_done, 4 * a + n + 1)
                pe.wait_ge(q_lo_done, 2 * a + n + 1)
                wait(pe, p_lo_done, 2 * a + n)
                for c in range(CPH):
                    ts = slice(n * BLK + c * CH, n * BLK + (c + 1) * CH)
                    mm = group(bank[SC_BANK][:, c * CH:(c + 1) * CH], passes(
                        k_hi[:, b, ts], k_lo[:, b, ts], q_hi[:, b, ts], q_lo[:, b, ts]))
                mm.then_inc(sc_done, 1)

            def update(a, b, n):
                pe.wait_ge(kT_lo_done, 2 * a + 2)
                pe.wait_ge(vd_lo_done, 2 * a + n + 1)
                wait(pe, st_done, NST * a + n * CPH)
                for c in range(CPH if n == 0 else CPH - 1):
                    ts = slice(n * BLK + c * CH, n * BLK + (c + 1) * CH)
                    mm = group(bank[U_BANK][:, c * HD:(c + 1) * HD], passes(
                        kT_hi[:, ts], kT_lo[:, ts], vd_hi[:, ts], vd_lo[:, ts]))
                mm.then_inc(upd_done, 1)

            def attention(a, b, n):
                pe.wait_ge(p_lo_done, 2 * a + n + 1)
                pe.wait_ge(st_lo_done, 2 * a + n + 1)
                pe.wait_ge(qd_lo_done, 2 * a + n + 1)
                if n == 0:
                    wait(pe, g_lo_done, 2 * a + n)
                else:
                    wait(pe, y_done, Y0 + NSLOT * (a - 1) + NSLOT)
                for c in range(CPH):
                    chunk = n * CPH + c
                    ts = slice(n * BLK + c * CH, n * BLK + (c + 1) * CH)
                    out = bank[O_BANK[n]][:, c * CH:(c + 1) * CH]
                    mm = group(out, passes(v_hi[:, b, ts], v_lo[:, b, ts], p_hi[:, ts], p_lo[:, ts]), stop=chunk == 0)
                    if chunk:
                        mm = group(out, passes(st_hi[:, chunk, :], st_lo[:, chunk, :], qd_hi[:, b, ts], qd_lo[:, b, ts]),
                                   start=False)
                mm.then_inc(o_done, 1)

            def output(i, tiles, h):
                if tiles[0] == 0:
                    pe.wait_ge(w_done[OW], h)
                for n in tiles:
                    ts = slice(n * P, (n + 1) * P)
                    if n % TPB == 0:
                        pe.wait_ge(g_lo_done, 2 * (i - 2) + n // TPB + 1)
                    if n == 1:
                        pe.wait_ge(g_lo_done, 2 * (i - 2) + 2)
                    pe.wait_ge(y_done, Y0 + NSLOT * (i - 2) + n - 1)
                    group(bank[C_BANK[n % 2]][:], passes(g_hi[:, ts], g_lo[:, ts], w_hi[:, OW, :], w_lo[:, OW, :])).then_inc(c_done, 1)

            def iteration(i, b, h, project, attend, out):
                a, ab = i - 1, 1 - b
                for s in range(NSLOT):
                    if project:
                        projection(i, b, s, h)
                    if attend:
                        if s < 2:
                            keys(a, ab, s)
                        elif s in (2, 4):
                            scores(a, ab, s // 2 - 1)
                        elif s in (3, 5):
                            update(a, ab, (s - 3) // 2)
                        else:
                            attention(a, ab, s - 6)
                    if out and 1 <= s <= 4:
                        output(i, (2 * s - 2, 2 * s - 1), h)

            def sum_squares(b):
                pe.wait_ge(ss_done, 2 * (NIT - 1 + b))
                for i in range(b * NTB, (b + 1) * NTB):
                    mm = nc.tensor.matmul(bank[SS_BANK][:, i:i + 1], ssum[:, i * P:(i + 1) * P], ones[:], start=True, stop=True)
                mm.then_inc(ss_mm, 1)

            pe.wait_ge(hw.ident_done, 2)
            iteration(0, 0, 0, True, False, False)
            iteration(1, 1, 0, True, True, False)
            with pe.Fori(1, HEADS) as h:
                iteration(2 * h, 0, h, True, True, True)
                iteration(2 * h + 1, 1, h, True, True, True)
            pe.wait_ge(ones_done, 1)
            iteration(NIT, 0, HEADS, False, True, True)
            sum_squares(0)
            for s in range(1, 5):
                output(NIT + 1, (2 * s - 2, 2 * s - 1), HEADS)
                if s == 2:
                    sum_squares(1)


def decay_tables():
    base = np.float32(1.0 / 2.0 ** (8.0 / HEADS))
    factor = np.float32(1.0 - LAYER_IDX / (N_LAYERS - 1 + 1e-05) + 1e-05)
    slope = (base ** (np.arange(HEADS, dtype=np.float32) + 1) * factor).astype(np.float64)
    n = np.arange(CH, dtype=np.float64)
    dist = n[None, :] - n[:, None]
    mask = np.where(dist >= 0, np.exp(-slope[:, None, None] * np.maximum(dist, 0)), 0.0)
    key = np.exp(-slope[:, None] * (CH - 1 - n))[:, :, None]
    block = np.broadcast_to(np.exp(-slope * CH)[:, None, None], (HEADS, P, 1))
    tables = np.concatenate([mask, key, block], axis=2).astype(np.float32)
    query = np.exp(-slope[:, None] * (n + 1)).astype(np.float32)
    return tables, query


def kernel(**inp):
    import concourse.bacc as bacc
    from concourse.bass_utils import run_bass_kernel_spmd

    a = {k: np.asarray(v) for k, v in inp.items()}

    def pad(m, rows=None, cols=None):
        out = np.zeros((rows or m.shape[0], cols or m.shape[1]), m.dtype)
        out[:m.shape[0], :m.shape[1]] = m
        return out

    def tiles(m):
        return m.reshape(-1, P, m.shape[-1]).transpose(1, 0, 2)

    qkv = a["L1_attn_qkv_w"].reshape(HEADS, 3, HD, KT, P).transpose(0, 4, 1, 3, 2)
    gate = a["L1_attn_gate_w"].reshape(HEADS, 1, HD, KT, P).transpose(0, 4, 1, 3, 2)
    proj = np.concatenate([qkv, gate], axis=2)
    out_w = a["L1_attn_out_w"].T.reshape(HEADS, HD, D)
    out_w = np.concatenate([out_w, a["L1_attn_norm_w"].reshape(HEADS, HD, 1)], axis=2)
    tables, query = decay_tables()
    arrays = dict(
        x=a["L0_attn_x"].reshape(TOK, D),
        wq0=a["L0_attn_Wq"].reshape(D, -1), wk0=a["L0_attn_Wk"].reshape(D, -1), wv0=a["L0_attn_Wv"].reshape(D, -1),
        bq0=a["L0_attn_bq"].reshape(-1), bk0=a["L0_attn_bk"].reshape(-1), bv0=a["L0_attn_bv"].reshape(-1),
        gate_q=pad(a["L0_ffn_gate_q"].T, cols=INT0P), up_q=pad(a["L0_ffn_up_q"].T, cols=INT0P),
        down_q=pad(a["L0_ffn_down_q"].T, rows=INT0P),
        gate_s=pad(a["L0_ffn_gate_scale"][:, None], rows=INT0P).reshape(OT0, P).T,
        up_s=pad(a["L0_ffn_up_scale"][:, None], rows=INT0P).reshape(OT0, P).T,
        down_s=a["L0_ffn_down_scale"],
        gate_A=a["L0_ffn_gate_A"], up_A=a["L0_ffn_up_A"], down_A=pad(a["L0_ffn_down_A"], rows=INT0P),
        gate_B=pad(a["L0_ffn_gate_B"], cols=INT0P), up_B=pad(a["L0_ffn_up_B"], cols=INT0P), down_B=a["L0_ffn_down_B"],
        w1=np.concatenate([tiles(a["L1_ffn_" + n]).reshape(P, -1)
                           for n in ("up_w", "down_w", "fc1_w", "expert_w", "fc2_w")], axis=1),
        route_w=tiles(a["L1_ffn_gate_w"]),
        gamma=a["L1_ffn_ln_gamma"], beta=a["L1_ffn_ln_beta"],
        proj_w=proj, out_w=out_w, decay=tables, q_decay=query,
    )
    nc = bacc.Bacc("TRN2", target_bir_lowering=False, num_devices=1)
    t, feed = {}, {}
    for name, v in arrays.items():
        v = np.ascontiguousarray(v)
        feed[f"{name}_dram"] = v
        t[name] = nc.dram_tensor(f"{name}_dram", v.shape, mybir.dt.from_np(v.dtype), kind="ExternalInput").ap()
    t["out"] = nc.dram_tensor("out_dram", (TOK, D), F32, kind="ExternalOutput").ap()
    build(nc, t)
    r = run_bass_kernel_spmd(nc, [feed], core_ids=[0])
    return r.results[0]["out_dram"].reshape(BATCH, SEQ, D)
```
